# Optimizing a Trainium2 kernel written in Bass

```python
import numpy as np
import jax
import jax.numpy as jnp

def _softmax(x, axis=-1):
    return jax.nn.softmax(x, axis=axis)

def _gelu(x):
    return jax.nn.gelu(x, approximate=True)

def _silu(x):
    return jax.nn.silu(x)

def _sigmoid(x):
    return jax.nn.sigmoid(x)

def _layernorm(x, axis=-1, eps=1e-05):
    m = jnp.mean(x, axis=axis, keepdims=True)
    v = jnp.var(x, axis=axis, keepdims=True)
    return (x - m) / jnp.sqrt(v + eps)

def _scatter_add(tgt, idx, src, axis=0):
    return tgt.at[idx].add(src)

def _segment_sum(src, seg, n):
    return jax.ops.segment_sum(src, seg, n)
kernel_name = 'mk_seq_postln_d2_jaxref_r8_ac3155'

def setup_inputs(seed: int=0):
    np.random.seed(seed)
    _w = jnp.asarray

    def _L0_attn_setup():
        import jax, jax.numpy as jnp
        import numpy as np
        EPS = 1e-06

        def elu1(x):
            return jax.nn.elu(x) + 1.0
        key = jax.random.key(seed)
        ks = jax.random.split(key, 8)
        B, S, H, NH, M = (1, 256, 128, 16, 4)
        D = H // NH
        scale = 1.0 / np.sqrt(H)
        return {'hidden_states': jax.random.normal(ks[0], (B, S, H), jnp.float32), 'w_q': jax.random.normal(ks[1], (H, H), jnp.float32) * scale, 'w_k': jax.random.normal(ks[2], (H, H), jnp.float32) * scale, 'w_v': jax.random.normal(ks[3], (H, H), jnp.float32) * scale, 'w_o': jax.random.normal(ks[4], (H, H), jnp.float32) * scale, 'gate': jax.random.normal(ks[5], (NH,), jnp.float32), 'memories': jax.random.uniform(ks[6], (M, NH, D, D), jnp.float32), 'memory_norms': jax.random.uniform(ks[7], (M, NH, D), jnp.float32)}
    _L0_attn_in = _L0_attn_setup()

    def _L0_ffn_setup():
        import jax, jax.numpy as jnp
        import numpy as np
        B, S, DIM = (2, 256, 128)
        HID = 256
        E, NSH, TOPK = (8, 2, 2)

        def _ffn(x, w1, w2, w3):
            return jax.nn.silu(x @ w1.T) * (x @ w3.T) @ w2.T
        key = jax.random.key(seed)
        ks = jax.random.split(key, 8)
        sc = 0.02
        return {'x': jax.random.normal(ks[0], (B, S, DIM), jnp.float32), 'router_w': jax.random.normal(ks[1], (E, DIM), jnp.float32) * sc, 'expert_bias': jnp.zeros((E,), jnp.float32), 'w1': jax.random.normal(ks[2], (E, HID, DIM), jnp.float32) * sc, 'w3': jax.random.normal(ks[3], (E, HID, DIM), jnp.float32) * sc, 'w2': jax.random.normal(ks[4], (E, DIM, HID), jnp.float32) * sc, 'sw1': jax.random.normal(ks[5], (NSH, HID, DIM), jnp.float32) * sc, 'sw3': jax.random.normal(ks[6], (NSH, HID, DIM), jnp.float32) * sc, 'sw2': jax.random.normal(ks[7], (NSH, DIM, HID), jnp.float32) * sc}
    _L0_ffn_in = _L0_ffn_setup()

    def _L1_attn_setup():
        import jax, jax.numpy as jnp
        import numpy as np
        import math
        NUM_HEADS = 8
        EMB = 128
        HEAD_DIM = 128
        B, T = (1, 512)

        def sinusoidal_pe(T, d, dtype=jnp.float32):
            pos = jnp.arange(T, dtype=dtype)[:, None]
            inv_freq = jnp.exp(-math.log(10000.0) * jnp.arange(0, d, 2, dtype=dtype) / d)
            ang = pos * inv_freq[None, :]
            pe = jnp.zeros((T, d), dtype=dtype)
            pe = pe.at[:, 0::2].set(jnp.sin(ang))
            pe = pe.at[:, 1::2].set(jnp.cos(ang))
            return pe
        key = jax.random.key(seed)
        ks = jax.random.split(key, 6)
        s = lambda fan_in: 1.0 / math.sqrt(fan_in)
        x = jax.random.normal(ks[0], (B, T, EMB), dtype=jnp.float32)
        Wq = jax.random.normal(ks[1], (EMB, NUM_HEADS * HEAD_DIM), dtype=jnp.float32) * s(EMB)
        bq = jax.random.normal(ks[2], (NUM_HEADS * HEAD_DIM,), dtype=jnp.float32) * s(EMB)
        Wkv = jax.random.normal(ks[3], (EMB, 2 * HEAD_DIM), dtype=jnp.float32) * s(EMB)
        bkv = jax.random.normal(ks[4], (2 * HEAD_DIM,), dtype=jnp.float32) * s(EMB)
        Wo = jax.random.normal(ks[5], (NUM_HEADS * HEAD_DIM, EMB), dtype=jnp.float32) * s(NUM_HEADS * HEAD_DIM)
        return {'x': x, 'Wq': Wq, 'bq': bq, 'Wkv': Wkv, 'bkv': bkv, 'Wo': Wo}
    _L1_attn_in = _L1_attn_setup()

    def _L1_ffn_setup():
        import jax, jax.numpy as jnp
        import numpy as np
        B, S, D = (4, 128, 128)
        I = 64
        E = 32
        TOP_K = 8
        N_GROUP = 8
        TOPK_GROUP = 4

        def _group_topk(scores):
            T = scores.shape[0]
            epg = E // N_GROUP
            group_scores = scores.reshape(T, N_GROUP, epg).sum(axis=-1)
            _, top_groups = jax.lax.top_k(group_scores, TOPK_GROUP)
            group_mask = jnp.zeros((T, N_GROUP), scores.dtype).at[jnp.arange(T)[:, None], top_groups].set(1.0)
            expert_mask = jnp.repeat(group_mask, epg, axis=1)
            masked_scores = scores * expert_mask
            topk_w, topk_i = jax.lax.top_k(masked_scores, TOP_K)
            return (topk_w, topk_i)

        def _reference_tuple_inner(hidden_states, gate_w, expert_gate, expert_up, expert_down, shared_gate_w, shared_up_w, shared_down_w):
            b, s, d = hidden_states.shape
            flat = hidden_states.reshape(-1, d)
            T = flat.shape[0]
            logits = flat @ gate_w.T
            scores = jax.nn.sigmoid(logits)
            topk_w, topk_i = _group_topk(scores)
            topk_w = topk_w / jnp.clip(topk_w.sum(axis=-1, keepdims=True), 1e-12)
            combine = jnp.zeros((T, E), flat.dtype).at[jnp.arange(T)[:, None], topk_i].add(topk_w)

            def body(acc, expert):
                wg, wu, wd, w = expert
                h = jax.nn.silu(flat @ wg.T) * (flat @ wu.T)
                return (acc + w[:, None] * (h @ wd.T), None)
            out, _ = jax.lax.scan(body, jnp.zeros_like(flat), (expert_gate, expert_up, expert_down, combine.T))
            shared = jax.nn.silu(flat @ shared_gate_w.T) * (flat @ shared_up_w.T) @ shared_down_w.T
            out = out + shared
            return (out.reshape(b, s, d), logits)
        key = jax.random.key(seed)
        ks = jax.random.split(key, 8)
        scale = 0.02
        return {'hidden_states': jax.random.normal(ks[0], (B, S, D), jnp.float32), 'gate_w': jax.random.normal(ks[1], (E, D), jnp.float32) * scale, 'expert_gate': jax.random.normal(ks[2], (E, I, D), jnp.float32) * scale, 'expert_up': jax.random.normal(ks[3], (E, I, D), jnp.float32) * scale, 'expert_down': jax.random.normal(ks[4], (E, D, I), jnp.float32) * scale, 'shared_gate_w': jax.random.normal(ks[5], (I, D), jnp.float32) * scale, 'shared_up_w': jax.random.normal(ks[6], (I, D), jnp.float32) * scale, 'shared_down_w': jax.random.normal(ks[7], (D, I), jnp.float32) * scale}
    _L1_ffn_in = _L1_ffn_setup()
    _d = {'L0_attn_hidden_states': _L0_attn_in['hidden_states'], 'L0_attn_w_q': _L0_attn_in['w_q'], 'L0_attn_w_k': _L0_attn_in['w_k'], 'L0_attn_w_v': _L0_attn_in['w_v'], 'L0_attn_w_o': _L0_attn_in['w_o'], 'L0_attn_gate': _L0_attn_in['gate'], 'L0_attn_memories': _L0_attn_in['memories'], 'L0_attn_memory_norms': _L0_attn_in['memory_norms'], 'L0_ffn_router_w': _L0_ffn_in['router_w'], 'L0_ffn_expert_bias': _L0_ffn_in['expert_bias'], 'L0_ffn_w1': _L0_ffn_in['w1'], 'L0_ffn_w3': _L0_ffn_in['w3'], 'L0_ffn_w2': _L0_ffn_in['w2'], 'L0_ffn_sw1': _L0_ffn_in['sw1'], 'L0_ffn_sw3': _L0_ffn_in['sw3'], 'L0_ffn_sw2': _L0_ffn_in['sw2'], 'L1_attn_Wq': _L1_attn_in['Wq'], 'L1_attn_bq': _L1_attn_in['bq'], 'L1_attn_Wkv': _L1_attn_in['Wkv'], 'L1_attn_bkv': _L1_attn_in['bkv'], 'L1_attn_Wo': _L1_attn_in['Wo'], 'L1_ffn_gate_w': _L1_ffn_in['gate_w'], 'L1_ffn_expert_gate': _L1_ffn_in['expert_gate'], 'L1_ffn_expert_up': _L1_ffn_in['expert_up'], 'L1_ffn_expert_down': _L1_ffn_in['expert_down'], 'L1_ffn_shared_gate_w': _L1_ffn_in['shared_gate_w'], 'L1_ffn_shared_up_w': _L1_ffn_in['shared_up_w'], 'L1_ffn_shared_down_w': _L1_ffn_in['shared_down_w']}
    _x0 = _d['L0_attn_hidden_states']
    _d['L0_attn_hidden_states'] = jax.random.normal(jax.random.fold_in(jax.random.key(seed), 1), (32, 256, 128), dtype=_x0.dtype)
    del _x0
    return _d

def reference(L0_attn_hidden_states, L0_attn_w_q, L0_attn_w_k, L0_attn_w_v, L0_attn_w_o, L0_attn_gate, L0_attn_memories, L0_attn_memory_norms, L0_ffn_router_w, L0_ffn_expert_bias, L0_ffn_w1, L0_ffn_w3, L0_ffn_w2, L0_ffn_sw1, L0_ffn_sw3, L0_ffn_sw2, L1_attn_Wq, L1_attn_bq, L1_attn_Wkv, L1_attn_bkv, L1_attn_Wo, L1_ffn_gate_w, L1_ffn_expert_gate, L1_ffn_expert_up, L1_ffn_expert_down, L1_ffn_shared_gate_w, L1_ffn_shared_up_w, L1_ffn_shared_down_w):

    def _L0_attn_ref(hidden_states, w_q, w_k, w_v, w_o, gate, memories, memory_norms):
        import jax, jax.numpy as jnp
        import numpy as np
        EPS = 1e-06

        def elu1(x):
            return jax.nn.elu(x) + 1.0
        B, S, H = hidden_states.shape
        NH = gate.shape[0]
        D = H // NH

        def proj(w):
            return (hidden_states @ w.T).reshape(B, S, NH, D).transpose(0, 2, 1, 3)
        q, k, v = (proj(w_q), proj(w_k), proj(w_v))
        sq = elu1(q)
        sk = elu1(k)
        out_m = jnp.einsum('bhsd,mhde->mbhse', sq, memories)
        rel = jnp.einsum('bhsd,mhd->mbhs', sq, memory_norms)
        out_m = out_m / jnp.clip(rel, EPS, None)[..., None]
        weights = jax.nn.softmax(rel.mean(axis=-1), axis=0)
        mem_out = jnp.einsum('mbhse,mbh->bhse', out_m, weights)
        kv = jnp.einsum('bhsd,bhse->bhsde', sk, v)
        kv_cum = jnp.cumsum(kv, axis=2)
        k_cum = jnp.cumsum(sk, axis=2)
        num = jnp.einsum('bhsd,bhsde->bhse', sq, kv_cum)
        den = jnp.clip(jnp.einsum('bhsd,bhsd->bhs', sq, k_cum), EPS, None)
        local = num / den[..., None]
        g = jax.nn.sigmoid(gate)[None, :, None, None]
        out = g * mem_out + (1.0 - g) * local
        out = out.transpose(0, 2, 1, 3).reshape(B, S, H)
        return out @ w_o.T

    def _L0_ffn_ref(x, router_w, expert_bias, w1, w3, w2, sw1, sw3, sw2):
        import jax, jax.numpy as jnp
        import numpy as np
        B, S, DIM = (2, 256, 128)
        HID = 256
        E, NSH, TOPK = (8, 2, 2)

        def _ffn(x, w1, w2, w3):
            return jax.nn.silu(x @ w1.T) * (x @ w3.T) @ w2.T
        bs, sl, d = x.shape
        xf = x.reshape(-1, d)
        shared = jnp.zeros_like(xf)
        for i in range(sw1.shape[0]):
            shared = shared + _ffn(xf, sw1[i], sw2[i], sw3[i])
        logits = xf @ router_w.T + expert_bias
        rw, sel = jax.lax.top_k(logits, TOPK)
        rw = jax.nn.softmax(rw.astype(jnp.float32), axis=-1).astype(x.dtype)
        onehot = jax.nn.one_hot(sel, E, dtype=x.dtype)
        combine = jnp.einsum('tk,tke->te', rw, onehot)

        def body(acc, ew):
            e1, e3, e2, cw = ew
            acc = acc + cw[:, None] * _ffn(xf, e1, e2, e3)
            return (acc, None)
        out, _ = jax.lax.scan(body, jnp.zeros_like(xf), (w1, w3, w2, combine.T))
        out = out + shared
        return out.reshape(bs, sl, -1)

    def _L1_attn_ref(x, Wq, bq, Wkv, bkv, Wo):
        import jax, jax.numpy as jnp
        import numpy as np
        import math
        NUM_HEADS = 8
        EMB = 128
        HEAD_DIM = 128
        B, T = (1, 512)

        def sinusoidal_pe(T, d, dtype=jnp.float32):
            pos = jnp.arange(T, dtype=dtype)[:, None]
            inv_freq = jnp.exp(-math.log(10000.0) * jnp.arange(0, d, 2, dtype=dtype) / d)
            ang = pos * inv_freq[None, :]
            pe = jnp.zeros((T, d), dtype=dtype)
            pe = pe.at[:, 0::2].set(jnp.sin(ang))
            pe = pe.at[:, 1::2].set(jnp.cos(ang))
            return pe
        Bsz, Tlen, E = x.shape
        q = (x @ Wq + bq).reshape(Bsz, Tlen, NUM_HEADS, HEAD_DIM)
        kv = x @ Wkv + bkv
        k, v = (kv[..., :HEAD_DIM], kv[..., HEAD_DIM:])
        q = jnp.transpose(q, (0, 2, 1, 3))
        pe = sinusoidal_pe(Tlen, HEAD_DIM, x.dtype)
        q = q + pe[None, None, :, :]
        k = k + pe[None, :, :]
        scale = 1.0 / math.sqrt(HEAD_DIM)
        scores = jnp.einsum('bhqd,bkd->bhqk', q, k) * scale
        causal = jnp.tril(jnp.ones((Tlen, Tlen), dtype=bool))
        scores = jnp.where(causal[None, None, :, :], scores, jnp.finfo(scores.dtype).min)
        probs = jax.nn.softmax(scores, axis=-1)
        attn = jnp.einsum('bhqk,bkd->bhqd', probs, v)
        out = jnp.transpose(attn, (0, 2, 1, 3)).reshape(Bsz, Tlen, NUM_HEADS * HEAD_DIM)
        return out @ Wo

    def _L1_ffn_ref(hidden_states, gate_w, expert_gate, expert_up, expert_down, shared_gate_w, shared_up_w, shared_down_w):
        import jax, jax.numpy as jnp
        import numpy as np
        B, S, D = (4, 128, 128)
        I = 64
        E = 32
        TOP_K = 8
        N_GROUP = 8
        TOPK_GROUP = 4

        def _group_topk(scores):
            T = scores.shape[0]
            epg = E // N_GROUP
            group_scores = scores.reshape(T, N_GROUP, epg).sum(axis=-1)
            _, top_groups = jax.lax.top_k(group_scores, TOPK_GROUP)
            group_mask = jnp.zeros((T, N_GROUP), scores.dtype).at[jnp.arange(T)[:, None], top_groups].set(1.0)
            expert_mask = jnp.repeat(group_mask, epg, axis=1)
            masked_scores = scores * expert_mask
            topk_w, topk_i = jax.lax.top_k(masked_scores, TOP_K)
            return (topk_w, topk_i)

        def _reference_tuple_inner(hidden_states, gate_w, expert_gate, expert_up, expert_down, shared_gate_w, shared_up_w, shared_down_w):
            b, s, d = hidden_states.shape
            flat = hidden_states.reshape(-1, d)
            T = flat.shape[0]
            logits = flat @ gate_w.T
            scores = jax.nn.sigmoid(logits)
            topk_w, topk_i = _group_topk(scores)
            topk_w = topk_w / jnp.clip(topk_w.sum(axis=-1, keepdims=True), 1e-12)
            combine = jnp.zeros((T, E), flat.dtype).at[jnp.arange(T)[:, None], topk_i].add(topk_w)

            def body(acc, expert):
                wg, wu, wd, w = expert
                h = jax.nn.silu(flat @ wg.T) * (flat @ wu.T)
                return (acc + w[:, None] * (h @ wd.T), None)
            out, _ = jax.lax.scan(body, jnp.zeros_like(flat), (expert_gate, expert_up, expert_down, combine.T))
            shared = jax.nn.silu(flat @ shared_gate_w.T) * (flat @ shared_up_w.T) @ shared_down_w.T
            out = out + shared
            return (out.reshape(b, s, d), logits)
        return _reference_tuple_inner(hidden_states, gate_w, expert_gate, expert_up, expert_down, shared_gate_w, shared_up_w, shared_down_w)[0]
    x = L0_attn_hidden_states
    x = _layernorm(x + _L0_attn_ref(x, L0_attn_w_q, L0_attn_w_k, L0_attn_w_v, L0_attn_w_o, L0_attn_gate, L0_attn_memories, L0_attn_memory_norms), axis=-1)
    x = _layernorm(x + _L0_ffn_ref(x, L0_ffn_router_w, L0_ffn_expert_bias, L0_ffn_w1, L0_ffn_w3, L0_ffn_w2, L0_ffn_sw1, L0_ffn_sw3, L0_ffn_sw2), axis=-1)
    x = _layernorm(x + _L1_attn_ref(x, L1_attn_Wq, L1_attn_bq, L1_attn_Wkv, L1_attn_bkv, L1_attn_Wo), axis=-1)
    x = _layernorm(x + _L1_ffn_ref(x, L1_ffn_gate_w, L1_ffn_expert_gate, L1_ffn_expert_up, L1_ffn_expert_down, L1_ffn_shared_gate_w, L1_ffn_shared_up_w, L1_ffn_shared_down_w), axis=-1)
    return x

_drawn_inputs = setup_inputs


def setup_inputs(seed=0):
    import zlib

    import numpy as np

    out = dict(_drawn_inputs(seed))
    spreads = {'L0_ffn_expert_bias': (0.0, 0.8)}
    factors = {'L0_attn_w_k': 2.694,
     'L0_ffn_router_w': 8.0,
     'L0_ffn_w1': 8.0,
     'L0_ffn_w3': 8.0,
     'L0_ffn_w2': 8.0,
     'L0_ffn_sw1': 5.021,
     'L0_ffn_sw3': 4.99,
     'L0_ffn_sw2': 5.029,
     'L1_attn_bq': 3.759,
     'L1_ffn_gate_w': 8.0,
     'L1_ffn_expert_gate': 8.0,
     'L1_ffn_expert_up': 8.0,
     'L1_ffn_expert_down': 8.0,
     'L1_ffn_shared_gate_w': 8.0,
     'L1_ffn_shared_up_w': 8.0,
     'L1_ffn_shared_down_w': 8.0}
    for name, (base, spread) in spreads.items():
        noise = np.random.default_rng([zlib.crc32(name.encode()), seed]).standard_normal(out[name].shape)
        drawn = base * np.exp(spread * noise) if base else spread * noise
        out[name] = jnp.asarray(drawn.astype(out[name].dtype))
    for name, factor in factors.items():
        out[name] = (out[name] * factor).astype(out[name].dtype)
    return out
```

```python
import math
from contextlib import ExitStack

import numpy as np

import concourse.bass as bass
from concourse import mybir

F32 = mybir.dt.float32
F32R = mybir.dt.float32r
BF16 = mybir.dt.bfloat16
U32 = mybir.dt.uint32
ALU = mybir.AluOpType
ACT = mybir.ActivationFunctionType
AX = mybir.AxisListType.X

P = 128
BATCH, SEQ, DM = 32, 256, 128
TOKENS = BATCH * SEQ
GT = 512
GROUPS = TOKENS // GT
TILES = GT // P
SEQS = GT // SEQ
L0_HEADS, L0_D, MEMS = 16, 8, 4
L1_HEADS = 8
L0_E, L0_HID, L0_SHARED = 8, 256, 2
L1_E, L1_HID = 32, 64
L1_GROUPS, L1_PER = 8, 4
EPS_DEN, EPS_LN, EPS_TOPK = 1e-6, 1e-5, 1e-12
SCALE = 1.0 / math.sqrt(P)
MASKED = -3.0e38
L0_TILES = (L0_E + L0_SHARED) * L0_HID // P
L1_TILES = L1_E * L1_HID // P + 1
REL = MEMS * L0_HEADS
DEN = REL + L0_HEADS


def wait(eng, sem, value):
    if isinstance(value, int) and value <= 0:
        return
    eng.wait_ge(sem, value)




def snapped(eng, value):
    return value if isinstance(value, int) else eng.to_reg(value)


def last_use(i, n, per, slots):
    if n >= slots:
        return i * per + n - slots + 1
    last = max(m for m in range(per) if m % slots == n % slots)
    return (i - 1) * per + last + 1


def build(nc, xT, w_l0, mem_bd, norms_bd, gate, w_ffn0, w_ffn1, router0, bias0, router1,
          w_l1, wo_l1, b_l1, bv_l1, peT, c_f32, c_tri, c_sel0, c_sel1, out):
    ctx = ExitStack()
    with ctx:
        def sb(name, shape, dt=F32):
            return ctx.enter_context(nc.sbuf_tensor(name, shape, dt))

        def sem(name):
            return ctx.enter_context(nc.semaphore(name))

        bank = [ctx.enter_context(nc.psum_tensor(f"bank{b}", [P, GT], F32)) for b in range(8)]

        resid = sb("resid", [P, TOKENS])
        x_hi, x_lo = sb("x_hi", [P, GT], F32R), sb("x_lo", [P, GT], F32R)
        cwT = sb("cwT", [96, TOKENS], BF16)
        NW0, NW1 = 3 * L0_TILES * P, 3 * L1_TILES * P
        ffn_hi, ffn_lo = sb("ffn_hi", [P, NW0], F32R), sb("ffn_lo", [P, NW0], F32R)
        CH0, CH1 = NW0 // GROUPS, NW1 // GROUPS
        stage = sb("stage", [P, max(CH0, CH1)])
        ident = sb("ident", [P, P])
        ident_bf = sb("ident_bf", [P, P], BF16)
        half = sb("half", [P, TILES])
        y_sb, z_sb = sb("y_sb", [P, GT]), sb("z_sb", [P, TILES, P])
        stats, mv = sb("stats", [P, TILES, 6]), sb("mv", [P, TILES, 2])
        var_eps, rstd = sb("var_eps", [P, TILES]), sb("rstd", [P, TILES])
        router0_sb, router1_sb = sb("router0_sb", [P, L0_E]), sb("router1_sb", [P, L1_E])
        bias0_sb = sb("bias0_sb", [P, L0_E])
        iota8 = sb("iota8", [P, 8])
        sel0 = sb("sel0", [3 * L0_E, L0_E, P], BF16)
        sel1 = sb("sel1", [3 * L1_E, L1_TILES - 1, P], BF16)
        lg = sb("lg", [P, TILES, L1_E])
        sg = sb("sg", [P, TILES, L1_E])
        cw = sb("cw", [P, TILES, L1_E])
        rest_w = sb("rest_w", [P, TILES, L1_E])
        cw3 = sb("cw3", [P, TILES, 3 * L1_E], BF16)
        top = sb("top", [P, TILES, 8])
        idx = sb("idx", [P, TILES, 8], U32)
        idxf = sb("idxf", [P, TILES, 8])
        gsum, gmask = sb("gsum", [P, TILES, 8]), sb("gmask", [P, TILES, 8])
        xf = sb("xf", [P, GT])
        eq4 = sb("eq4", [P, TILES, 8, 4])
        pair = sb("pair", [P, 4, TILES])

        only_l0 = ExitStack()

        def sb0(name, shape, dt=F32):
            return only_l0.enter_context(nc.sbuf_tensor(name, shape, dt))

        wl0_hi, wl0_lo = sb0("wl0_hi", [P, 10, P], F32R), sb0("wl0_lo", [P, 10, P], F32R)
        wo0 = sb0("wo0", [P, P])
        mem_sb, norms_sb = sb0("mem_sb", [P, MEMS, P]), sb0("norms_sb", [P, REL])
        headsum = sb0("headsum", [P, L0_HEADS])
        spread = sb0("spread", [DEN, MEMS + 1, P])
        blocksum = sb0("blocksum", [P, L0_D, P])
        reset = sb0("reset", [P, GT])
        gate_row, gate_col = sb0("gate_row", [SEQS, L0_HEADS]), sb0("gate_col", [DEN, 1])
        wcol = sb0("wcol", [DEN, SEQS])
        s_const, s_raw, s_ones, s_cast = sem("consts_loaded"), sem("raw_loaded"), sem("gates_exp"), sem("setup_done")
        with nc.sbuf_tensor("raw", [P, 10, P], F32) as raw, nc.sbuf_tensor("gtmp", [P, 16], F32) as gtmp, \
                nc.sbuf_tensor("sel0_raw", [3 * L0_E, L0_E, P], F32) as sel0_raw, \
                nc.sbuf_tensor("sel1_raw", [3 * L1_E, L1_TILES - 1, P], F32) as sel1_raw, \
                nc.Block() as block:
            @block.sync
            def _(sp):
                o = 0
                for dst, w in ((ident[:], P), (headsum[:], L0_HEADS), (blocksum[:], L0_D * P), (reset[:], GT),
                               (iota8[:], 8)):
                    src = c_f32[:, o:o + w]
                    if len(dst.shape) == 3:
                        src = src.rearrange("p (a b) -> p a b", a=dst.shape[1])
                    sp.dma_start(dst, src).then_inc(s_const, 16)
                    o += w
                sp.dma_start(spread[:], c_f32[0:DEN, o:o + (MEMS + 1) * P].rearrange("p (a b) -> p a b", a=MEMS + 1)).then_inc(s_const, 16)
                sp.dma_start(sel0_raw[:], c_sel0).then_inc(s_const, 16)
                sp.dma_start(sel1_raw[:], c_sel1).then_inc(s_const, 16)
                sp.dma_start(mem_sb[:], mem_bd).then_inc(s_const, 16)
                sp.dma_start(norms_sb[:], norms_bd).then_inc(s_const, 16)
                sp.dma_start(router0_sb[:], router0).then_inc(s_const, 16)
                sp.dma_start(router1_sb[:], router1).then_inc(s_const, 16)
                sp.dma_start(bias0_sb[:], bias0.partition_broadcast(P)).then_inc(s_const, 16)
                sp.wait_ge(s_const, 16 * 13)

            @block.scalar
            def _(act):
                act.dma_start(raw[:], w_l0[:, 0:10, :]).then_inc(s_raw, 16)
                act.dma_start(wo0[:], w_l0[:, 10, :]).then_inc(s_raw, 16)
                act.dma_start(gate_row[:], gate.partition_broadcast(SEQS)).then_inc(s_raw, 16)
                act.dma_start(gate_col[REL:DEN, :], gate.rearrange("(h a) -> h a", a=1)).then_inc(s_raw, 16)
                act.wait_ge(s_raw, 64)
                nc.scalar.activation(gtmp[0:SEQS, :], gate_row[:], ACT.Exp, scale=-1.0).then_inc(s_ones, 1)
                nc.scalar.activation(gtmp[REL:DEN, 0:1], gate_col[REL:DEN, :], ACT.Exp).then_inc(s_ones, 1)

            @block.vector
            def _(dve):
                nc.vector.memset(half[:], -0.5)
                dve.wait_ge(s_raw, 64)
                nc.vector.tensor_copy(wl0_hi[:], raw[:])
                dve.drain()
                nc.vector.tensor_tensor(wl0_lo[:], raw[:], wl0_hi[:].bitcast(F32), ALU.subtract)
                dve.wait_ge(s_ones, 2)
                nc.vector.tensor_scalar(gtmp[0:SEQS, :], gtmp[0:SEQS, :], 1.0, None, ALU.add)
                nc.vector.tensor_scalar(gtmp[REL:DEN, 0:1], gtmp[REL:DEN, 0:1], 1.0, None, ALU.add)
                dve.drain()
                nc.vector.reciprocal(gate_row[:], gtmp[0:SEQS, :])
                nc.vector.reciprocal(gate_col[REL:DEN, :], gtmp[REL:DEN, 0:1])
                dve.drain()
                for s in range(SEQS):
                    nc.vector.tensor_copy(wcol[REL:DEN, s:s + 1], gate_col[REL:DEN, :])
                dve.wait_ge(s_const, 16 * 13)
                nc.vector.tensor_copy(sel0[:], sel0_raw[:])
                nc.vector.tensor_copy(sel1[:], sel1_raw[:])
                nc.vector.tensor_copy(ident_bf[:], ident[:]).then_inc(s_cast, 1)
                dve.wait_ge(s_cast, 1)

        def group(i, n=GT):
            return bass.ds(i * n, n)

        class Tail:

            def __init__(self, part, last=False, route=None):
                self.last, self.route = last, route
                self.y_ready = sem(f"{part}_y_ready")
                self.tok_ready = sem(f"{part}_tok_ready")
                self.stats_ready = sem(f"{part}_stats_ready")
                self.var_ready = sem(f"{part}_var_ready")
                self.rstd_ready = sem(f"{part}_rstd_ready")
                self.z_ready = sem(f"{part}_z_ready")
                self.feat_ready = sem(f"{part}_feat_ready")
                self.x_ready = sem(f"{part}_x_ready")
                self.stored = sem(f"{part}_stored")

            def pe_tokens(self, pe, i):
                wait(pe, self.y_ready, i + 1)
                if self.last:
                    wait(pe, self.z_ready, i)
                else:
                    wait(pe, self.x_ready, i)
                for t in range(TILES):
                    last = nc.tensor.transpose(bank[0][:, t * P:(t + 1) * P], y_sb[:, t * P:(t + 1) * P], ident[:])
                last.then_inc(self.tok_ready, 1)

            def pe_features(self, pe, i):
                if self.last:
                    return
                wait(pe, self.z_ready, i + 1)
                for t in range(TILES):
                    last = nc.tensor.transpose(bank[0][:, t * P:(t + 1) * P], z_sb[:, t, :], ident[:])
                last.then_inc(self.feat_ready, 1)

            def dve_stats(self, dve, i):
                dve.wait_ge(s_cast, 1)
                wait(dve, self.rstd_ready, i)
                wait(dve, self.tok_ready, i + 1)
                for t in range(TILES):
                    nc.vector.bn_stats(stats[:, t, :], bank[0][:, t * P:(t + 1) * P])
                dve.drain()
                for t in range(TILES):
                    last = nc.vector.bn_aggr(mv[:, t, :], stats[:, t, :])
                last.then_inc(self.stats_ready, 1)

            def pool_rstd(self, pool, i):
                pool.wait_ge(s_cast, 1)
                wait(pool, self.z_ready, i)
                wait(pool, self.stats_ready, i + 1)
                nc.gpsimd.tensor_scalar(var_eps[:], mv[:, :, 1], EPS_LN, None, ALU.add).then_inc(self.var_ready, 1)
                wait(pool, self.var_ready, i + 1)
                nc.gpsimd.tensor_tensor(rstd[:], var_eps[:], half[:], ALU.pow).then_inc(self.rstd_ready, 1)

            def dve_normalise(self, dve, i):
                if self.last:
                    wait(dve, self.stored, 16 * i)
                else:
                    wait(dve, self.feat_ready, i)
                wait(dve, self.rstd_ready, i + 1)
                for t in range(TILES):
                    last = nc.vector.tensor_scalar(z_sb[:, t, :], bank[0][:, t * P:(t + 1) * P], mv[:, t, 0:1],
                                                   rstd[:, t:t + 1], ALU.subtract, ALU.mult)
                last.then_inc(self.z_ready, 1)

            def act_resid(self, act, i):
                if self.route:
                    wait(act, self.route.logits_ready, i)
                wait(act, self.feat_ready, i + 1)
                if self.route:
                    nc.scalar.activation(xf[:], bank[0][:], ACT.Copy)
                act.wait_ge(s_cast, 1)
                nc.scalar.activation(resid[:, group(i)], bank[0][:], ACT.Copy).then_inc(self.x_ready, 1)

            def sp_store(self, sp, i):
                wait(sp, self.z_ready, i + 1)
                sp.dma_start(out[group(i), :].rearrange("(t p) f -> p t f", p=P), z_sb[:]).then_inc(self.stored, 16)

        class Split:

            def __init__(self, part):
                self.hi_ready, self.lo_ready = sem(f"{part}_x_hi_ready"), sem(f"{part}_x_lo_ready")

            def act_hi(self, act, i):
                nc.scalar.activation(x_hi[:], resid[:, group(i)], ACT.Copy).then_inc(self.hi_ready, 1)

            def pool_lo(self, pool, i):
                wait(pool, self.hi_ready, i + 1)
                pool.wait_ge(s_cast, 1)
                nc.gpsimd.tensor_tensor(x_lo[:], resid[:, group(i)], x_hi[:].bitcast(F32), ALU.subtract)\
                    .then_inc(self.lo_ready, 1)

        class Stream:

            def __init__(self, part, src, chunk):
                self.src, self.chunk = src, chunk
                self.loaded, self.hi_done, self.split = (sem(f"{part}_chunk_{n}") for n in ("loaded", "hi", "split"))

            def sp_load(self, sp, i):
                wait(sp, self.split, i)
                sp.dma_start(stage[:, 0:self.chunk], self.src[:, group(i, self.chunk)]).then_inc(self.loaded, 16)

            def pool_split(self, pool, i):
                c = self.chunk
                pool.wait_ge(s_cast, 1)
                wait(pool, self.loaded, 16 * i + 16)
                nc.gpsimd.tensor_copy(ffn_hi[:, group(i, c)], stage[:, 0:c]).then_inc(self.hi_done, 1)
                wait(pool, self.hi_done, i + 1)
                pool.wait_ge(s_cast, 1)
                nc.gpsimd.tensor_tensor(ffn_lo[:, group(i, c)], stage[:, 0:c], ffn_hi[:, group(i, c)].bitcast(F32),
                                        ALU.subtract).then_inc(self.split, 1)

        def three_pass(out_, w_hi, w_lo, m_hi, m_lo, start=True, stop=True):
            nc.tensor.matmul(out_, w_hi, m_hi, start=start, stop=False)
            nc.tensor.matmul(out_, w_hi, m_lo, start=False, stop=False)
            return nc.tensor.matmul(out_, w_lo, m_hi, start=False, stop=stop)

        def run(engine, first, rest):
            first(0)
            with engine.Fori(1, GROUPS) as i:
                rest(i)

        class Route:
            def __init__(self, part, e, router):
                self.e, self.router = e, router
                self.logits_ready = sem(f"{part}_logits_ready")
                self.pre_exp, self.exp_done = sem(f"{part}_route_pre_exp"), sem(f"{part}_route_exp")
                self.cw_ready = sem(f"{part}_cw_ready")
                self.part_done = sem(f"{part}_cw_part")
                self.cwT_psum = sem(f"{part}_cwT_psum")
                self.cwT_ready = sem(f"{part}_cwT_ready")
                self.logits = bank[1][:, 0:TILES * e].rearrange("p (t e) -> p t e", e=e)
                self.cwT_p = bank[1][:, GT // 2:GT].bitcast(BF16)

            def pe_logits(self, pe, i, tail):
                wait(pe, self.cwT_ready, i)
                wait(pe, tail.x_ready, i + 1)
                pe.wait_ge(s_cast, 1)
                for t in range(TILES):
                    last = nc.tensor.matmul(self.logits[:, t, :], xf[:, t * P:(t + 1) * P], self.router[:],
                                            start=True, stop=True)
                last.then_inc(self.logits_ready, 1)

            def pool_parts(self, pool, i):
                e = self.e
                pool.wait_ge(s_cast, 1)
                wait(pool, self.cwT_psum, i)
                wait(pool, self.cw_ready, i + 1)
                src = cw[:, :, 0:e]
                for k in range(3):
                    part = cw3[:, :, k * e:(k + 1) * e]
                    nc.gpsimd.tensor_copy(part, src).then_inc(self.part_done, 1)
                    wait(pool, self.part_done, 5 * i + 2 * k + 1)
                    if k < 2:
                        nc.gpsimd.tensor_tensor(rest_w[:, :, 0:e], src, part, ALU.subtract).then_inc(self.part_done, 1)
                        done = snapped(pool, 5 * i + 2 * k + 2)
                        pool.wait_ge(s_cast, 1)
                        wait(pool, self.part_done, done)
                        src = rest_w[:, :, 0:e]

            def pe_transpose(self, pe, i):
                e3 = 3 * self.e
                wait(pe, self.part_done, 5 * i + 5)
                for t in range(TILES):
                    last = nc.tensor.transpose(self.cwT_p[0:e3, t * P:(t + 1) * P], cw3[:, t, 0:e3], ident_bf[:])
                last.then_inc(self.cwT_psum, 1)

            def act_cwT(self, act, i):
                e3 = 3 * self.e
                wait(act, self.cwT_psum, i + 1)
                act.wait_ge(s_cast, 1)
                nc.scalar.activation(cwT[0:e3, group(i)], self.cwT_p[0:e3, :], ACT.Copy).then_inc(self.cwT_ready, 1)

        class RouteTop2(Route):

            def dve_1(self, dve, i):
                wait(dve, self.part_done, 5 * i)
                wait(dve, self.logits_ready, i + 1)
                nc.vector.tensor_tensor(lg[:, :, 0:8], self.logits, bias0_sb[:].unsqueeze(1).broadcast_to([P, TILES, 8]),
                                        ALU.add)
                dve.drain()
                for t in range(TILES):
                    nc.vector.max(top[:, t, :], lg[:, t, 0:8])
                dve.drain()
                for t in range(TILES):
                    nc.vector.max_index(idx[:, t, :], top[:, t, :], lg[:, t, 0:8])
                nc.vector.tensor_tensor(pair[:, 0, :], top[:, :, 1], top[:, :, 0], ALU.subtract).then_inc(self.pre_exp, 1)

            def act_exp(self, act, i):
                wait(act, self.pre_exp, i + 1)
                nc.scalar.activation(pair[:, 1, :], pair[:, 0, :], ACT.Exp).then_inc(self.exp_done, 1)

            def dve_2(self, dve, i):
                dve.drain()
                nc.vector.tensor_copy(idxf[:], idx[:])
                dve.drain()
                wait(dve, self.exp_done, i + 1)
                nc.vector.tensor_scalar(pair[:, 2, :], pair[:, 1, :], 1.0, None, ALU.add)
                dve.drain()
                nc.vector.reciprocal(pair[:, 2, :], pair[:, 2, :])
                dve.drain()
                nc.vector.tensor_tensor(pair[:, 3, :], pair[:, 1, :], pair[:, 2, :], ALU.mult)
                io = iota8[:].unsqueeze(1).broadcast_to([P, TILES, 8])
                for k, m in ((0, gmask), (1, gsum)):
                    nc.vector.tensor_tensor(m[:], io, idxf[:, :, k:k + 1].broadcast_to([P, TILES, 8]), ALU.is_equal)
                dve.drain()
                for k, m in ((2, gmask), (3, gsum)):
                    nc.vector.tensor_tensor(m[:], m[:], pair[:, k, :].unsqueeze(2).broadcast_to([P, TILES, 8]), ALU.mult)
                dve.drain()
                nc.vector.tensor_tensor(cw[:, :, 0:8], gmask[:], gsum[:], ALU.add).then_inc(self.cw_ready, 1)

        class RouteGrouped(Route):

            def act_exp(self, act, i):
                wait(act, self.logits_ready, i + 1)
                nc.scalar.activation(lg[:], self.logits, ACT.Exp, scale=-1.0).then_inc(self.exp_done, 1)

            def dve_1(self, dve, i):
                wait(dve, self.exp_done, i + 1)
                nc.vector.tensor_scalar(lg[:], lg[:], 1.0, None, ALU.add)
                dve.drain()
                nc.vector.reciprocal(sg[:], lg[:]).then_inc(self.pre_exp, 1)
                dve.drain()
                nc.vector.tensor_reduce(gsum[:], sg[:].rearrange("p t (g k) -> p t g k", k=L1_PER), AX, ALU.add)
                dve.drain()
                for t in range(TILES):
                    nc.vector.max(top[:, t, :], gsum[:, t, :])
                dve.drain()
                for t in range(TILES):
                    nc.vector.max_index(idx[:, t, :], top[:, t, :], gsum[:, t, :])
                dve.drain()
                nc.vector.tensor_copy(idxf[:], idx[:])
                dve.drain()

            def dve_2(self, dve, i):
                for t in range(TILES):
                    nc.vector.tensor_tensor(eq4[:, t, :, :], iota8[:].unsqueeze(2).broadcast_to([P, 8, 4]),
                                            idxf[:, t, 0:4].unsqueeze(1).broadcast_to([P, 8, 4]), ALU.is_equal)
                dve.drain()
                nc.vector.tensor_reduce(gmask[:], eq4[:], AX, ALU.add)
                dve.drain()
                nc.vector.tensor_tensor(sg[:].rearrange("p t (g k) -> p (t g) k", k=L1_PER),
                                        sg[:].rearrange("p t (g k) -> p (t g) k", k=L1_PER),
                                        gmask[:].rearrange("p t g -> p (t g)").unsqueeze(2)
                                        .broadcast_to([P, TILES * 8, L1_PER]), ALU.mult)
                dve.drain()
                for t in range(TILES):
                    nc.vector.max(top[:, t, :], sg[:, t, :])
                dve.drain()
                for t in range(TILES):
                    nc.vector.match_replace(lg[:, t, :], top[:, t, :], sg[:, t, :], 0.0)
                nc.vector.tensor_reduce(pair[:, 0, :], top[:], AX, ALU.add)
                dve.drain()
                nc.vector.tensor_scalar(pair[:, 0, :], pair[:, 0, :], EPS_TOPK, None, ALU.max)
                nc.vector.tensor_tensor(sg[:], sg[:], lg[:], ALU.subtract)
                dve.drain()
                nc.vector.reciprocal(pair[:, 1, :], pair[:, 0, :])
                dve.drain()
                wait(dve, self.part_done, 5 * i)
                nc.vector.tensor_tensor(cw[:], sg[:], pair[:, 1, :].unsqueeze(2).broadcast_to([P, TILES, L1_E]),
                                        ALU.mult).then_inc(self.cw_ready, 1)

        def attention0():
            s = lambda n: sem(f"a0_{n}")
            route = RouteTop2("a0", L0_E, router0_sb)
            tail, split, stream = Tail("a0", route=route), Split("a0"), Stream("a0", w_ffn0, CH0)
            x_loaded = s("x_loaded")
            k_ready, q_ready, v_ready = s("k_ready"), s("q_ready"), s("v_ready")
            ek_ready, eq_ready = s("exp_k_ready"), s("exp_q_ready")
            sk_ready, sq_ready = s("sk_ready"), s("sq_ready")
            kv_ready, cum_ready = s("kv_ready"), s("cum_ready")
            qk_ready, qkv_ready = s("qk_ready"), s("qkv_ready")
            rel_ready, den_ready = s("rel_ready"), s("den_ready")
            rs_ready, rsT_ready, dlt_ready, ew_ready = s("relsum"), s("relsum_T"), s("softmax_in"), s("softmax_exp")
            w_ready, wT_ready, wcol_ready = s("w_ready"), s("w_T"), s("wcol_ready")
            rec_ready, r_ready = s("reciprocals"), s("factors")
            bc_ready, qm_ready = s("spread_ready"), s("qm_ready")
            acc_ready, o_ready, wo_ready = s("acc_ready"), s("o_ready"), s("wo_ready")
            ORDER = [MEMS, 0, 1, 2, 3]

            with ExitStack() as own:
                def tb(name, shape, dt=F32):
                    return own.enter_context(nc.sbuf_tensor(f"a0_{name}", shape, dt))

                ek, eq, sq, sq4 = tb("ek", [P, GT]), tb("eq", [P, GT]), tb("sq", [P, GT]), tb("sq4", [P, GT])
                kv = tb("kv", [P, 3, GT])
                cum = tb("cum", [P, L0_D + 1, GT])
                qkv = tb("qkv", [P, 3, GT])
                relsum, rowT = tb("relsum", [REL, SEQS]), tb("rowT", [SEQS, REL])
                erow, mx, wrow = tb("erow", [SEQS, REL]), tb("mx", [SEQS, L0_HEADS]), tb("wrow", [SEQS, REL])
                clip, rec, fac = tb("clip", [DEN, GT]), tb("rec", [DEN, GT]), tb("fac", [DEN, GT])
                qm = tb("qm", [P, 2, GT])
                o_sb = tb("o_sb", [P, GT])
                ring, spreadP, denP, acc = bank[2:4], bank[5:7], bank[4], bank[7]
                rsT, wT = bank[1][0:SEQS, 128:128 + REL], bank[1][0:REL, 192:192 + SEQS]
                block = own.enter_context(nc.Block())

                @block.sync
                def _(sp):
                    sp.dma_start(resid[:, 0:GT], xT[:, 0:GT]).then_inc(x_loaded, 16)
                    with sp.Fori(0, GROUPS - 1) as i:
                        wait(sp, x_loaded, 16 * i + 16)
                        sp.dma_start(resid[:, bass.ds(i * GT + GT, GT)], xT[:, bass.ds(i * GT + GT, GT)])\
                            .then_inc(x_loaded, 16)
                    stream.sp_load(sp, 0)
                    with sp.Fori(1, GROUPS) as i:
                        stream.sp_load(sp, i)

                @block.tensor
                def _(pe):
                    def body(i):
                        wait(pe, split.lo_ready, i + 1)
                        wait(pe, kv_ready, 8 * i - 1)
                        three_pass(ring[0][:], wl0_hi[:, 1, :], wl0_lo[:, 1, :], x_hi[:], x_lo[:]).then_inc(k_ready, 1)
                        wait(pe, kv_ready, 8 * i)
                        three_pass(ring[1][:], wl0_hi[:, 0, :], wl0_lo[:, 0, :], x_hi[:], x_lo[:]).then_inc(q_ready, 1)
                        for e in range(L0_D):
                            if e == 0:
                                wait(pe, sk_ready, i + 1)
                            elif e == 1:
                                wait(pe, sq_ready, i + 1)
                            else:
                                wait(pe, kv_ready, 8 * i + e - 1)
                            three_pass(ring[e % 2][:], wl0_hi[:, 2 + e, :], wl0_lo[:, 2 + e, :], x_hi[:], x_lo[:])\
                                .then_inc(v_ready, 1)
                            if e == 1:
                                wait(pe, tail.y_ready, i)
                                nc.tensor.matmul(denP[0:REL, :], norms_sb[:], sq[:], start=True, stop=True)\
                                    .then_inc(rel_ready, 1)
                            if e == 4:
                                wait(pe, qk_ready, i + 1)
                                nc.tensor.matmul(denP[REL:DEN, :], headsum[:], qkv[:, 2, :], start=True, stop=True)\
                                    .then_inc(den_ready, 1)
                            if e == 3:
                                pe.wait_ge(s_cast, 1)
                                wait(pe, rs_ready, i + 1)
                                nc.tensor.transpose(rsT, relsum[:], ident[0:REL, 0:REL]).then_inc(rsT_ready, 1)
                        pe.wait_ge(s_cast, 1)
                        wait(pe, w_ready, i + 1)
                        nc.tensor.transpose(wT, wrow[:], ident[0:SEQS, 0:SEQS]).then_inc(wT_ready, 1)
                        wait(pe, r_ready, i + 1)
                        for o, j in enumerate(ORDER):
                            wait(pe, qm_ready, last_use(i, o, 5, 2))
                            nc.tensor.matmul(spreadP[o % 2][:], spread[:, j, :], fac[:], start=True, stop=True)\
                                .then_inc(bc_ready, 1)
                            if o >= 2:
                                if o == 2:
                                    wait(pe, o_ready, i)
                                wait(pe, qm_ready, 5 * i + o)
                                nc.tensor.matmul(acc[:], mem_sb[:, o - 2, :], qm[:, o % 2, :], start=(o == 2), stop=False)\
                                    .then_inc(acc_ready, 1)
                        wait(pe, qm_ready, 5 * i + 5)
                        nc.tensor.matmul(acc[:], mem_sb[:, 3, :], qm[:, 1, :], start=False, stop=False).then_inc(acc_ready, 1)
                        for e in range(L0_D):
                            wait(pe, qkv_ready, 8 * i + e + 1)
                            nc.tensor.matmul(acc[:], blocksum[:, e, :], qkv[:, e % 2, :], start=False, stop=(e == L0_D - 1))\
                                .then_inc(acc_ready, 1)
                        wait(pe, o_ready, i + 1)
                        nc.tensor.matmul(denP[:], wo0[:], o_sb[:], start=True, stop=True).then_inc(wo_ready, 1)
                        tail.pe_tokens(pe, i)
                        tail.pe_features(pe, i)
                        route.pe_logits(pe, i, tail)
                        route.pe_transpose(pe, i)

                    run(pe, body, body)

                @block.scalar
                def _(act):
                    def body(i):
                        wait(act, k_ready, i + 1)
                        nc.scalar.activation(ek[:], ring[0][:], ACT.Exp).then_inc(ek_ready, 1)
                        wait(act, q_ready, i + 1)
                        nc.scalar.activation(eq[:], ring[1][:], ACT.Exp).then_inc(eq_ready, 1)
                        wait(act, dlt_ready, i + 1)
                        nc.scalar.activation(erow[:], rowT[:], ACT.Exp, scale=1.0 / SEQ).then_inc(ew_ready, 1)
                        wait(act, wcol_ready, i + 1)
                        wait(act, rec_ready, i + 1)
                        for q in range(SEQS):
                            cols = slice(q * SEQ, (q + 1) * SEQ)
                            last = nc.scalar.activation(fac[:, cols], rec[:, cols], ACT.Copy, scale=wcol[:, q:q + 1])
                        last.then_inc(r_ready, 1)
                        wait(act, acc_ready, 12 * i + 12)
                        nc.scalar.activation(o_sb[:], acc[:], ACT.Copy).then_inc(o_ready, 1)
                        tail.act_resid(act, i)
                        route.act_exp(act, i)
                        route.act_cwT(act, i)

                    def prepare(i):
                        wait(act, x_loaded, 16 * i + 16)
                        act.wait_ge(s_cast, 1)
                        split.act_hi(act, i)

                    prepare(0)
                    body(0)
                    with act.Fori(1, GROUPS) as i:
                        wait(act, v_ready, 8 * i)
                        prepare(i)
                        body(i)

                @block.vector
                def _(dve):
                    def body(i):
                        for e_ready, e_sb, src, dst, done in ((ek_ready, ek, ring[0], kv[:, 2, :], sk_ready),
                                                              (eq_ready, eq, ring[1], sq[:], sq_ready)):
                            wait(dve, e_ready, i + 1)
                            nc.vector.tensor_scalar(e_sb[:], e_sb[:], 1.0, None, ALU.min)
                            dve.drain()
                            if done is sk_ready:
                                wait(dve, cum_ready, 9 * i)
                            else:
                                wait(dve, qkv_ready, 8 * i)
                            nc.vector.scalar_tensor_tensor(out=dst, in0=src[:], scalar=0.0, in1=e_sb[:], op0=ALU.max,
                                                           op1=ALU.add).then_inc(done, 1)
                        wait(dve, sk_ready, i + 1)
                        nc.vector.tensor_tensor_scan(cum[:, L0_D, :], reset[:], kv[:, 2, :], 0.0, ALU.mult, ALU.add)\
                            .then_inc(cum_ready, 1)
                        wait(dve, rel_ready, i + 1)
                        nc.vector.tensor_reduce(relsum[:], denP[0:REL, :].rearrange("p (s n) -> p s n", s=SEQS), AX, ALU.add)\
                            .then_inc(rs_ready, 1)

                        def product(e):
                            wait(dve, cum_ready, 9 * i + e if e >= 2 else 9 * (i - 1) + 8 + e)
                            wait(dve, v_ready, 8 * i + e + 1)
                            nc.vector.tensor_tensor(kv[:, e % 2, :], ring[e % 2][:], kv[:, 2, :], ALU.mult).then_inc(kv_ready, 1)

                        def running(e):
                            wait(dve, kv_ready, 8 * i + e + 1)
                            nc.vector.tensor_tensor_scan(cum[:, e, :], reset[:], kv[:, e % 2, :], 0.0, ALU.mult, ALU.add)\
                                .then_inc(cum_ready, 1)

                        product(0)
                        for e in range(1, L0_D):
                            product(e)
                            running(e - 1)
                            if e == 5:
                                wait(dve, rsT_ready, i + 1)
                                nc.vector.tensor_reduce(mx[:], rsT.rearrange("p (m h) -> p h m", m=MEMS), AX, ALU.max)
                                dve.drain()
                                nc.vector.tensor_tensor(rowT[:].rearrange("p (m h) -> p m h", m=MEMS),
                                                        rsT.rearrange("p (m h) -> p m h", m=MEMS),
                                                        mx[:].unsqueeze(1).broadcast_to([SEQS, MEMS, L0_HEADS]),
                                                        ALU.subtract).then_inc(dlt_ready, 1)
                            if e == 7:
                                wait(dve, ew_ready, i + 1)
                                nc.vector.tensor_reduce(mx[:], erow[:].rearrange("p (m h) -> p h m", m=MEMS), AX, ALU.add)
                                dve.drain()
                                nc.vector.reciprocal(mx[:], mx[:])
                                dve.drain()
                                nc.vector.tensor_tensor(mx[:], mx[:], gate_row[:], ALU.mult)
                                dve.drain()
                                nc.vector.tensor_tensor(wrow[:].rearrange("p (m h) -> p m h", m=MEMS),
                                                        erow[:].rearrange("p (m h) -> p m h", m=MEMS),
                                                        mx[:].unsqueeze(1).broadcast_to([SEQS, MEMS, L0_HEADS]),
                                                        ALU.mult).then_inc(w_ready, 1)
                        wait(dve, den_ready, i + 1)
                        nc.vector.tensor_scalar(clip[:], denP[0:DEN, :], EPS_DEN, None, ALU.max)
                        dve.drain()
                        nc.vector.reciprocal(rec[:], clip[:]).then_inc(rec_ready, 1)
                        running(L0_D - 1)
                        wait(dve, wT_ready, i + 1)
                        nc.vector.tensor_copy(wcol[0:REL, :], wT).then_inc(wcol_ready, 1)
                        for o in range(5):
                            if o == 0:
                                wait(dve, qkv_ready, 8 * i)
                            else:
                                wait(dve, acc_ready, 12 * i + o - 2 if o >= 3 else 12 * (i - 1) + 4)
                            wait(dve, bc_ready, 5 * i + o + 1)
                            nc.vector.tensor_tensor(sq4[:] if o == 0 else qm[:, (o - 1) % 2, :], spreadP[o % 2][:], sq[:],
                                                    ALU.mult).then_inc(qm_ready, 1)
                        wait(dve, tail.tok_ready, i)
                        wait(dve, wo_ready, i + 1)
                        nc.vector.tensor_tensor(y_sb[:], denP[:], resid[:, group(i)], ALU.add).then_inc(tail.y_ready, 1)
                        tail.dve_stats(dve, i)
                        tail.dve_normalise(dve, i)
                        route.dve_1(dve, i)
                        route.dve_2(dve, i)

                    run(dve, body, body)

                @block.gpsimd
                def _(pool):
                    def body(i):
                        wait(pool, den_ready, i)
                        wait(pool, sq_ready, i + 1)
                        wait(pool, cum_ready, 9 * i + 1)
                        nc.gpsimd.tensor_tensor(qkv[:, 2, :], cum[:, L0_D, :], sq[:], ALU.mult).then_inc(qk_ready, 1)
                        stream.pool_split(pool, i)
                        wait(pool, qm_ready, 5 * i + 1)
                        for e in range(L0_D):
                            wait(pool, acc_ready, 12 * i + 4 + e - 1 if e >= 2 else 12 * (i - 1) + 12 - 1 + e)
                            wait(pool, cum_ready, 9 * i + e + 2)
                            nc.gpsimd.tensor_tensor(qkv[:, e % 2, :], cum[:, e, :], sq4[:], ALU.mult).then_inc(qkv_ready, 1)
                        tail.pool_rstd(pool, i)
                        route.pool_parts(pool, i)

                    split.pool_lo(pool, 0)
                    body(0)
                    with pool.Fori(1, GROUPS) as i:
                        split.pool_lo(pool, i)
                        body(i)

        def attention1():
            s = lambda n: sem(f"a1_{n}")
            route = RouteGrouped("a1", L1_E, router1_sb)
            tail, split, stream = Tail("a1", route=route), Split("a1"), Stream("a1", w_ffn1, CH1)
            H, U = L1_HEADS, L1_HEADS * SEQS
            kp_ready, vp_ready, qp_ready = s("k_psum"), s("v_psum"), s("q_psum")
            k_ready, v_ready, q_ready = s("k_ready"), s("v_ready"), s("q_ready")
            sc_ready, nm_ready = s("scores_ready"), s("masked_ready")
            e_ready, r_ready, p_ready = s("exp_ready"), s("recip_ready"), s("probs_ready")
            tr_ready, pt_ready = s("probsT_psum"), s("probsT_ready")
            pv_ready, at_ready, acc_ready = s("pv_ready"), s("attn_ready"), s("acc_ready")

            with ExitStack() as own:
                def tb(name, shape, dt=F32):
                    return own.enter_context(nc.sbuf_tensor(f"a1_{name}", shape, dt))

                kT, vt, qT = tb("kT", [P, GT]), tb("vt", [P, TILES, P]), tb("qT", [P, 2, GT])
                SC = 3 * P
                ms, ex, pn = tb("ms", [P, 2, SC]), tb("ex", [P, 2, SC]), tb("pn", [P, 2, SC])
                mx, nm, rs, rr = (tb(n, [P, 2, 2]) for n in ("mx", "nm", "rs", "rr"))
                pT = tb("pT", [P, 2, SEQS, SC])
                at = tb("at", [P, H, GT])
                ring, scP, trP, pvP = bank[2:4], bank[4:6], bank[6], bank[7]
                wl1_hi, wl1_lo = tb("wl1_hi", [P, 10, P], F32R), tb("wl1_lo", [P, 10, P], F32R)
                wo1 = tb("wo1", [P, L1_HEADS, P])
                b_sb, bv_sb, pe_sb = tb("b_sb", [P, 9]), tb("bv_sb", [P, P]), tb("pe_sb", [P, GT])
                tri = tb("tri", [P, 2, P])
                raw1 = at[:, 0:4, :].rearrange("p a b -> p (a b)")[:, 0:10 * P].rearrange("p (a b) -> p a b", a=10)
                w_loaded, w_split = s("w_loaded"), s("w_split")
                with nc.Block() as setup:
                    @setup.sync
                    def _(sp):
                        sp.dma_start(raw1, w_l1).then_inc(w_loaded, 16)
                        sp.dma_start(wo1[:], wo_l1).then_inc(w_loaded, 16)
                        sp.dma_start(b_sb[:], b_l1).then_inc(w_loaded, 16)
                        sp.dma_start(bv_sb[:], bv_l1.partition_broadcast(P)).then_inc(w_loaded, 16)
                        sp.dma_start(pe_sb[:], peT).then_inc(w_loaded, 16)
                        sp.dma_start(tri[:], c_tri).then_inc(w_loaded, 16)

                    @setup.vector
                    def _(dve):
                        dve.wait_ge(w_loaded, 96)
                        nc.vector.tensor_copy(wl1_hi[:], raw1).then_inc(w_split, 1)
                        dve.wait_ge(w_split, 1)
                        nc.vector.tensor_tensor(wl1_lo[:], raw1, wl1_hi[:].bitcast(F32), ALU.subtract).then_inc(w_split, 1)
                        dve.wait_ge(w_split, 2)
                block = own.enter_context(nc.Block())

                @block.sync
                def _(sp):
                    stream.sp_load(sp, 0)
                    with sp.Fori(1, GROUPS) as i:
                        stream.sp_load(sp, i)

                @block.tensor
                def _(pe):
                    def body(i):
                        def project_q(h):
                            if h == 0:
                                wait(pe, k_ready, i + 1)
                            elif h == 1:
                                wait(pe, v_ready, i + 1)
                            else:
                                wait(pe, q_ready, H * i + h - 1)
                            three_pass(ring[h % 2][:], wl1_hi[:, h, :], wl1_lo[:, h, :], x_hi[:], x_lo[:]).then_inc(qp_ready, 1)

                        wait(pe, split.lo_ready, i + 1)
                        wait(pe, q_ready, H * i - 1)
                        three_pass(ring[0][:], wl1_hi[:, H, :], wl1_lo[:, H, :], x_hi[:], x_lo[:]).then_inc(kp_ready, 1)
                        wait(pe, q_ready, H * i)
                        for t in range(TILES):
                            c = slice(t * P, (t + 1) * P)
                            last = three_pass(ring[1][:, c], x_hi[:, c], x_lo[:, c], wl1_hi[:, H + 1, :], wl1_lo[:, H + 1, :])
                        last.then_inc(vp_ready, 1)
                        project_q(0)
                        for h in range(H + 2):
                            if h + 1 < H:
                                project_q(h + 1)
                            if h < H:
                                wait(pe, q_ready, H * i + h + 1)
                                for q in range(SEQS):
                                    u = SEQS * h + q
                                    wait(pe, nm_ready, U * i + u - 1)
                                    o = q * SEQ
                                    nc.tensor.matmul(scP[u % 2][:, 0:P], qT[:, h % 2, o:o + P], kT[:, o:o + P],
                                                     start=True, stop=True)
                                    nc.tensor.matmul(scP[u % 2][:, P:SC], qT[:, h % 2, o + P:o + SEQ], kT[:, o:o + SEQ],
                                                     start=True, stop=True).then_inc(sc_ready, 1)
                            if 1 <= h <= H:
                                for q in range(SEQS):
                                    u = SEQS * (h - 1) + q
                                    wait(pe, pt_ready, U * i + u)
                                    wait(pe, p_ready, U * i + u + 1)
                                    for b, c in enumerate((0, P, 2 * P)):
                                        last = nc.tensor.transpose(trP[:, b * P:(b + 1) * P], pn[:, u % 2, c:c + P], ident[:])
                                    last.then_inc(tr_ready, 1)
                            if h >= 2:
                                g = h - 2
                                if g == 0:
                                    wait(pe, tail.y_ready, i)
                                else:
                                    wait(pe, at_ready, H * i + g)
                                wait(pe, pt_ready, U * i + SEQS * g + SEQS)
                                for q in range(SEQS):
                                    nc.tensor.matmul(pvP[:, q * SEQ:(q + 1) * SEQ], vt[:, 2 * q, :],
                                                     pT[:, g % 2, q, 0:SEQ], start=True, stop=False)
                                    last = nc.tensor.matmul(pvP[:, q * SEQ + P:(q + 1) * SEQ], vt[:, 2 * q + 1, :],
                                                            pT[:, g % 2, q, SEQ:SC], start=False, stop=True)
                                last.then_inc(pv_ready, 1)
                        wait(pe, at_ready, H * i + H)
                        for h in range(H):
                            last = nc.tensor.matmul(pvP[:], wo1[:, h, :], at[:, h, :], start=(h == 0), stop=(h == H - 1))
                        last.then_inc(acc_ready, 1)
                        tail.pe_tokens(pe, i)
                        tail.pe_features(pe, i)
                        route.pe_logits(pe, i, tail)
                        route.pe_transpose(pe, i)

                    run(pe, body, body)

                @block.scalar
                def _(act):
                    def body(i):
                        for h in range(H + 2):
                            if h < H:
                                for q in range(SEQS):
                                    u = SEQS * h + q
                                    wait(act, p_ready, U * i + u - 1)
                                    wait(act, nm_ready, U * i + u + 1)
                                    for b, c in enumerate((slice(0, P), slice(P, SC))):
                                        last = nc.scalar.activation(ex[:, u % 2, c], ms[:, u % 2, c], ACT.Exp, scale=SCALE,
                                                                    bias=nm[:, u % 2, b:b + 1], accum_out=rs[:, u % 2, b:b + 1])
                                    last.then_inc(e_ready, 1)
                            if 1 <= h <= H:
                                for q in range(SEQS):
                                    u = SEQS * (h - 1) + q
                                    if h >= 3:
                                        wait(act, pv_ready, H * i + h - 2)
                                    else:
                                        wait(act, pv_ready, H * (i - 1) + H - 2 + h)
                                    wait(act, tr_ready, U * i + u + 1)
                                    nc.scalar.activation(pT[:, (h - 1) % 2, q, :], trP[:, 0:SC], ACT.Copy).then_inc(pt_ready, 1)
                            if h >= 2:
                                g = h - 2
                                if g == 0:
                                    wait(act, acc_ready, i)
                                wait(act, pv_ready, H * i + g + 1)
                                nc.scalar.activation(at[:, g, :], pvP[:], ACT.Copy).then_inc(at_ready, 1)
                        tail.act_resid(act, i)
                        route.act_exp(act, i)
                        route.act_cwT(act, i)

                    split.act_hi(act, 0)
                    body(0)
                    with act.Fori(1, GROUPS) as i:
                        wait(act, qp_ready, H * i)
                        act.wait_ge(s_cast, 1)
                        split.act_hi(act, i)
                        body(i)

                @block.vector
                def _(dve):
                    def body(i):
                        wait(dve, sc_ready, U * i)
                        wait(dve, kp_ready, i + 1)
                        nc.vector.scalar_tensor_tensor(out=kT[:], in0=ring[0][:], scalar=b_sb[:, H:H + 1], in1=pe_sb[:],
                                                       op0=ALU.add, op1=ALU.add).then_inc(k_ready, 1)
                        wait(dve, pv_ready, H * i)
                        wait(dve, vp_ready, i + 1)
                        nc.vector.tensor_tensor(vt[:], ring[1][:].rearrange("p (t n) -> p t n", t=TILES),
                                                bv_sb[:].unsqueeze(1).broadcast_to([P, TILES, P]), ALU.add).then_inc(v_ready, 1)

                        def evacuate_q(h):
                            wait(dve, sc_ready, U * i + SEQS * (h - 1) if h >= 2 else U * (i - 1) + U - SEQS * (1 - h))
                            wait(dve, qp_ready, H * i + h + 1)
                            nc.vector.scalar_tensor_tensor(out=qT[:, h % 2, :], in0=ring[h % 2][:], scalar=b_sb[:, h:h + 1],
                                                           in1=pe_sb[:], op0=ALU.add, op1=ALU.add).then_inc(q_ready, 1)

                        evacuate_q(0)
                        for h in range(H + 1):
                            if h >= 1:
                                for q in range(SEQS):
                                    u = SEQS * (h - 1) + q
                                    wait(dve, e_ready, U * i + u + 1)
                                    nc.vector.reciprocal(rr[:, u % 2, :], rs[:, u % 2, :]).then_inc(r_ready, 1)
                            if h + 1 < H:
                                evacuate_q(h + 1)
                            if h < H:
                                for q in range(SEQS):
                                    u = SEQS * h + q
                                    read, scored = snapped(dve, U * i + u - 1), snapped(dve, U * i + u + 1)
                                    dve.wait_ge(s_cast, 1)
                                    wait(dve, e_ready, read)
                                    wait(dve, sc_ready, scored)
                                    nc.vector.tensor_tensor_reduce(out=ms[:, u % 2, 0:P], in0=scP[u % 2][:, 0:P], in1=tri[:, 1, :],
                                                                   scale=1.0, scalar=MASKED, op0=ALU.add, op1=ALU.max,
                                                                   accum_out=mx[:, u % 2, 0:1])
                                    nc.vector.tensor_tensor_reduce(out=ms[:, u % 2, P:SC], in0=scP[u % 2][:, P:SC],
                                                                   in1=tri[:].rearrange("p a b -> p (a b)"),
                                                                   scale=1.0, scalar=MASKED, op0=ALU.add, op1=ALU.max,
                                                                   accum_out=mx[:, u % 2, 1:2])
                                    dve.drain()
                                    nc.vector.tensor_scalar(nm[:, u % 2, :], mx[:, u % 2, :], -SCALE, None, ALU.mult)\
                                        .then_inc(nm_ready, 1)
                        wait(dve, tail.tok_ready, i)
                        wait(dve, acc_ready, i + 1)
                        nc.vector.tensor_tensor(y_sb[:], pvP[:], resid[:, group(i)], ALU.add).then_inc(tail.y_ready, 1)
                        tail.dve_stats(dve, i)
                        tail.dve_normalise(dve, i)
                        route.dve_1(dve, i)
                        route.dve_2(dve, i)

                    run(dve, body, body)

                @block.gpsimd
                def _(pool):
                    def body(i):
                        split.pool_lo(pool, i)
                        for u in range(U):
                            wait(pool, tr_ready, U * i + u - 1)
                            wait(pool, r_ready, U * i + u + 1)
                            nc.gpsimd.tensor_tensor(pn[:, u % 2, 0:P], ex[:, u % 2, 0:P],
                                                    rr[:, u % 2, 0:1].broadcast_to([P, P]), ALU.mult)
                            nc.gpsimd.tensor_tensor(pn[:, u % 2, P:SC], ex[:, u % 2, P:SC],
                                                    rr[:, u % 2, 1:2].broadcast_to([P, SC - P]), ALU.mult).then_inc(p_ready, 1)
                            if u == 4:
                                stream.pool_split(pool, i)
                        tail.pool_rstd(pool, i)
                        route.pool_parts(pool, i)

                    run(pool, body, body)

        def experts(part, NT, routed, per_weight, sel, e3, last):
            s = lambda n: sem(f"{part}_{n}")
            tail, split = Tail(part, last=last), Split(part)
            NB = routed // per_weight
            gu_ready, bc_ready = s("gate_up_ready"), s("weight_psum")
            s_ready, bw_ready = s("silu_ready"), s("weight_ready")
            w_ready = s("weighted_ready")
            h_ready, hhi_ready, hlo_ready = s("h_ready"), s("h_hi_ready"), s("h_lo_ready")
            down_ready = s("down_done")
            LAG = 2
            GATE, UP, DOWN = 0, NT * P, 2 * NT * P

            def w(which, base, t):
                return which[:, base + t * P:base + (t + 1) * P]

            def was_broadcast(i, t):
                return t

            with ExitStack() as own:
                def tb(name, shape, dt=F32):
                    return own.enter_context(nc.sbuf_tensor(f"{part}_{name}", shape, dt))

                sl, sw, bw = tb("sl", [P, 2, GT]), tb("sw", [P, 2, GT]), tb("bw", [P, 2, GT])
                hh, h_hi, h_lo = tb("hh", [P, 2, GT]), tb("h_hi", [P, 2, GT], F32R), tb("h_lo", [P, 2, GT], F32R)
                bcP, gP, uP, acc = bank[1], bank[2:4], bank[4:6], bank[6]
                block = own.enter_context(nc.Block())

                if last:
                    @block.sync
                    def _(sp):
                        def body(i):
                            tail.sp_store(sp, i)
                        run(sp, body, body)
                        sp.wait_ge(tail.stored, 16 * GROUPS)

                @block.tensor
                def _(pe):
                    def down(i, t):
                        if t == 0:
                            wait(pe, tail.y_ready, i)
                        wait(pe, hlo_ready, NT * i + t + 1)
                        three_pass(acc[:], w(ffn_hi, DOWN, t), w(ffn_lo, DOWN, t), h_hi[:, t % 2, :], h_lo[:, t % 2, :],
                                   start=(t == 0), stop=(t == NT - 1)).then_inc(down_ready, 1)

                    def body(i, prev):
                        wait(pe, split.lo_ready, i + 1)
                        for t in range(NT):
                            if t < routed and t % per_weight == 0:
                                b = t // per_weight
                                read = snapped(pe, NB * i + b)
                                pe.wait_ge(s_cast, 1)
                                wait(pe, bw_ready, read)
                                nc.tensor.matmul(bcP[:], sel[:, b, :], cwT[0:e3, group(i)], start=True, stop=True)\
                                    .then_inc(bc_ready, 1)
                            wait(pe, h_ready, last_use(i, t, NT, 2))
                            three_pass(gP[t % 2][:], w(ffn_hi, GATE, t), w(ffn_lo, GATE, t), x_hi[:], x_lo[:])
                            three_pass(uP[t % 2][:], w(ffn_hi, UP, t), w(ffn_lo, UP, t), x_hi[:], x_lo[:])\
                                .then_inc(gu_ready, 1)
                            if t >= LAG:
                                down(i, t - LAG)
                            if prev is not None and t == 3:
                                tail.pe_tokens(pe, prev)
                            if prev is not None and t == 7:
                                tail.pe_features(pe, prev)
                        for t in range(NT - LAG, NT):
                            down(i, t)

                    body(0, None)
                    with pe.Fori(1, GROUPS) as i:
                        body(i, i - 1)
                    tail.pe_tokens(pe, GROUPS - 1)
                    tail.pe_features(pe, GROUPS - 1)

                @block.scalar
                def _(act):
                    def high(i, t):
                        wait(act, down_ready, last_use(i, t, NT, 2))
                        wait(act, h_ready, NT * i + t + 1)
                        nc.scalar.activation(h_hi[:, t % 2, :], hh[:, t % 2, :], ACT.Copy).then_inc(hhi_ready, 1)

                    def body(i, prev):
                        for t in range(NT):
                            if t < routed and t % per_weight == 0:
                                b = t // per_weight
                                wait(act, h_ready, NT * i + t - per_weight if b >= 2 else NT * (i - 1) + routed)
                                wait(act, bc_ready, NB * i + b + 1)
                                nc.scalar.activation(bw[:, b % 2, :], bcP[:], ACT.Copy).then_inc(bw_ready, 1)
                            wait(act, h_ready, last_use(i, t, NT, 2))
                            wait(act, gu_ready, NT * i + t + 1)
                            nc.scalar.activation(sl[:, t % 2, :], gP[t % 2][:], ACT.Silu).then_inc(s_ready, 1)
                            if t >= 1:
                                high(i, t - 1)
                            if prev is not None and not last and t == 8:
                                tail.act_resid(act, prev)
                        if prev is None or not isinstance(i, int):
                            pass

                    split.act_hi(act, 0)
                    body(0, None)

                    def prepare(i):
                        wait(act, gu_ready, NT * i)
                        act.wait_ge(s_cast, 1)
                        split.act_hi(act, i)
                        high(i - 1, NT - 1)

                    with act.Fori(1, GROUPS) as i:
                        prepare(i)
                        body(i, i - 1)
                    high(GROUPS - 1, NT - 1)
                    if not last:
                        tail.act_resid(act, GROUPS - 1)

                @block.vector
                def _(dve):
                    def low(i, t):
                        wait(dve, down_ready, last_use(i, t, NT, 2))
                        wait(dve, hhi_ready, NT * i + t + 1)
                        nc.vector.tensor_tensor(h_lo[:, t % 2, :], hh[:, t % 2, :], h_hi[:, t % 2, :].bitcast(F32),
                                                ALU.subtract).then_inc(hlo_ready, 1)

                    def body(i, prev):
                        for t in range(NT):
                            wait(dve, hlo_ready, last_use(i, t, NT, 2))
                            wait(dve, gu_ready, NT * i + t + 1)
                            if t < routed:
                                wait(dve, w_ready, routed * i + t + 1)
                            else:
                                wait(dve, s_ready, NT * i + t + 1)
                            nc.vector.tensor_tensor(hh[:, t % 2, :], uP[t % 2][:], (sw if t < routed else sl)[:, t % 2, :],
                                                    ALU.mult).then_inc(h_ready, 1)
                            if t >= 1:
                                low(i, t - 1)
                            if prev is not None and t == 4:
                                tail.dve_stats(dve, prev)
                            if prev is not None and t == 5:
                                tail.dve_normalise(dve, prev)
                        low(i, NT - 1)
                        wait(dve, tail.tok_ready, i)
                        wait(dve, down_ready, NT * i + NT)
                        nc.vector.tensor_tensor(y_sb[:], acc[:], resid[:, group(i)], ALU.add).then_inc(tail.y_ready, 1)

                    body(0, None)
                    with dve.Fori(1, GROUPS) as i:
                        body(i, i - 1)
                    tail.dve_stats(dve, GROUPS - 1)
                    tail.dve_normalise(dve, GROUPS - 1)

                @block.gpsimd
                def _(pool):
                    def body(i, prev):
                        split.pool_lo(pool, i)
                        for t in range(routed):
                            b = t // per_weight
                            wait(pool, h_ready, last_use(i, t, NT, 2) if t >= 2 else NT * (i - 1) + routed)
                            wait(pool, bw_ready, NB * i + b + 1)
                            wait(pool, s_ready, NT * i + t + 1)
                            nc.gpsimd.tensor_tensor(sw[:, t % 2, :], sl[:, t % 2, :], bw[:, b % 2, :], ALU.mult)\
                                .then_inc(w_ready, 1)
                            if prev is not None and t == 4:
                                tail.pool_rstd(pool, prev)

                    body(0, None)
                    with pool.Fori(1, GROUPS) as i:
                        body(i, i - 1)
                    tail.pool_rstd(pool, GROUPS - 1)

        attention0()
        only_l0.close()
        experts("f0", L0_TILES, L0_E * L0_HID // P, L0_HID // P, sel0, 3 * L0_E, False)
        attention1()
        experts("f1", L1_TILES, L1_TILES - 1, 1, sel1, 3 * L1_E, True)


def constants():
    p = np.arange(P)
    head = p // L0_D
    f = [np.eye(P), head[:, None] == np.arange(L0_HEADS)[None, :]]
    e, c = np.arange(L0_D)[None, :, None], p[None, None, :]
    f.append(((head[:, None, None] == c // L0_D) & (c % L0_D == e)).reshape(P, -1))
    f.append(np.broadcast_to(np.arange(GT)[None, :] % SEQ != 0, (P, GT)))
    f.append(np.broadcast_to(np.arange(8), (P, 8)))
    row = p[:, None, None]
    f.append((row == np.arange(MEMS + 1)[None, :, None] * L0_HEADS + head[None, None, :]).reshape(P, -1))
    c_f32 = np.concatenate([np.asarray(a, np.float32) for a in f], axis=1)
    tri = np.stack([np.zeros((P, P)), np.where(p[None, :] <= p[:, None], 0.0, MASKED)], axis=1).astype(np.float32)
    r0 = np.arange(3 * L0_E) % L0_E
    sel0 = np.broadcast_to(r0[:, None, None] == np.arange(L0_E)[None, :, None], (3 * L0_E, L0_E, P))
    r1 = np.arange(3 * L1_E) % L1_E
    per = P // L1_HID
    sel1 = r1[:, None, None] == np.arange(L1_TILES - 1)[None, :, None] * per + p[None, None, :] // L1_HID
    pos = np.arange(SEQ, dtype=np.float32)[:, None]
    inv = np.exp(np.float32(-math.log(10000.0)) * np.arange(0, P, 2, dtype=np.float32) / np.float32(P))
    ang = (pos * inv[None, :]).astype(np.float32)
    pe = np.zeros((SEQ, P), np.float32)
    pe[:, 0::2], pe[:, 1::2] = np.sin(ang), np.cos(ang)
    peT = np.concatenate([pe.T] * SEQS, axis=1)
    return (np.ascontiguousarray(c_f32), tri, np.ascontiguousarray(sel0.astype(np.float32)),
            np.ascontiguousarray(sel1.astype(np.float32)), np.ascontiguousarray(peT))


def kernel(**inputs):
    import concourse.bacc as bacc
    from concourse.bass_utils import run_bass_kernel_spmd

    g = {k: np.asarray(v) for k, v in inputs.items()}
    c_f32, c_tri, c_sel0, c_sel1, peT = constants()
    a = {}
    a["xT"] = g["L0_attn_hidden_states"].reshape(TOKENS, DM).T
    wl0 = np.zeros((P, 11, P), np.float32)
    wl0[:, 0], wl0[:, 1], wl0[:, 10] = g["L0_attn_w_q"].T, g["L0_attn_w_k"].T, g["L0_attn_w_o"].T
    wv = g["L0_attn_w_v"].T.reshape(P, L0_HEADS, L0_D)
    for e in range(L0_D):
        wl0[:, 2 + e] = np.repeat(wv[:, :, e], L0_D, axis=1)
    a["w_l0"] = wl0
    mem = np.zeros((P, MEMS, P), np.float32)
    norms = np.zeros((P, REL), np.float32)
    for h in range(L0_HEADS):
        r = slice(h * L0_D, (h + 1) * L0_D)
        for m in range(MEMS):
            mem[r, m, r] = g["L0_attn_memories"][m, h]
            norms[r, m * L0_HEADS + h] = g["L0_attn_memory_norms"][m, h]
    a["mem_bd"], a["norms_bd"], a["gate"] = mem, norms, g["L0_attn_gate"]

    def up(*ws):
        return np.concatenate([w.reshape(-1, DM).T for w in ws], axis=1)

    def down(*ws):
        rows = np.concatenate([w.swapaxes(1, 2).reshape(-1, DM) for w in ws], axis=0)
        return rows.reshape(-1, P, DM).swapaxes(0, 1).reshape(P, -1)

    def padded(w, axis):
        return np.concatenate([w, np.zeros_like(w)], axis=axis)

    a["w_ffn0"] = np.concatenate([up(g["L0_ffn_w1"], g["L0_ffn_sw1"]), up(g["L0_ffn_w3"], g["L0_ffn_sw3"]),
                                  down(g["L0_ffn_w2"], g["L0_ffn_sw2"])], axis=1)
    a["w_ffn1"] = np.concatenate([
        up(g["L1_ffn_expert_gate"], padded(g["L1_ffn_shared_gate_w"], 0)),
        up(g["L1_ffn_expert_up"], padded(g["L1_ffn_shared_up_w"], 0)),
        down(g["L1_ffn_expert_down"], padded(g["L1_ffn_shared_down_w"], 1)[None])], axis=1)
    a["router0"], a["bias0"], a["router1"] = g["L0_ffn_router_w"].T, g["L0_ffn_expert_bias"], g["L1_ffn_gate_w"].T
    wl1 = np.concatenate([g["L1_attn_Wq"], g["L1_attn_Wkv"]], axis=1)
    a["w_l1"] = wl1.reshape(P, 10, P)
    a["wo_l1"] = g["L1_attn_Wo"].reshape(L1_HEADS, P, P).swapaxes(0, 1)
    a["b_l1"] = np.concatenate([g["L1_attn_bq"].reshape(L1_HEADS, P).T, g["L1_attn_bkv"][:P, None]], axis=1)
    a["bv_l1"] = g["L1_attn_bkv"][P:]
    a["peT"], a["c_f32"], a["c_tri"], a["c_sel0"], a["c_sel1"] = peT, c_f32, c_tri, c_sel0, c_sel1

    nc = bacc.Bacc("TRN2", target_bir_lowering=False, num_devices=1)
    arrays, args = {}, []
    for name, x in a.items():
        x = np.ascontiguousarray(x)
        arrays[f"in_{name}"] = x
        args.append(nc.dram_tensor(f"in_{name}", x.shape, mybir.dt.from_np(x.dtype), kind="ExternalInput").ap())
    args.append(nc.dram_tensor("out_x", (TOKENS, DM), F32, kind="ExternalOutput").ap())
    build(nc, *args)
    r = run_bass_kernel_spmd(nc, [arrays], core_ids=[0])
    return r.results[0]["out_x"].reshape(BATCH, SEQ, DM)
```

```python
import math
from contextlib import ExitStack

import numpy as np

import concourse.bass as bass
from concourse import mybir

F32 = mybir.dt.float32
F32R = mybir.dt.float32r
BF16 = mybir.dt.bfloat16
U32 = mybir.dt.uint32
ALU = mybir.AluOpType
ACT = mybir.ActivationFunctionType
AX = mybir.AxisListType.X

P = 128
BATCH, SEQ, DM = 32, 256, 128
TOKENS = BATCH * SEQ
GT = 512
GROUPS = TOKENS // GT
TILES = GT // P
SEQS = GT // SEQ
L0_HEADS, L0_D, MEMS = 16, 8, 4
L1_HEADS = 8
L0_E, L0_HID, L0_SHARED = 8, 256, 2
L1_E, L1_HID = 32, 64
L1_GROUPS, L1_PER = 8, 4
EPS_DEN, EPS_LN, EPS_TOPK = 1e-6, 1e-5, 1e-12
SCALE = 1.0 / math.sqrt(P)
MASKED = -3.0e38
L0_TILES = (L0_E + L0_SHARED) * L0_HID // P
L1_TILES = L1_E * L1_HID // P + 1
REL = MEMS * L0_HEADS
DEN = REL + L0_HEADS


def counted(value):
    return not isinstance(value, int) or value > 0




def snapped(eng, value):
    return value if isinstance(value, int) else eng.to_reg(value)


def last_use(i, n, per, slots):
    if n >= slots:
        return i * per + n - slots + 1
    last = max(m for m in range(per) if m % slots == n % slots)
    return (i - 1) * per + last + 1


def build(nc, xT, w_l0, mem_bd, norms_bd, gate, w_ffn0, w_ffn1, router0, bias0, router1,
          w_l1, wo_l1, b_l1, bv_l1, peT, c_f32, c_tri, c_sel0, c_sel1, out):
    ctx = ExitStack()
    with ctx:
        def sb(name, shape, dt=F32):
            return ctx.enter_context(nc.sbuf_tensor(name, shape, dt))

        def sem(name):
            return ctx.enter_context(nc.semaphore(name))

        bank = [ctx.enter_context(nc.psum_tensor(f"bank{b}", [P, GT], F32)) for b in range(8)]

        resid = sb("resid", [P, TOKENS])
        x_hi, x_lo = sb("x_hi", [P, GT], F32R), sb("x_lo", [P, GT], F32R)
        cwT = sb("cwT", [96, TOKENS], BF16)
        NW0, NW1 = 3 * L0_TILES * P, 3 * L1_TILES * P
        ffn_hi, ffn_lo = sb("ffn_hi", [P, NW0], F32R), sb("ffn_lo", [P, NW0], F32R)
        CH0, CH1 = NW0 // GROUPS, NW1 // GROUPS
        stage = sb("stage", [P, max(CH0, CH1)])
        ident = sb("ident", [P, P])
        ident_bf = sb("ident_bf", [P, P], BF16)
        half = sb("half", [P, TILES])
        y_sb, z_sb = sb("y_sb", [P, GT]), sb("z_sb", [P, TILES, P])
        stats, mv = sb("stats", [P, TILES, 6]), sb("mv", [P, TILES, 2])
        var_eps, rstd = sb("var_eps", [P, TILES]), sb("rstd", [P, TILES])
        router0_sb, router1_sb = sb("router0_sb", [P, L0_E]), sb("router1_sb", [P, L1_E])
        bias0_sb = sb("bias0_sb", [P, L0_E])
        iota8 = sb("iota8", [P, 8])
        sel0 = sb("sel0", [3 * L0_E, L0_E, P], BF16)
        sel1 = sb("sel1", [3 * L1_E, L1_TILES - 1, P], BF16)
        def staged(engine, period):
            period(0, True, False, False)
            period(1, True, True, False)
            period(2, True, True, True)
            with engine.Fori(3, GROUPS - 1) as i:
                period(i, True, True, True)
            period(GROUPS - 1, True, True, True)
            period(GROUPS, False, True, True)
            period(GROUPS + 1, False, False, True)

        lg = sb("lg", [P, TILES, L1_E])
        sg = sb("sg", [P, TILES, L1_E])
        cw = sb("cw", [P, TILES, L1_E])
        rest_w = sb("rest_w", [P, TILES, L1_E])
        cw3 = sb("cw3", [P, TILES, 3 * L1_E], BF16)
        top = sb("top", [P, TILES, 8])
        idx = sb("idx", [P, TILES, 8], U32)
        idxf = sb("idxf", [P, TILES, 8])
        gsum, gmask = sb("gsum", [P, TILES, 8]), sb("gmask", [P, TILES, 8])
        xf = sb("xf", [P, GT])
        eq4 = sb("eq4", [P, TILES, 8, 4])
        pair = sb("pair", [P, 4, TILES])

        only_l0 = ExitStack()

        def sb0(name, shape, dt=F32):
            return only_l0.enter_context(nc.sbuf_tensor(name, shape, dt))

        wl0_hi, wl0_lo = sb0("wl0_hi", [P, 10, P], F32R), sb0("wl0_lo", [P, 10, P], F32R)
        wo0 = sb0("wo0", [P, P])
        mem_sb, norms_sb = sb0("mem_sb", [P, MEMS, P]), sb0("norms_sb", [P, REL])
        headsum = sb0("headsum", [P, L0_HEADS])
        spread = sb0("spread", [DEN, MEMS + 1, P])
        blocksum = sb0("blocksum", [P, L0_D, P])
        reset = sb0("reset", [P, GT])
        gate_row, gate_col = sb0("gate_row", [SEQS, L0_HEADS]), sb0("gate_col", [DEN, 1])
        wcol = sb0("wcol", [DEN, SEQS])
        s_const, s_raw, s_ones, s_cast = sem("consts_loaded"), sem("raw_loaded"), sem("gates_exp"), sem("setup_done")
        with nc.sbuf_tensor("raw", [P, 10, P], F32) as raw, nc.sbuf_tensor("gtmp", [P, 16], F32) as gtmp, \
                nc.sbuf_tensor("sel0_raw", [3 * L0_E, L0_E, P], F32) as sel0_raw, \
                nc.sbuf_tensor("sel1_raw", [3 * L1_E, L1_TILES - 1, P], F32) as sel1_raw, \
                nc.Block() as block:
            @block.sync
            def _(sp):
                o = 0
                for dst, w in ((ident[:], P), (headsum[:], L0_HEADS), (blocksum[:], L0_D * P), (reset[:], GT),
                               (iota8[:], 8)):
                    src = c_f32[:, o:o + w]
                    if len(dst.shape) == 3:
                        src = src.rearrange("p (a b) -> p a b", a=dst.shape[1])
                    sp.dma_start(dst, src).then_inc(s_const, 16)
                    o += w
                sp.dma_start(spread[:], c_f32[0:DEN, o:o + (MEMS + 1) * P].rearrange("p (a b) -> p a b", a=MEMS + 1)).then_inc(s_const, 16)
                sp.dma_start(sel0_raw[:], c_sel0).then_inc(s_const, 16)
                sp.dma_start(sel1_raw[:], c_sel1).then_inc(s_const, 16)
                sp.dma_start(mem_sb[:], mem_bd).then_inc(s_const, 16)
                sp.dma_start(norms_sb[:], norms_bd).then_inc(s_const, 16)
                sp.dma_start(router0_sb[:], router0).then_inc(s_const, 16)
                sp.dma_start(router1_sb[:], router1).then_inc(s_const, 16)
                sp.dma_start(bias0_sb[:], bias0.partition_broadcast(P)).then_inc(s_const, 16)
                sp.wait_ge(s_const, 16 * 13)

            @block.scalar
            def _(act):
                act.dma_start(raw[:], w_l0[:, 0:10, :]).then_inc(s_raw, 16)
                act.dma_start(wo0[:], w_l0[:, 10, :]).then_inc(s_raw, 16)
                act.dma_start(gate_row[:], gate.partition_broadcast(SEQS)).then_inc(s_raw, 16)
                act.dma_start(gate_col[REL:DEN, :], gate.rearrange("(h a) -> h a", a=1)).then_inc(s_raw, 16)
                act.wait_ge(s_raw, 64)
                nc.scalar.activation(gtmp[0:SEQS, :], gate_row[:], ACT.Exp, scale=-1.0).then_inc(s_ones, 1)
                nc.scalar.activation(gtmp[REL:DEN, 0:1], gate_col[REL:DEN, :], ACT.Exp).then_inc(s_ones, 1)

            @block.vector
            def _(dve):
                nc.vector.memset(half[:], -0.5)
                dve.wait_ge(s_raw, 64)
                nc.vector.tensor_copy(wl0_hi[:], raw[:])
                dve.drain()
                nc.vector.tensor_tensor(wl0_lo[:], raw[:], wl0_hi[:].bitcast(F32), ALU.subtract)
                dve.wait_ge(s_ones, 2)
                nc.vector.tensor_scalar(gtmp[0:SEQS, :], gtmp[0:SEQS, :], 1.0, None, ALU.add)
                nc.vector.tensor_scalar(gtmp[REL:DEN, 0:1], gtmp[REL:DEN, 0:1], 1.0, None, ALU.add)
                dve.drain()
                nc.vector.reciprocal(gate_row[:], gtmp[0:SEQS, :])
                nc.vector.reciprocal(gate_col[REL:DEN, :], gtmp[REL:DEN, 0:1])
                dve.drain()
                for s in range(SEQS):
                    nc.vector.tensor_copy(wcol[REL:DEN, s:s + 1], gate_col[REL:DEN, :])
                dve.wait_ge(s_const, 16 * 13)
                nc.vector.tensor_copy(sel0[:], sel0_raw[:])
                nc.vector.tensor_copy(sel1[:], sel1_raw[:])
                nc.vector.tensor_copy(ident_bf[:], ident[:]).then_inc(s_cast, 1)
                dve.wait_ge(s_cast, 1)

        def group(i, n=GT):
            return bass.ds(i * n, n)

        class Tail:

            def __init__(self, part, last=False, route=None):
                self.last, self.route = last, route
                self.y_ready = sem(f"{part}_y_ready")
                self.tok_ready = sem(f"{part}_tok_ready")
                self.stats_ready = sem(f"{part}_stats_ready")
                self.var_ready = sem(f"{part}_var_ready")
                self.rstd_ready = sem(f"{part}_rstd_ready")
                self.z_ready = sem(f"{part}_z_ready")
                self.feat_ready = sem(f"{part}_feat_ready")
                self.x_ready = sem(f"{part}_x_ready")
                self.stored = sem(f"{part}_stored")

            def pe_tokens(self, pe, i):
                pe.wait_ge(self.y_ready, i + 1)
                if self.last:
                    pe.wait_ge(self.z_ready, i)
                else:
                    if counted(i):
                        pe.wait_ge(self.x_ready, i)
                for t in range(TILES):
                    last = nc.tensor.transpose(bank[0][:, t * P:(t + 1) * P], y_sb[:, t * P:(t + 1) * P], ident[:])
                last.then_inc(self.tok_ready, 1)

            def pe_features(self, pe, i):
                if self.last:
                    return
                pe.wait_ge(self.z_ready, i + 1)
                for t in range(TILES):
                    last = nc.tensor.transpose(bank[0][:, t * P:(t + 1) * P], z_sb[:, t, :], ident[:])
                last.then_inc(self.feat_ready, 1)

            def dve_stats(self, dve, i):
                dve.wait_ge(s_cast, 1)
                if counted(i):
                    dve.wait_ge(self.rstd_ready, i)
                dve.wait_ge(self.tok_ready, i + 1)
                for t in range(TILES):
                    nc.vector.bn_stats(stats[:, t, :], bank[0][:, t * P:(t + 1) * P])
                dve.drain()
                for t in range(TILES):
                    last = nc.vector.bn_aggr(mv[:, t, :], stats[:, t, :])
                last.then_inc(self.stats_ready, 1)

            def pool_rstd(self, pool, i):
                normalised, ready = snapped(pool, i), snapped(pool, i + 1)
                pool.wait_ge(s_cast, 1)
                if counted(normalised):
                    pool.wait_ge(self.z_ready, normalised)
                pool.wait_ge(self.stats_ready, ready)
                nc.gpsimd.tensor_scalar(var_eps[:], mv[:, :, 1], EPS_LN, None, ALU.add).then_inc(self.var_ready, 1)
                pool.wait_ge(self.var_ready, i + 1)
                nc.gpsimd.tensor_tensor(rstd[:], var_eps[:], half[:], ALU.pow).then_inc(self.rstd_ready, 1)

            def dve_normalise(self, dve, i):
                if self.last:
                    dve.wait_ge(self.stored, 16 * i)
                else:
                    if counted(i):
                        dve.wait_ge(self.feat_ready, i)
                dve.wait_ge(self.rstd_ready, i + 1)
                for t in range(TILES):
                    last = nc.vector.tensor_scalar(z_sb[:, t, :], bank[0][:, t * P:(t + 1) * P], mv[:, t, 0:1],
                                                   rstd[:, t:t + 1], ALU.subtract, ALU.mult)
                last.then_inc(self.z_ready, 1)

            def act_resid(self, act, i):
                if self.route:
                    if counted(i):
                        act.wait_ge(self.route.logits_ready, i)
                act.wait_ge(self.feat_ready, i + 1)
                if self.route:
                    nc.scalar.activation(xf[:], bank[0][:], ACT.Copy)
                act.wait_ge(s_cast, 1)
                nc.scalar.activation(resid[:, group(i)], bank[0][:], ACT.Copy).then_inc(self.x_ready, 1)

            def sp_store(self, sp, i):
                sp.wait_ge(self.z_ready, i + 1)
                sp.dma_start(out[group(i), :].rearrange("(t p) f -> p t f", p=P), z_sb[:]).then_inc(self.stored, 16)

        class Split:

            def __init__(self, part):
                self.hi_ready, self.lo_ready = sem(f"{part}_x_hi_ready"), sem(f"{part}_x_lo_ready")

            def act_hi(self, act, i):
                nc.scalar.activation(x_hi[:], resid[:, group(i)], ACT.Copy).then_inc(self.hi_ready, 1)

            def pool_lo(self, pool, i):
                pool.wait_ge(self.hi_ready, i + 1)
                pool.wait_ge(s_cast, 1)
                nc.gpsimd.tensor_tensor(x_lo[:], resid[:, group(i)], x_hi[:].bitcast(F32), ALU.subtract)\
                    .then_inc(self.lo_ready, 1)

        class Stream:

            def __init__(self, part, src, chunk):
                self.src, self.chunk = src, chunk
                self.loaded, self.hi_done, self.split = (sem(f"{part}_chunk_{n}") for n in ("loaded", "hi", "split"))

            def sp_load(self, sp, i):
                if counted(i):
                    sp.wait_ge(self.split, i)
                sp.dma_start(stage[:, 0:self.chunk], self.src[:, group(i, self.chunk)]).then_inc(self.loaded, 16)

            def pool_split(self, pool, i):
                c = self.chunk
                pool.wait_ge(s_cast, 1)
                pool.wait_ge(self.loaded, 16 * i + 16)
                nc.gpsimd.tensor_copy(ffn_hi[:, group(i, c)], stage[:, 0:c]).then_inc(self.hi_done, 1)
                pool.wait_ge(self.hi_done, i + 1)
                pool.wait_ge(s_cast, 1)
                nc.gpsimd.tensor_tensor(ffn_lo[:, group(i, c)], stage[:, 0:c], ffn_hi[:, group(i, c)].bitcast(F32),
                                        ALU.subtract).then_inc(self.split, 1)

        def three_pass(out_, w_hi, w_lo, m_hi, m_lo, start=True, stop=True):
            nc.tensor.matmul(out_, w_hi, m_hi, start=start, stop=False)
            nc.tensor.matmul(out_, w_hi, m_lo, start=False, stop=False)
            return nc.tensor.matmul(out_, w_lo, m_hi, start=False, stop=stop)

        def run(engine, first, rest):
            first(0)
            with engine.Fori(1, GROUPS) as i:
                rest(i)

        class Route:
            def __init__(self, part, e, router):
                self.e, self.router = e, router
                self.logits_ready = sem(f"{part}_logits_ready")
                self.pre_exp, self.exp_done = sem(f"{part}_route_pre_exp"), sem(f"{part}_route_exp")
                self.cw_ready = sem(f"{part}_cw_ready")
                self.part_done = sem(f"{part}_cw_part")
                self.cwT_psum = sem(f"{part}_cwT_psum")
                self.cwT_ready = sem(f"{part}_cwT_ready")
                self.logits = bank[1][:, 0:TILES * e].rearrange("p (t e) -> p t e", e=e)
                self.cwT_p = bank[1][:, GT // 2:GT].bitcast(BF16)

            def pe_logits(self, pe, i, tail):
                if counted(i):
                    pe.wait_ge(self.cwT_ready, i)
                pe.wait_ge(tail.x_ready, i + 1)
                pe.wait_ge(s_cast, 1)
                for t in range(TILES):
                    last = nc.tensor.matmul(self.logits[:, t, :], xf[:, t * P:(t + 1) * P], self.router[:],
                                            start=True, stop=True)
                last.then_inc(self.logits_ready, 1)

            def pool_parts(self, pool, i):
                e = self.e
                pool.wait_ge(s_cast, 1)
                if counted(i):
                    pool.wait_ge(self.cwT_psum, i)
                pool.wait_ge(self.cw_ready, i + 1)
                src = cw[:, :, 0:e]
                for k in range(3):
                    part = cw3[:, :, k * e:(k + 1) * e]
                    nc.gpsimd.tensor_copy(part, src).then_inc(self.part_done, 1)
                    pool.wait_ge(self.part_done, 5 * i + 2 * k + 1)
                    if k < 2:
                        nc.gpsimd.tensor_tensor(rest_w[:, :, 0:e], src, part, ALU.subtract).then_inc(self.part_done, 1)
                        done = snapped(pool, 5 * i + 2 * k + 2)
                        pool.wait_ge(s_cast, 1)
                        pool.wait_ge(self.part_done, done)
                        src = rest_w[:, :, 0:e]

            def pe_transpose(self, pe, i):
                e3 = 3 * self.e
                pe.wait_ge(self.part_done, 5 * i + 5)
                for t in range(TILES):
                    last = nc.tensor.transpose(self.cwT_p[0:e3, t * P:(t + 1) * P], cw3[:, t, 0:e3], ident_bf[:])
                last.then_inc(self.cwT_psum, 1)

            def act_cwT(self, act, i):
                e3 = 3 * self.e
                act.wait_ge(self.cwT_psum, i + 1)
                act.wait_ge(s_cast, 1)
                nc.scalar.activation(cwT[0:e3, group(i)], self.cwT_p[0:e3, :], ACT.Copy).then_inc(self.cwT_ready, 1)

        class RouteTop2(Route):

            def dve_1(self, dve, i):
                if counted(5 * i):
                    dve.wait_ge(self.part_done, 5 * i)
                dve.wait_ge(self.logits_ready, i + 1)
                nc.vector.tensor_tensor(lg[:, :, 0:8], self.logits, bias0_sb[:].unsqueeze(1).broadcast_to([P, TILES, 8]),
                                        ALU.add)
                dve.drain()
                for t in range(TILES):
                    nc.vector.max(top[:, t, :], lg[:, t, 0:8])
                dve.drain()
                for t in range(TILES):
                    nc.vector.max_index(idx[:, t, :], top[:, t, :], lg[:, t, 0:8])
                nc.vector.tensor_tensor(pair[:, 0, :], top[:, :, 1], top[:, :, 0], ALU.subtract).then_inc(self.pre_exp, 1)

            def act_exp(self, act, i):
                act.wait_ge(self.pre_exp, i + 1)
                nc.scalar.activation(pair[:, 1, :], pair[:, 0, :], ACT.Exp).then_inc(self.exp_done, 1)

            def dve_2(self, dve, i):
                dve.drain()
                nc.vector.tensor_copy(idxf[:], idx[:])
                dve.drain()
                dve.wait_ge(self.exp_done, i + 1)
                nc.vector.tensor_scalar(pair[:, 2, :], pair[:, 1, :], 1.0, None, ALU.add)
                dve.drain()
                nc.vector.reciprocal(pair[:, 2, :], pair[:, 2, :])
                dve.drain()
                nc.vector.tensor_tensor(pair[:, 3, :], pair[:, 1, :], pair[:, 2, :], ALU.mult)
                io = iota8[:].unsqueeze(1).broadcast_to([P, TILES, 8])
                for k, m in ((0, gmask), (1, gsum)):
                    nc.vector.tensor_tensor(m[:], io, idxf[:, :, k:k + 1].broadcast_to([P, TILES, 8]), ALU.is_equal)
                dve.drain()
                for k, m in ((2, gmask), (3, gsum)):
                    nc.vector.tensor_tensor(m[:], m[:], pair[:, k, :].unsqueeze(2).broadcast_to([P, TILES, 8]), ALU.mult)
                dve.drain()
                nc.vector.tensor_tensor(cw[:, :, 0:8], gmask[:], gsum[:], ALU.add).then_inc(self.cw_ready, 1)

        class RouteGrouped(Route):

            def act_exp(self, act, i):
                act.wait_ge(self.logits_ready, i + 1)
                nc.scalar.activation(lg[:], self.logits, ACT.Exp, scale=-1.0).then_inc(self.exp_done, 1)

            def dve_1(self, dve, i):
                dve.wait_ge(self.exp_done, i + 1)
                nc.vector.tensor_scalar(lg[:], lg[:], 1.0, None, ALU.add)
                dve.drain()
                nc.vector.reciprocal(sg[:], lg[:]).then_inc(self.pre_exp, 1)
                dve.drain()
                nc.vector.tensor_reduce(gsum[:], sg[:].rearrange("p t (g k) -> p t g k", k=L1_PER), AX, ALU.add)
                dve.drain()
                for t in range(TILES):
                    nc.vector.max(top[:, t, :], gsum[:, t, :])
                dve.drain()
                for t in range(TILES):
                    nc.vector.max_index(idx[:, t, :], top[:, t, :], gsum[:, t, :])
                dve.drain()
                nc.vector.tensor_copy(idxf[:], idx[:])
                dve.drain()

            def dve_2(self, dve, i):
                for t in range(TILES):
                    nc.vector.tensor_tensor(eq4[:, t, :, :], iota8[:].unsqueeze(2).broadcast_to([P, 8, 4]),
                                            idxf[:, t, 0:4].unsqueeze(1).broadcast_to([P, 8, 4]), ALU.is_equal)
                dve.drain()
                nc.vector.tensor_reduce(gmask[:], eq4[:], AX, ALU.add)
                dve.drain()
                nc.vector.tensor_tensor(sg[:].rearrange("p t (g k) -> p (t g) k", k=L1_PER),
                                        sg[:].rearrange("p t (g k) -> p (t g) k", k=L1_PER),
                                        gmask[:].rearrange("p t g -> p (t g)").unsqueeze(2)
                                        .broadcast_to([P, TILES * 8, L1_PER]), ALU.mult)
                dve.drain()
                for t in range(TILES):
                    nc.vector.max(top[:, t, :], sg[:, t, :])
                dve.drain()
                for t in range(TILES):
                    nc.vector.match_replace(lg[:, t, :], top[:, t, :], sg[:, t, :], 0.0)
                nc.vector.tensor_reduce(pair[:, 0, :], top[:], AX, ALU.add)
                dve.drain()
                nc.vector.tensor_scalar(pair[:, 0, :], pair[:, 0, :], EPS_TOPK, None, ALU.max)
                nc.vector.tensor_tensor(sg[:], sg[:], lg[:], ALU.subtract)
                dve.drain()
                nc.vector.reciprocal(pair[:, 1, :], pair[:, 0, :])
                dve.drain()
                if counted(5 * i):
                    dve.wait_ge(self.part_done, 5 * i)
                nc.vector.tensor_tensor(cw[:], sg[:], pair[:, 1, :].unsqueeze(2).broadcast_to([P, TILES, L1_E]),
                                        ALU.mult).then_inc(self.cw_ready, 1)

        def attention0():
            s = lambda n: sem(f"a0_{n}")
            route = RouteTop2("a0", L0_E, router0_sb)
            tail, split, stream = Tail("a0", route=route), Split("a0"), Stream("a0", w_ffn0, CH0)
            x_loaded = s("x_loaded")
            k_ready, q_ready, v_ready = s("k_ready"), s("q_ready"), s("v_ready")
            ek_ready, eq_ready = s("exp_k_ready"), s("exp_q_ready")
            sk_ready, sq_ready = s("sk_ready"), s("sq_ready")
            kv_ready, cum_ready = s("kv_ready"), s("cum_ready")
            qk_ready, qkv_ready = s("qk_ready"), s("qkv_ready")
            rel_ready, den_ready = s("rel_ready"), s("den_ready")
            rs_ready, rsT_ready, dlt_ready, ew_ready = s("relsum"), s("relsum_T"), s("softmax_in"), s("softmax_exp")
            w_ready, wT_ready, wcol_ready = s("w_ready"), s("w_T"), s("wcol_ready")
            rec_ready, r_ready = s("reciprocals"), s("factors")
            bc_ready, qm_ready = s("spread_ready"), s("qm_ready")
            acc_ready, o_ready, wo_ready = s("acc_ready"), s("o_ready"), s("wo_ready")
            ORDER = [MEMS, 0, 1, 2, 3]

            with ExitStack() as own:
                def tb(name, shape, dt=F32):
                    return own.enter_context(nc.sbuf_tensor(f"a0_{name}", shape, dt))

                ek, eq, sq, sq4 = tb("ek", [P, GT]), tb("eq", [P, GT]), tb("sq", [P, GT]), tb("sq4", [P, GT])
                kv = tb("kv", [P, 3, GT])
                cum = tb("cum", [P, L0_D + 1, GT])
                qkv = tb("qkv", [P, 3, GT])
                relsum, rowT = tb("relsum", [REL, SEQS]), tb("rowT", [SEQS, REL])
                erow, mx, wrow = tb("erow", [SEQS, REL]), tb("mx", [SEQS, L0_HEADS]), tb("wrow", [SEQS, REL])
                clip, rec, fac = tb("clip", [DEN, GT]), tb("rec", [DEN, GT]), tb("fac", [DEN, GT])
                qm = tb("qm", [P, 2, GT])
                o_sb = tb("o_sb", [P, GT])
                ring, spreadP, denP, acc = bank[2:4], bank[5:7], bank[4], bank[7]
                rsT, wT = bank[1][0:SEQS, 128:128 + REL], bank[1][0:REL, 192:192 + SEQS]
                block = own.enter_context(nc.Block())

                @block.sync
                def _(sp):
                    sp.dma_start(resid[:, 0:GT], xT[:, 0:GT]).then_inc(x_loaded, 16)
                    with sp.Fori(0, GROUPS - 1) as i:
                        sp.wait_ge(x_loaded, 16 * i + 16)
                        sp.dma_start(resid[:, bass.ds(i * GT + GT, GT)], xT[:, bass.ds(i * GT + GT, GT)])\
                            .then_inc(x_loaded, 16)
                    stream.sp_load(sp, 0)
                    with sp.Fori(1, GROUPS) as i:
                        stream.sp_load(sp, i)

                @block.tensor
                def _(pe):
                    def values(i, e):
                        if e == 0:
                            pe.wait_ge(sk_ready, i + 1)
                        elif e == 1:
                            pe.wait_ge(sq_ready, i + 1)
                        else:
                            pe.wait_ge(kv_ready, 8 * i + e - 1)
                        three_pass(ring[e % 2][:], wl0_hi[:, 2 + e, :], wl0_lo[:, 2 + e, :], x_hi[:], x_lo[:])\
                            .then_inc(v_ready, 1)

                    def spread_factor(g, o):
                        if o == 0:
                            pe.wait_ge(r_ready, g + 1)
                            if counted(5 * g):
                                pe.wait_ge(qm_ready, 5 * g)
                        elif o == 1:
                            if counted(g):
                                pe.wait_ge(tail.y_ready, g)
                        else:
                            pe.wait_ge(qm_ready, 5 * g + o - 1)
                        nc.tensor.matmul(spreadP[o % 2][:], spread[:, ORDER[o], :], fac[:], start=True, stop=True)\
                            .then_inc(bc_ready, 1)

                    def memory(g, m):
                        if m == 0:
                            if counted(g):
                                pe.wait_ge(o_ready, g)
                        pe.wait_ge(qm_ready, 5 * g + m + 2)
                        nc.tensor.matmul(acc[:], mem_sb[:, m, :], qm[:, m % 2, :], start=(m == 0), stop=False)\
                            .then_inc(acc_ready, 1)

                    def local(g, e):
                        pe.wait_ge(qkv_ready, 8 * g + e + 1)
                        nc.tensor.matmul(acc[:], blocksum[:, e, :], qkv[:, e % 2, :], start=False, stop=(e == L0_D - 1))\
                            .then_inc(acc_ready, 1)

                    def period(i, A, B, C):
                        g, c = i - 1, i - 2
                        if A:
                            pe.wait_ge(split.lo_ready, i + 1)
                            if counted(8 * i - 1):
                                pe.wait_ge(kv_ready, 8 * i - 1)
                            three_pass(ring[0][:], wl0_hi[:, 1, :], wl0_lo[:, 1, :], x_hi[:], x_lo[:]).then_inc(k_ready, 1)
                            if counted(8 * i):
                                pe.wait_ge(kv_ready, 8 * i)
                            three_pass(ring[1][:], wl0_hi[:, 0, :], wl0_lo[:, 0, :], x_hi[:], x_lo[:]).then_inc(q_ready, 1)
                        if C:
                            tail.pe_tokens(pe, c)
                        if B:
                            spread_factor(g, 0)
                            spread_factor(g, 1)
                        if A:
                            values(i, 0)
                        if B:
                            spread_factor(g, 2)
                            memory(g, 0)
                            spread_factor(g, 3)
                            memory(g, 1)
                            spread_factor(g, 4)
                            memory(g, 2)
                            memory(g, 3)
                        if C:
                            tail.pe_features(pe, c)
                        for e in range(L0_D):
                            if A and e >= 1:
                                values(i, e)
                            if A and e == 1:
                                if counted(i):
                                    pe.wait_ge(rec_ready, i)
                                nc.tensor.matmul(denP[0:REL, :], norms_sb[:], sq[:], start=True, stop=True)\
                                    .then_inc(rel_ready, 1)
                            if B:
                                local(g, e)
                            if A and e == 2:
                                pe.wait_ge(s_cast, 1)
                                if counted(i - 2):
                                    pe.wait_ge(route.cwT_ready, i - 2)
                                pe.wait_ge(rs_ready, i + 1)
                                nc.tensor.transpose(rsT, relsum[:], ident[0:REL, 0:REL]).then_inc(rsT_ready, 1)
                            if A and e == 3:
                                pe.wait_ge(dlt_ready, i + 1)
                            if C and e == 3:
                                route.pe_logits(pe, c, tail)
                            if A and e == 4:
                                pe.wait_ge(qk_ready, i + 1)
                                nc.tensor.matmul(denP[REL:DEN, :], headsum[:], qkv[:, 2, :], start=True, stop=True)\
                                    .then_inc(den_ready, 1)
                            if A and e == 6:
                                pe.wait_ge(s_cast, 1)
                                pe.wait_ge(w_ready, i + 1)
                                nc.tensor.transpose(wT, wrow[:], ident[0:SEQS, 0:SEQS]).then_inc(wT_ready, 1)
                        if A:
                            pe.wait_ge(wcol_ready, i + 1)
                        if C:
                            route.pe_transpose(pe, c)
                        if B:
                            pe.wait_ge(o_ready, g + 1)
                            nc.tensor.matmul(spreadP[1][:], wo0[:], o_sb[:], start=True, stop=True).then_inc(wo_ready, 1)

                    staged(pe, period)

                @block.scalar
                def _(act):
                    def prepare(i):
                        act.wait_ge(x_loaded, 16 * i + 16)
                        if counted(8 * i):
                            act.wait_ge(v_ready, 8 * i)
                        act.wait_ge(s_cast, 1)
                        split.act_hi(act, i)

                    def period(i, A, B, C):
                        g, c = i - 1, i - 2
                        if A:
                            act.wait_ge(k_ready, i + 1)
                            nc.scalar.activation(ek[:], ring[0][:], ACT.Exp).then_inc(ek_ready, 1)
                            act.wait_ge(q_ready, i + 1)
                            nc.scalar.activation(eq[:], ring[1][:], ACT.Exp).then_inc(eq_ready, 1)
                        if C:
                            tail.act_resid(act, c)
                        if A:
                            act.wait_ge(dlt_ready, i + 1)
                            nc.scalar.activation(erow[:], rowT[:], ACT.Exp, scale=1.0 / SEQ).then_inc(ew_ready, 1)
                        if C:
                            route.act_exp(act, c)
                        if A:
                            if counted(5 * i):
                                act.wait_ge(bc_ready, 5 * i)
                            act.wait_ge(wcol_ready, i + 1)
                            act.wait_ge(rec_ready, i + 1)
                            for q in range(SEQS):
                                cols = slice(q * SEQ, (q + 1) * SEQ)
                                last = nc.scalar.activation(fac[:, cols], rec[:, cols], ACT.Copy, scale=wcol[:, q:q + 1])
                            last.then_inc(r_ready, 1)
                        if B:
                            if counted(g):
                                act.wait_ge(wo_ready, g)
                            act.wait_ge(acc_ready, 12 * g + 12)
                            nc.scalar.activation(o_sb[:], acc[:], ACT.Copy).then_inc(o_ready, 1)
                        if A and not (isinstance(i, int) and i == GROUPS - 1):
                            prepare(i + 1)
                        if C:
                            route.act_cwT(act, c)

                    prepare(0)
                    staged(act, period)

                @block.vector
                def _(dve):
                    def elu(i, e_ready, e_sb, src, dst, done):
                        dve.wait_ge(e_ready, i + 1)
                        nc.vector.tensor_scalar(e_sb[:], e_sb[:], 1.0, None, ALU.min)
                        dve.drain()
                        if done is sk_ready:
                            if counted(9 * i):
                                dve.wait_ge(cum_ready, 9 * i)
                        else:
                            if counted(i):
                                dve.wait_ge(qk_ready, i)
                        nc.vector.scalar_tensor_tensor(out=dst, in0=src[:], scalar=0.0, in1=e_sb[:], op0=ALU.max,
                                                       op1=ALU.add).then_inc(done, 1)

                    def product(i, e):
                        if counted(v := 9 * i + e if e >= 2 else 9 * (i - 1) + 8 + e):
                            dve.wait_ge(cum_ready, v)
                        dve.wait_ge(v_ready, 8 * i + e + 1)
                        nc.vector.tensor_tensor(kv[:, e % 2, :], ring[e % 2][:], kv[:, 2, :], ALU.mult).then_inc(kv_ready, 1)

                    def running(i, e):
                        if counted(8 * (i - 1) + e + 1):
                            dve.wait_ge(qkv_ready, 8 * (i - 1) + e + 1)
                        dve.wait_ge(kv_ready, 8 * i + e + 1)
                        nc.vector.tensor_tensor_scan(cum[:, e, :], reset[:], kv[:, e % 2, :], 0.0, ALU.mult, ALU.add)\
                            .then_inc(cum_ready, 1)

                    def scaled_q(g, o):
                        if o == 0:
                            if counted(8 * g):
                                dve.wait_ge(qkv_ready, 8 * g)
                        else:
                            if counted(v := 12 * g + o - 2 if o >= 3 else 12 * (g - 1) + 2 + o):
                                dve.wait_ge(acc_ready, v)
                        dve.wait_ge(bc_ready, 5 * g + o + 1)
                        nc.vector.tensor_tensor(sq4[:] if o == 0 else qm[:, (o - 1) % 2, :], spreadP[o % 2][:], sq[:],
                                                ALU.mult).then_inc(qm_ready, 1)

                    def softmax_in(i):
                        dve.wait_ge(rsT_ready, i + 1)
                        nc.vector.tensor_reduce(mx[:], rsT.rearrange("p (m h) -> p h m", m=MEMS), AX, ALU.max)
                        dve.drain()
                        nc.vector.tensor_tensor(rowT[:].rearrange("p (m h) -> p m h", m=MEMS),
                                                rsT.rearrange("p (m h) -> p m h", m=MEMS),
                                                mx[:].unsqueeze(1).broadcast_to([SEQS, MEMS, L0_HEADS]),
                                                ALU.subtract).then_inc(dlt_ready, 1)

                    def softmax_out(i):
                        dve.wait_ge(ew_ready, i + 1)
                        nc.vector.tensor_reduce(mx[:], erow[:].rearrange("p (m h) -> p h m", m=MEMS), AX, ALU.add)
                        dve.drain()
                        nc.vector.reciprocal(mx[:], mx[:])
                        dve.drain()
                        nc.vector.tensor_tensor(mx[:], mx[:], gate_row[:], ALU.mult)
                        dve.drain()
                        nc.vector.tensor_tensor(wrow[:].rearrange("p (m h) -> p m h", m=MEMS),
                                                erow[:].rearrange("p (m h) -> p m h", m=MEMS),
                                                mx[:].unsqueeze(1).broadcast_to([SEQS, MEMS, L0_HEADS]),
                                                ALU.mult).then_inc(w_ready, 1)

                    def period(i, A, B, C):
                        g, c = i - 1, i - 2
                        if A:
                            elu(i, ek_ready, ek, ring[0], kv[:, 2, :], sk_ready)
                        if B:
                            scaled_q(g, 0)
                            scaled_q(g, 1)
                        if A:
                            if counted(i):
                                dve.wait_ge(qk_ready, i)
                            dve.wait_ge(sk_ready, i + 1)
                            nc.vector.tensor_tensor_scan(cum[:, L0_D, :], reset[:], kv[:, 2, :], 0.0, ALU.mult, ALU.add)\
                                .then_inc(cum_ready, 1)
                        if B:
                            scaled_q(g, 2)
                        if C:
                            tail.dve_stats(dve, c)
                        if B:
                            scaled_q(g, 3)
                        if A:
                            product(i, 0)
                        if B:
                            scaled_q(g, 4)
                        if A:
                            if counted(5 * i):
                                dve.wait_ge(qm_ready, 5 * i)
                            elu(i, eq_ready, eq, ring[1], sq[:], sq_ready)
                        if C:
                            tail.dve_normalise(dve, c)
                        for e in range(1, L0_D):
                            if A:
                                product(i, e)
                            if A and e == 1:
                                dve.wait_ge(rel_ready, i + 1)
                                nc.vector.tensor_reduce(relsum[:], denP[0:REL, :].rearrange("p (s n) -> p s n", s=SEQS), AX,
                                                        ALU.add).then_inc(rs_ready, 1)
                            if A:
                                running(i, e - 1)
                            if A and e == 3:
                                softmax_in(i)
                            if C and e == 4:
                                route.dve_1(dve, c)
                            if A and e == 5:
                                softmax_out(i)
                                if counted(i):
                                    dve.wait_ge(rec_ready, i)
                                dve.wait_ge(den_ready, i + 1)
                                nc.vector.tensor_scalar(clip[:], denP[0:DEN, :], EPS_DEN, None, ALU.max)
                                dve.drain()
                                if counted(i):
                                    dve.wait_ge(r_ready, i)
                                nc.vector.reciprocal(rec[:], clip[:]).then_inc(rec_ready, 1)
                            if C and e == 6:
                                route.dve_2(dve, c)
                            if A and e == 7:
                                dve.wait_ge(wT_ready, i + 1)
                                nc.vector.tensor_copy(wcol[0:REL, :], wT).then_inc(wcol_ready, 1)
                        if A:
                            running(i, L0_D - 1)
                        if B:
                            if counted(g):
                                dve.wait_ge(tail.tok_ready, g)
                            dve.wait_ge(wo_ready, g + 1)
                            nc.vector.tensor_tensor(y_sb[:], spreadP[1][:], resid[:, group(g)], ALU.add)\
                                .then_inc(tail.y_ready, 1)

                    staged(dve, period)

                @block.gpsimd
                def _(pool):
                    def period(i, A, B, C):
                        g, c = i - 1, i - 2
                        if B:
                            pool.wait_ge(qm_ready, 5 * g + 1)
                        for e in range(L0_D):
                            if B:
                                if counted(v := 12 * g + 4 + e - 1 if e >= 2 else 12 * (g - 1) + 11 + e):
                                    pool.wait_ge(acc_ready, v)
                                pool.wait_ge(cum_ready, 9 * g + e + 2)
                                nc.gpsimd.tensor_tensor(qkv[:, e % 2, :], cum[:, e, :], sq4[:], ALU.mult).then_inc(qkv_ready, 1)
                            if C and e == 1:
                                tail.pool_rstd(pool, c)
                            if A and e == 2:
                                if counted(i):
                                    pool.wait_ge(den_ready, i)
                                pool.wait_ge(sq_ready, i + 1)
                                pool.wait_ge(cum_ready, 9 * i + 1)
                                nc.gpsimd.tensor_tensor(qkv[:, 2, :], cum[:, L0_D, :], sq[:], ALU.mult).then_inc(qk_ready, 1)
                        if C:
                            route.pool_parts(pool, c)
                        if A:
                            stream.pool_split(pool, i)
                            if not (isinstance(i, int) and i == GROUPS - 1):
                                split.pool_lo(pool, i + 1)

                    split.pool_lo(pool, 0)
                    staged(pool, period)

        def attention1():
            s = lambda n: sem(f"a1_{n}")
            route = RouteGrouped("a1", L1_E, router1_sb)
            tail, split, stream = Tail("a1", route=route), Split("a1"), Stream("a1", w_ffn1, CH1)
            H, U = L1_HEADS, L1_HEADS * SEQS
            kp_ready, vp_ready, qp_ready = s("k_psum"), s("v_psum"), s("q_psum")
            k_ready, v_ready, q_ready = s("k_ready"), s("v_ready"), s("q_ready")
            sc_ready, nm_ready = s("scores_ready"), s("masked_ready")
            e_ready, r_ready, p_ready = s("exp_ready"), s("recip_ready"), s("probs_ready")
            tr_ready, pt_ready = s("probsT_psum"), s("probsT_ready")
            pv_ready, at_ready, acc_ready = s("pv_ready"), s("attn_ready"), s("acc_ready")

            with ExitStack() as own:
                def tb(name, shape, dt=F32):
                    return own.enter_context(nc.sbuf_tensor(f"a1_{name}", shape, dt))

                kT, vt, qT = tb("kT", [P, GT]), tb("vt", [P, TILES, P]), tb("qT", [P, 2, GT])
                SC = 3 * P
                ms, ex, pn = tb("ms", [P, 4, SC]), tb("ex", [P, 4, SC]), tb("pn", [P, 4, SC])
                mx, nm, rs, rr = (tb(n, [P, 4, 2]) for n in ("mx", "nm", "rs", "rr"))
                pT = tb("pT", [P, 2, SEQS, SC])
                at = tb("at", [P, H, GT])
                ring, scP, trP, pvP = bank[2:4], bank[4:6], bank[6], bank[7]
                wl1_hi, wl1_lo = tb("wl1_hi", [P, 10, P], F32R), tb("wl1_lo", [P, 10, P], F32R)
                wo1 = tb("wo1", [P, L1_HEADS, P])
                b_sb, bv_sb, pe_sb = tb("b_sb", [P, 9]), tb("bv_sb", [P, P]), tb("pe_sb", [P, GT])
                tri = tb("tri", [P, 2, P])
                raw1 = at[:, 0:4, :].rearrange("p a b -> p (a b)")[:, 0:10 * P].rearrange("p (a b) -> p a b", a=10)
                w_loaded, w_split = s("w_loaded"), s("w_split")
                with nc.Block() as setup:
                    @setup.sync
                    def _(sp):
                        sp.dma_start(raw1, w_l1).then_inc(w_loaded, 16)
                        sp.dma_start(wo1[:], wo_l1).then_inc(w_loaded, 16)
                        sp.dma_start(b_sb[:], b_l1).then_inc(w_loaded, 16)
                        sp.dma_start(bv_sb[:], bv_l1.partition_broadcast(P)).then_inc(w_loaded, 16)
                        sp.dma_start(pe_sb[:], peT).then_inc(w_loaded, 16)
                        sp.dma_start(tri[:], c_tri).then_inc(w_loaded, 16)

                    @setup.vector
                    def _(dve):
                        dve.wait_ge(w_loaded, 96)
                        nc.vector.tensor_copy(wl1_hi[:], raw1).then_inc(w_split, 1)
                        dve.wait_ge(w_split, 1)
                        nc.vector.tensor_tensor(wl1_lo[:], raw1, wl1_hi[:].bitcast(F32), ALU.subtract).then_inc(w_split, 1)
                        dve.wait_ge(w_split, 2)
                block = own.enter_context(nc.Block())

                @block.sync
                def _(sp):
                    stream.sp_load(sp, 0)
                    with sp.Fori(1, GROUPS) as i:
                        stream.sp_load(sp, i)

                @block.tensor
                def _(pe):
                    def project_q(i, h):
                        if h == 0:
                            pe.wait_ge(k_ready, i + 1)
                        elif h == 1:
                            pe.wait_ge(v_ready, i + 1)
                        else:
                            pe.wait_ge(q_ready, H * i + h - 1)
                        three_pass(ring[h % 2][:], wl1_hi[:, h, :], wl1_lo[:, h, :], x_hi[:], x_lo[:])\
                            .then_inc(qp_ready, 1)

                    def scores(i, h, q):
                        u = SEQS * h + q
                        if q == 0:
                            pe.wait_ge(q_ready, H * i + h + 1)
                        if counted(U * i + u - 1):
                            pe.wait_ge(nm_ready, U * i + u - 1)
                        o = q * SEQ
                        nc.tensor.matmul(scP[u % 2][:, 0:P], qT[:, h % 2, o:o + P], kT[:, o:o + P],
                                         start=True, stop=True)
                        nc.tensor.matmul(scP[u % 2][:, P:SC], qT[:, h % 2, o + P:o + SEQ], kT[:, o:o + SEQ],
                                         start=True, stop=True).then_inc(sc_ready, 1)

                    def transpose_probs(i, h, q):
                        u = SEQS * h + q
                        if counted(U * i + u):
                            pe.wait_ge(pt_ready, U * i + u)
                        pe.wait_ge(p_ready, U * i + u + 1)
                        for b in range(3):
                            cols = slice(b * P, (b + 1) * P)
                            last = nc.tensor.transpose(trP[:, cols], pn[:, u % 4, cols], ident[:])
                        last.then_inc(tr_ready, 1)

                    def values(i, h, q):
                        if q == 0:
                            if counted(H * i + h):
                                pe.wait_ge(at_ready, H * i + h)
                            pe.wait_ge(pt_ready, U * i + SEQS * h + SEQS)
                        nc.tensor.matmul(pvP[:, q * SEQ:(q + 1) * SEQ], vt[:, 2 * q, :],
                                         pT[:, h % 2, q, 0:SEQ], start=True, stop=False)
                        last = nc.tensor.matmul(pvP[:, q * SEQ + P:(q + 1) * SEQ], vt[:, 2 * q + 1, :],
                                                pT[:, h % 2, q, SEQ:SC], start=False, stop=True)
                        if q == SEQS - 1:
                            last.then_inc(pv_ready, 1)

                    def output(i, heads):
                        for h in heads:
                            if h == 0:
                                pe.wait_ge(q_ready, H * i + H)
                            pe.wait_ge(at_ready, H * i + h + 1)
                            last = nc.tensor.matmul(ring[1][:], wo1[:, h, :], at[:, h, :], start=(h == 0),
                                                    stop=(h == H - 1))
                        return last

                    def body(i, prev):
                        pe.wait_ge(split.lo_ready, i + 1)
                        if counted(H * i - 1):
                            pe.wait_ge(q_ready, H * i - 1)
                        three_pass(ring[0][:], wl1_hi[:, H, :], wl1_lo[:, H, :], x_hi[:], x_lo[:]).then_inc(kp_ready, 1)
                        if counted(i):
                            pe.wait_ge(tail.y_ready, i)
                        for t in range(TILES):
                            c = slice(t * P, (t + 1) * P)
                            last = three_pass(ring[1][:, c], x_hi[:, c], x_lo[:, c], wl1_hi[:, H + 1, :], wl1_lo[:, H + 1, :])
                        last.then_inc(vp_ready, 1)
                        project_q(i, 0)
                        for h in range(H + 3):
                            if h + 1 < H:
                                project_q(i, h + 1)
                            if prev is not None and h == 0:
                                tail.pe_tokens(pe, prev)
                            if h < H:
                                scores(i, h, 0)
                            if 2 <= h < H + 2:
                                transpose_probs(i, h - 2, 0)
                            if h < H:
                                scores(i, h, 1)
                            if h >= 3:
                                values(i, h - 3, 0)
                            if h >= H:
                                output(i, ((0, 1, 2), (3, 4, 5), (6,))[h - H])
                            if 2 <= h < H + 2:
                                transpose_probs(i, h - 2, 1)
                            if h >= 3:
                                values(i, h - 3, 1)
                            if prev is not None and h == 2:
                                tail.pe_features(pe, prev)
                            if prev is not None and h == 4:
                                route.pe_logits(pe, prev, tail)
                        if prev is not None:
                            route.pe_transpose(pe, prev)
                        output(i, (H - 1,)).then_inc(acc_ready, 1)

                    body(0, None)
                    body(1, 0)
                    with pe.Fori(2, GROUPS) as i:
                        body(i, i - 1)
                    tail.pe_tokens(pe, GROUPS - 1)
                    tail.pe_features(pe, GROUPS - 1)
                    route.pe_logits(pe, GROUPS - 1, tail)
                    route.pe_transpose(pe, GROUPS - 1)

                @block.scalar
                def _(act):
                    def exponent(i, h, q):
                        u = SEQS * h + q
                        if counted(U * i + u - 3):
                            act.wait_ge(p_ready, U * i + u - 3)
                        act.wait_ge(nm_ready, U * i + u + 1)
                        for b, c in enumerate((slice(0, P), slice(P, SC))):
                            last = nc.scalar.activation(ex[:, u % 4, c], ms[:, u % 4, c], ACT.Exp, scale=SCALE,
                                                        bias=nm[:, u % 4, b:b + 1], accum_out=rs[:, u % 4, b:b + 1])
                        last.then_inc(e_ready, 1)

                    def store_transposed(i, h, q):
                        u = SEQS * h + q
                        if counted(H * i + h - 1):
                            act.wait_ge(pv_ready, H * i + h - 1)
                        act.wait_ge(tr_ready, U * i + u + 1)
                        nc.scalar.activation(pT[:, h % 2, q, :], trP[:, 0:SC], ACT.Copy).then_inc(pt_ready, 1)

                    def body(i, prev):
                        for h in range(H + 3):
                            if 2 <= h < H + 2:
                                store_transposed(i, h - 2, 0)
                            if h < H:
                                exponent(i, h, 0)
                                exponent(i, h, 1)
                            if 2 <= h < H + 2:
                                store_transposed(i, h - 2, 1)
                            if h >= 3:
                                g = h - 3
                                if g == 0:
                                    if counted(i):
                                        act.wait_ge(acc_ready, i)
                                act.wait_ge(pv_ready, H * i + g + 1)
                                nc.scalar.activation(at[:, g, :], pvP[:], ACT.Copy).then_inc(at_ready, 1)
                            if prev is not None and h == 3:
                                tail.act_resid(act, prev)
                            if prev is not None and h == 4:
                                route.act_exp(act, prev)
                            if h == H and not (isinstance(i, int) and i == GROUPS - 1):
                                act.wait_ge(qp_ready, H * i + H)
                                act.wait_ge(s_cast, 1)
                                split.act_hi(act, i + 1)
                        if prev is not None:
                            route.act_cwT(act, prev)

                    split.act_hi(act, 0)
                    body(0, None)
                    body(1, 0)
                    with act.Fori(2, GROUPS - 1) as i:
                        body(i, i - 1)
                    body(GROUPS - 1, GROUPS - 2)
                    tail.act_resid(act, GROUPS - 1)
                    route.act_exp(act, GROUPS - 1)
                    route.act_cwT(act, GROUPS - 1)

                @block.vector
                def _(dve):
                    def evacuate_q(i, h):
                        if counted(v := U * i + SEQS * (h - 1) if h >= 2 else U * (i - 1) + U - SEQS * (1 - h)):
                            dve.wait_ge(sc_ready, v)
                        dve.wait_ge(qp_ready, H * i + h + 1)
                        nc.vector.scalar_tensor_tensor(out=qT[:, h % 2, :], in0=ring[h % 2][:], scalar=b_sb[:, h:h + 1],
                                                       in1=pe_sb[:], op0=ALU.add, op1=ALU.add).then_inc(q_ready, 1)

                    def mask_and_max(i, h, q):
                        u = SEQS * h + q
                        read, scored = snapped(dve, U * i + u - 3), snapped(dve, U * i + u + 1)
                        dve.wait_ge(s_cast, 1)
                        if counted(read):
                            dve.wait_ge(e_ready, read)
                        dve.wait_ge(sc_ready, scored)
                        nc.vector.tensor_tensor_reduce(out=ms[:, u % 4, 0:P], in0=scP[u % 2][:, 0:P], in1=tri[:, 1, :],
                                                       scale=1.0, scalar=MASKED, op0=ALU.add, op1=ALU.max,
                                                       accum_out=mx[:, u % 4, 0:1])
                        nc.vector.tensor_tensor_reduce(out=ms[:, u % 4, P:SC], in0=scP[u % 2][:, P:SC],
                                                       in1=tri[:].rearrange("p a b -> p (a b)"),
                                                       scale=1.0, scalar=MASKED, op0=ALU.add, op1=ALU.max,
                                                       accum_out=mx[:, u % 4, 1:2])
                        dve.drain()
                        nc.vector.tensor_scalar(nm[:, u % 4, :], mx[:, u % 4, :], -SCALE, None, ALU.mult)\
                            .then_inc(nm_ready, 1)

                    def residual(i):
                        if counted(i):
                            dve.wait_ge(tail.tok_ready, i)
                        dve.wait_ge(acc_ready, i + 1)
                        nc.vector.tensor_tensor(y_sb[:], ring[1][:], resid[:, group(i)], ALU.add).then_inc(tail.y_ready, 1)

                    def body(i, prev):
                        if counted(U * i):
                            dve.wait_ge(sc_ready, U * i)
                        dve.wait_ge(kp_ready, i + 1)
                        nc.vector.scalar_tensor_tensor(out=kT[:], in0=ring[0][:], scalar=b_sb[:, H:H + 1], in1=pe_sb[:],
                                                       op0=ALU.add, op1=ALU.add).then_inc(k_ready, 1)
                        if counted(H * i):
                            dve.wait_ge(pv_ready, H * i)
                        dve.wait_ge(vp_ready, i + 1)
                        nc.vector.tensor_tensor(vt[:], ring[1][:].rearrange("p (t n) -> p t n", t=TILES),
                                                bv_sb[:].unsqueeze(1).broadcast_to([P, TILES, P]), ALU.add).then_inc(v_ready, 1)
                        evacuate_q(i, 0)
                        for h in range(H + 1):
                            if h + 1 < H:
                                evacuate_q(i, h + 1)
                            if h < H:
                                mask_and_max(i, h, 0)
                                mask_and_max(i, h, 1)
                            if h >= 1:
                                for u in range(SEQS * (h - 1), SEQS * h):
                                    dve.wait_ge(e_ready, U * i + u + 1)
                                    nc.vector.reciprocal(rr[:, u % 4, :], rs[:, u % 4, :]).then_inc(r_ready, 1)
                            if prev is not None and h == 0:
                                tail.dve_stats(dve, prev)
                            if prev is not None and h == 1:
                                tail.dve_normalise(dve, prev)
                            if prev is not None and h == 5:
                                route.dve_1(dve, prev)
                        if prev is not None:
                            route.dve_2(dve, prev)
                        residual(i)

                    body(0, None)
                    body(1, 0)
                    with dve.Fori(2, GROUPS) as i:
                        body(i, i - 1)
                    tail.dve_stats(dve, GROUPS - 1)
                    tail.dve_normalise(dve, GROUPS - 1)
                    route.dve_1(dve, GROUPS - 1)
                    route.dve_2(dve, GROUPS - 1)

                @block.gpsimd
                def _(pool):
                    def body(i, prev):
                        if prev is not None:
                            tail.pool_rstd(pool, prev)
                        for u in range(U):
                            if counted(U * i + u - 3):
                                pool.wait_ge(tr_ready, U * i + u - 3)
                            pool.wait_ge(r_ready, U * i + u + 1)
                            nc.gpsimd.tensor_tensor(pn[:, u % 4, 0:P], ex[:, u % 4, 0:P],
                                                    rr[:, u % 4, 0:1].broadcast_to([P, P]), ALU.mult)
                            nc.gpsimd.tensor_tensor(pn[:, u % 4, P:SC], ex[:, u % 4, P:SC],
                                                    rr[:, u % 4, 1:2].broadcast_to([P, SC - P]), ALU.mult).then_inc(p_ready, 1)
                            if u == 4:
                                stream.pool_split(pool, i)
                        if not (isinstance(i, int) and i == GROUPS - 1):
                            split.pool_lo(pool, i + 1)
                        if prev is not None:
                            route.pool_parts(pool, prev)

                    split.pool_lo(pool, 0)
                    body(0, None)
                    body(1, 0)
                    with pool.Fori(2, GROUPS - 1) as i:
                        body(i, i - 1)
                    body(GROUPS - 1, GROUPS - 2)
                    tail.pool_rstd(pool, GROUPS - 1)
                    route.pool_parts(pool, GROUPS - 1)

        def experts(part, NT, routed, per_weight, sel, e3, last):
            s = lambda n: sem(f"{part}_{n}")
            tail, split = Tail(part, last=last), Split(part)
            NB = routed // per_weight
            gu_ready, bc_ready = s("gate_up_ready"), s("weight_psum")
            s_ready, bw_ready = s("silu_ready"), s("weight_ready")
            w_ready = s("weighted_ready")
            h_ready, hhi_ready, hlo_ready = s("h_ready"), s("h_hi_ready"), s("h_lo_ready")
            down_ready = s("down_done")
            LAG = 3
            GATE, UP, DOWN = 0, NT * P, 2 * NT * P

            def w(which, base, t):
                return which[:, base + t * P:base + (t + 1) * P]

            with ExitStack() as own:
                def tb(name, shape, dt=F32):
                    return own.enter_context(nc.sbuf_tensor(f"{part}_{name}", shape, dt))

                sl, sw, bw = tb("sl", [P, 2, GT]), tb("sw", [P, 2, GT]), tb("bw", [P, 2, GT])
                hh, h_hi, h_lo = tb("hh", [P, 2, GT]), tb("h_hi", [P, LAG, GT], F32R), tb("h_lo", [P, LAG, GT], F32R)
                bcP, gP, uP, acc = bank[1], bank[2:4], bank[4:6], bank[6]
                block = own.enter_context(nc.Block())

                if last:
                    @block.sync
                    def _(sp):
                        def body(i):
                            tail.sp_store(sp, i)
                        run(sp, body, body)
                        sp.wait_ge(tail.stored, 16 * GROUPS)

                @block.tensor
                def _(pe):
                    def down(i, t):
                        if t == 0:
                            if counted(i):
                                pe.wait_ge(tail.y_ready, i)
                        pe.wait_ge(hlo_ready, NT * i + t + 1)
                        three_pass(acc[:], w(ffn_hi, DOWN, t), w(ffn_lo, DOWN, t), h_hi[:, t % LAG, :], h_lo[:, t % LAG, :],
                                   start=(t == 0), stop=(t == NT - 1)).then_inc(down_ready, 1)

                    def body(i, prev):
                        pe.wait_ge(split.lo_ready, i + 1)
                        for t in range(NT):
                            if t < routed and t % per_weight == 0:
                                b = t // per_weight
                                read = snapped(pe, NB * i + b)
                                pe.wait_ge(s_cast, 1)
                                if counted(read):
                                    pe.wait_ge(bw_ready, read)
                                nc.tensor.matmul(bcP[:], sel[:, b, :], cwT[0:e3, group(i)], start=True, stop=True)\
                                    .then_inc(bc_ready, 1)
                            if counted(last_use(i, t, NT, 2)):
                                pe.wait_ge(h_ready, last_use(i, t, NT, 2))
                            three_pass(gP[t % 2][:], w(ffn_hi, GATE, t), w(ffn_lo, GATE, t), x_hi[:], x_lo[:])
                            three_pass(uP[t % 2][:], w(ffn_hi, UP, t), w(ffn_lo, UP, t), x_hi[:], x_lo[:])\
                                .then_inc(gu_ready, 1)
                            if t >= LAG:
                                down(i, t - LAG)
                            if prev is not None and t == 3:
                                tail.pe_tokens(pe, prev)
                            if prev is not None and t == 7:
                                tail.pe_features(pe, prev)
                        for t in range(NT - LAG, NT):
                            down(i, t)

                    body(0, None)
                    body(1, 0)
                    with pe.Fori(2, GROUPS) as i:
                        body(i, i - 1)
                    tail.pe_tokens(pe, GROUPS - 1)
                    tail.pe_features(pe, GROUPS - 1)

                @block.scalar
                def _(act):
                    def high(i, t):
                        if counted(v := last_use(i, t, NT, LAG)):
                            act.wait_ge(down_ready, v)
                        act.wait_ge(h_ready, NT * i + t + 1)
                        nc.scalar.activation(h_hi[:, t % LAG, :], hh[:, t % 2, :], ACT.Copy).then_inc(hhi_ready, 1)

                    def body(i, prev):
                        for t in range(NT):
                            if t < routed and t % per_weight == 0:
                                b = t // per_weight
                                if counted(v := NT * i + t - per_weight if b >= 2 else NT * (i - 1) + routed):
                                    act.wait_ge(h_ready, v)
                                act.wait_ge(bc_ready, NB * i + b + 1)
                                nc.scalar.activation(bw[:, b % 2, :], bcP[:], ACT.Copy).then_inc(bw_ready, 1)
                            if counted(last_use(i, t, NT, 2)):
                                act.wait_ge(h_ready, last_use(i, t, NT, 2))
                            act.wait_ge(gu_ready, NT * i + t + 1)
                            nc.scalar.activation(sl[:, t % 2, :], gP[t % 2][:], ACT.Silu).then_inc(s_ready, 1)
                            if t >= 1:
                                high(i, t - 1)
                            if prev is not None and not last and t == 8:
                                tail.act_resid(act, prev)

                    split.act_hi(act, 0)
                    body(0, None)

                    def prepare(i):
                        act.wait_ge(gu_ready, NT * i)
                        act.wait_ge(s_cast, 1)
                        split.act_hi(act, i)
                        high(i - 1, NT - 1)

                    prepare(1)
                    body(1, 0)
                    with act.Fori(2, GROUPS) as i:
                        prepare(i)
                        body(i, i - 1)
                    high(GROUPS - 1, NT - 1)
                    if not last:
                        tail.act_resid(act, GROUPS - 1)

                @block.vector
                def _(dve):
                    def low(i, t):
                        if counted(v := last_use(i, t, NT, LAG)):
                            dve.wait_ge(down_ready, v)
                        dve.wait_ge(hhi_ready, NT * i + t + 1)
                        nc.vector.tensor_tensor(h_lo[:, t % LAG, :], hh[:, t % 2, :], h_hi[:, t % LAG, :].bitcast(F32),
                                                ALU.subtract).then_inc(hlo_ready, 1)

                    def body(i, prev):
                        for t in range(NT):
                            if counted(last_use(i, t, NT, 2)):
                                dve.wait_ge(hlo_ready, last_use(i, t, NT, 2))
                            dve.wait_ge(gu_ready, NT * i + t + 1)
                            if t < routed:
                                dve.wait_ge(w_ready, routed * i + t + 1)
                            else:
                                dve.wait_ge(s_ready, NT * i + t + 1)
                            nc.vector.tensor_tensor(hh[:, t % 2, :], uP[t % 2][:], (sw if t < routed else sl)[:, t % 2, :],
                                                    ALU.mult).then_inc(h_ready, 1)
                            if t >= 1:
                                low(i, t - 1)
                            if prev is not None and t == 4:
                                tail.dve_stats(dve, prev)
                            if prev is not None and t == 5:
                                tail.dve_normalise(dve, prev)
                        low(i, NT - 1)
                        if counted(i):
                            dve.wait_ge(tail.tok_ready, i)
                        dve.wait_ge(down_ready, NT * i + NT)
                        nc.vector.tensor_tensor(y_sb[:], acc[:], resid[:, group(i)], ALU.add).then_inc(tail.y_ready, 1)

                    body(0, None)
                    body(1, 0)
                    with dve.Fori(2, GROUPS) as i:
                        body(i, i - 1)
                    tail.dve_stats(dve, GROUPS - 1)
                    tail.dve_normalise(dve, GROUPS - 1)

                @block.gpsimd
                def _(pool):
                    def body(i, prev):
                        split.pool_lo(pool, i)
                        for t in range(routed):
                            b = t // per_weight
                            if counted(v := last_use(i, t, NT, 2) if t >= 2 else NT * (i - 1) + routed):
                                pool.wait_ge(h_ready, v)
                            pool.wait_ge(bw_ready, NB * i + b + 1)
                            pool.wait_ge(s_ready, NT * i + t + 1)
                            nc.gpsimd.tensor_tensor(sw[:, t % 2, :], sl[:, t % 2, :], bw[:, b % 2, :], ALU.mult)\
                                .then_inc(w_ready, 1)
                            if prev is not None and t == 4:
                                tail.pool_rstd(pool, prev)

                    body(0, None)
                    body(1, 0)
                    with pool.Fori(2, GROUPS) as i:
                        body(i, i - 1)
                    tail.pool_rstd(pool, GROUPS - 1)

        attention0()
        only_l0.close()
        experts("f0", L0_TILES, L0_E * L0_HID // P, L0_HID // P, sel0, 3 * L0_E, False)
        attention1()
        experts("f1", L1_TILES, L1_TILES - 1, 1, sel1, 3 * L1_E, True)


def constants():
    p = np.arange(P)
    head = p // L0_D
    f = [np.eye(P), head[:, None] == np.arange(L0_HEADS)[None, :]]
    e, c = np.arange(L0_D)[None, :, None], p[None, None, :]
    f.append(((head[:, None, None] == c // L0_D) & (c % L0_D == e)).reshape(P, -1))
    f.append(np.broadcast_to(np.arange(GT)[None, :] % SEQ != 0, (P, GT)))
    f.append(np.broadcast_to(np.arange(8), (P, 8)))
    row = p[:, None, None]
    f.append((row == np.arange(MEMS + 1)[None, :, None] * L0_HEADS + head[None, None, :]).reshape(P, -1))
    c_f32 = np.concatenate([np.asarray(a, np.float32) for a in f], axis=1)
    tri = np.stack([np.zeros((P, P)), np.where(p[None, :] <= p[:, None], 0.0, MASKED)], axis=1).astype(np.float32)
    r0 = np.arange(3 * L0_E) % L0_E
    sel0 = np.broadcast_to(r0[:, None, None] == np.arange(L0_E)[None, :, None], (3 * L0_E, L0_E, P))
    r1 = np.arange(3 * L1_E) % L1_E
    per = P // L1_HID
    sel1 = r1[:, None, None] == np.arange(L1_TILES - 1)[None, :, None] * per + p[None, None, :] // L1_HID
    pos = np.arange(SEQ, dtype=np.float32)[:, None]
    inv = np.exp(np.float32(-math.log(10000.0)) * np.arange(0, P, 2, dtype=np.float32) / np.float32(P))
    ang = (pos * inv[None, :]).astype(np.float32)
    pe = np.zeros((SEQ, P), np.float32)
    pe[:, 0::2], pe[:, 1::2] = np.sin(ang), np.cos(ang)
    peT = np.concatenate([pe.T] * SEQS, axis=1)
    return (np.ascontiguousarray(c_f32), tri, np.ascontiguousarray(sel0.astype(np.float32)),
            np.ascontiguousarray(sel1.astype(np.float32)), np.ascontiguousarray(peT))


def kernel(**inputs):
    import concourse.bacc as bacc
    from concourse.bass_utils import run_bass_kernel_spmd

    g = {k: np.asarray(v) for k, v in inputs.items()}
    c_f32, c_tri, c_sel0, c_sel1, peT = constants()
    a = {}
    a["xT"] = g["L0_attn_hidden_states"].reshape(TOKENS, DM).T
    wl0 = np.zeros((P, 11, P), np.float32)
    wl0[:, 0], wl0[:, 1], wl0[:, 10] = g["L0_attn_w_q"].T, g["L0_attn_w_k"].T, g["L0_attn_w_o"].T
    wv = g["L0_attn_w_v"].T.reshape(P, L0_HEADS, L0_D)
    for e in range(L0_D):
        wl0[:, 2 + e] = np.repeat(wv[:, :, e], L0_D, axis=1)
    a["w_l0"] = wl0
    mem = np.zeros((P, MEMS, P), np.float32)
    norms = np.zeros((P, REL), np.float32)
    for h in range(L0_HEADS):
        r = slice(h * L0_D, (h + 1) * L0_D)
        for m in range(MEMS):
            mem[r, m, r] = g["L0_attn_memories"][m, h]
            norms[r, m * L0_HEADS + h] = g["L0_attn_memory_norms"][m, h]
    a["mem_bd"], a["norms_bd"], a["gate"] = mem, norms, g["L0_attn_gate"]

    def up(*ws):
        return np.concatenate([w.reshape(-1, DM).T for w in ws], axis=1)

    def down(*ws):
        rows = np.concatenate([w.swapaxes(1, 2).reshape(-1, DM) for w in ws], axis=0)
        return rows.reshape(-1, P, DM).swapaxes(0, 1).reshape(P, -1)

    def padded(w, axis):
        return np.concatenate([w, np.zeros_like(w)], axis=axis)

    a["w_ffn0"] = np.concatenate([up(g["L0_ffn_w1"], g["L0_ffn_sw1"]), up(g["L0_ffn_w3"], g["L0_ffn_sw3"]),
                                  down(g["L0_ffn_w2"], g["L0_ffn_sw2"])], axis=1)
    a["w_ffn1"] = np.concatenate([
        up(g["L1_ffn_expert_gate"], padded(g["L1_ffn_shared_gate_w"], 0)),
        up(g["L1_ffn_expert_up"], padded(g["L1_ffn_shared_up_w"], 0)),
        down(g["L1_ffn_expert_down"], padded(g["L1_ffn_shared_down_w"], 1)[None])], axis=1)
    a["router0"], a["bias0"], a["router1"] = g["L0_ffn_router_w"].T, g["L0_ffn_expert_bias"], g["L1_ffn_gate_w"].T
    wl1 = np.concatenate([g["L1_attn_Wq"], g["L1_attn_Wkv"]], axis=1)
    a["w_l1"] = wl1.reshape(P, 10, P)
    a["wo_l1"] = g["L1_attn_Wo"].reshape(L1_HEADS, P, P).swapaxes(0, 1)
    a["b_l1"] = np.concatenate([g["L1_attn_bq"].reshape(L1_HEADS, P).T, g["L1_attn_bkv"][:P, None]], axis=1)
    a["bv_l1"] = g["L1_attn_bkv"][P:]
    a["peT"], a["c_f32"], a["c_tri"], a["c_sel0"], a["c_sel1"] = peT, c_f32, c_tri, c_sel0, c_sel1

    nc = bacc.Bacc("TRN2", target_bir_lowering=False, num_devices=1)
    arrays, args = {}, []
    for name, x in a.items():
        x = np.ascontiguousarray(x)
        arrays[f"in_{name}"] = x
        args.append(nc.dram_tensor(f"in_{name}", x.shape, mybir.dt.from_np(x.dtype), kind="ExternalInput").ap())
    args.append(nc.dram_tensor("out_x", (TOKENS, DM), F32, kind="ExternalOutput").ap())
    build(nc, *args)
    r = run_bass_kernel_spmd(nc, [arrays], core_ids=[0])
    return r.results[0]["out_x"].reshape(BATCH, SEQ, DM)
```

```python
import math
from contextlib import ExitStack

import numpy as np

import concourse.bass as bass
from concourse import mybir

F32 = mybir.dt.float32
F32R = mybir.dt.float32r
BF16 = mybir.dt.bfloat16
U32 = mybir.dt.uint32
ALU = mybir.AluOpType
ACT = mybir.ActivationFunctionType
AX = mybir.AxisListType.X

P = 128
BATCH, SEQ, DM = 32, 256, 128
TOKENS = BATCH * SEQ
GT = 512
GROUPS = TOKENS // GT
TILES = GT // P
SEQS = GT // SEQ
L0_HEADS, L0_D, MEMS = 16, 8, 4
L1_HEADS = 8
L0_E, L0_HID, L0_SHARED = 8, 256, 2
L1_E, L1_HID = 32, 64
L1_PER = 4
EPS_DEN, EPS_LN, EPS_TOPK = 1e-6, 1e-5, 1e-12
SCALE = 1.0 / math.sqrt(P)
MASKED = -3.0e38
L0_TILES = (L0_E + L0_SHARED) * L0_HID // P
L1_TILES = L1_E * L1_HID // P + 1
REL = MEMS * L0_HEADS
DEN = REL + L0_HEADS


def counted(value):
    return not isinstance(value, int) or value > 0




def snapped(eng, value):
    return value if isinstance(value, int) else eng.to_reg(value)


def last_use(i, n, per, slots):
    if n >= slots:
        return i * per + n - slots + 1
    last = max(m for m in range(per) if m % slots == n % slots)
    return (i - 1) * per + last + 1


def build(nc, xT, w_l0, mem_bd, norms_bd, gate, w_ffn0, w_ffn1, router0, bias0, router1,
          w_l1, wo_l1, b_l1, bv_l1, peT, c_f32, c_tri, c_sel0, c_sel1, out):
    ctx = ExitStack()
    with ctx:
        def sb(name, shape, dt=F32):
            return ctx.enter_context(nc.sbuf_tensor(name, shape, dt))

        def sem(name):
            return ctx.enter_context(nc.semaphore(name))

        bank = [ctx.enter_context(nc.psum_tensor(f"bank{b}", [P, GT], F32)) for b in range(8)]

        resid = sb("resid", [P, TOKENS])
        x_hi, x_lo = sb("x_hi", [P, GT], F32R), sb("x_lo", [P, GT], F32R)
        cwT = sb("cwT", [96, TOKENS], BF16)
        NW0, NW1 = 3 * L0_TILES * P, 3 * L1_TILES * P
        ffn_hi, ffn_lo = sb("ffn_hi", [P, NW0], F32R), sb("ffn_lo", [P, NW0], F32R)
        CH0, CH1 = NW0 // GROUPS, NW1 // GROUPS
        stage = sb("stage", [P, max(CH0, CH1)])
        ident = sb("ident", [P, P])
        ident_bf = sb("ident_bf", [P, P], BF16)
        half = sb("half", [P, TILES])
        y_sb, z_sb = sb("y_sb", [P, GT]), sb("z_sb", [P, TILES, P])
        stats, mv = sb("stats", [P, TILES, 6]), sb("mv", [P, TILES, 3])
        var_eps, rstd, shift = sb("var_eps", [P, TILES]), sb("rstd", [P, TILES]), sb("shift", [P, TILES])
        router0_sb, router1_sb = sb("router0_sb", [P, L0_E]), sb("router1_sb", [P, L1_E])
        bias0_sb = sb("bias0_sb", [P, L0_E])
        iota8 = sb("iota8", [P, 8])
        sel0 = sb("sel0", [3 * L0_E, L0_E, P], BF16)
        sel1 = sb("sel1", [3 * L1_E, L1_TILES - 1, P], BF16)

        lg = sb("lg", [P, TILES, L1_E])
        sg = sb("sg", [P, TILES, L1_E])
        cw = sb("cw", [P, TILES, L1_E])
        rest_w = sb("rest_w", [P, TILES, L1_E])
        cw3 = sb("cw3", [P, TILES, 3 * L1_E], BF16)
        top = sb("top", [P, TILES, 8])
        idx = sb("idx", [P, TILES, 8], U32)
        idxf = sb("idxf", [P, TILES, 8])
        gsum, gmask = sb("gsum", [P, TILES, 8]), sb("gmask", [P, TILES, 8])
        xf = sb("xf", [P, GT])
        eq4 = sb("eq4", [P, TILES, 8, 4])
        pair = sb("pair", [P, 4, TILES])

        only_l0 = ExitStack()

        def sb0(name, shape, dt=F32):
            return only_l0.enter_context(nc.sbuf_tensor(name, shape, dt))

        wl0_hi, wl0_lo = sb0("wl0_hi", [P, 10, P], F32R), sb0("wl0_lo", [P, 10, P], F32R)
        wo0 = sb0("wo0", [P, P])
        mem_sb, norms_sb = sb0("mem_sb", [P, MEMS, P]), sb0("norms_sb", [P, REL])
        headsum = sb0("headsum", [P, L0_HEADS])
        spread = sb0("spread", [DEN, MEMS + 1, P])
        blocksum = sb0("blocksum", [P, L0_D, P])
        reset = sb0("reset", [P, GT])
        gate_row, gate_col = sb0("gate_row", [SEQS, L0_HEADS]), sb0("gate_col", [DEN, 1])
        wcol = sb0("wcol", [DEN, SEQS])
        x_loaded = sem("x_loaded")
        s_const, s_raw, s_ones, s_cast = sem("consts_loaded"), sem("raw_loaded"), sem("gates_exp"), sem("setup_done")
        with nc.sbuf_tensor("raw", [P, 10, P], F32) as raw, nc.sbuf_tensor("gtmp", [P, 16], F32) as gtmp, \
                nc.sbuf_tensor("sel0_raw", [3 * L0_E, L0_E, P], F32) as sel0_raw, \
                nc.sbuf_tensor("sel1_raw", [3 * L1_E, L1_TILES - 1, P], F32) as sel1_raw, \
                nc.Block() as block:
            @block.sync
            def _(sp):
                o = 0
                for dst, w in ((ident[:], P), (headsum[:], L0_HEADS), (blocksum[:], L0_D * P), (reset[:], GT),
                               (iota8[:], 8)):
                    src = c_f32[:, o:o + w]
                    if len(dst.shape) == 3:
                        src = src.rearrange("p (a b) -> p a b", a=dst.shape[1])
                    sp.dma_start(dst, src).then_inc(s_const, 16)
                    o += w
                c_spread = c_f32[0:DEN, o:o + (MEMS + 1) * P].rearrange("p (a b) -> p a b", a=MEMS + 1)
                sp.dma_start(spread[:], c_spread).then_inc(s_const, 16)
                sp.dma_start(sel0_raw[:], c_sel0).then_inc(s_const, 16)
                sp.dma_start(sel1_raw[:], c_sel1).then_inc(s_const, 16)
                sp.dma_start(mem_sb[:], mem_bd).then_inc(s_const, 16)
                sp.dma_start(norms_sb[:], norms_bd).then_inc(s_const, 16)
                sp.dma_start(router0_sb[:], router0).then_inc(s_const, 16)
                sp.dma_start(router1_sb[:], router1).then_inc(s_const, 16)
                sp.dma_start(bias0_sb[:], bias0.partition_broadcast(P)).then_inc(s_const, 16)
                sp.wait_ge(s_const, 16 * 13)

            @block.scalar
            def _(act):
                act.dma_start(raw[:], w_l0[:, 0:10, :]).then_inc(s_raw, 16)
                act.dma_start(resid[:, 0:GT], xT[:, 0:GT]).then_inc(x_loaded, 16)
                act.dma_start(wo0[:], w_l0[:, 10, :]).then_inc(s_raw, 16)
                act.dma_start(gate_row[:], gate.partition_broadcast(SEQS)).then_inc(s_raw, 16)
                act.dma_start(gate_col[REL:DEN, :], gate.rearrange("(h a) -> h a", a=1)).then_inc(s_raw, 16)
                act.wait_ge(s_raw, 64)
                nc.scalar.activation(gtmp[0:SEQS, :], gate_row[:], ACT.Exp, scale=-1.0).then_inc(s_ones, 1)
                nc.scalar.activation(gtmp[REL:DEN, 0:1], gate_col[REL:DEN, :], ACT.Exp).then_inc(s_ones, 1)
                act.wait_ge(s_const, 16 * 13)
                nc.scalar.activation(sel0[:], sel0_raw[:], ACT.Copy)
                nc.scalar.activation(sel1[:], sel1_raw[:], ACT.Copy)
                nc.scalar.activation(ident_bf[:], ident[:], ACT.Copy)

            @block.vector
            def _(dve):
                nc.vector.memset(half[:], -0.5)
                dve.wait_ge(s_raw, 64)
                nc.vector.tensor_copy(wl0_hi[:], raw[:])
                dve.drain()
                nc.vector.tensor_tensor(wl0_lo[:], raw[:], wl0_hi[:].bitcast(F32), ALU.subtract)
                dve.wait_ge(s_ones, 2)
                nc.vector.tensor_scalar(gtmp[0:SEQS, :], gtmp[0:SEQS, :], 1.0, None, ALU.add)
                nc.vector.tensor_scalar(gtmp[REL:DEN, 0:1], gtmp[REL:DEN, 0:1], 1.0, None, ALU.add)
                dve.drain()
                nc.vector.reciprocal(gate_row[:], gtmp[0:SEQS, :])
                nc.vector.reciprocal(gate_col[REL:DEN, :], gtmp[REL:DEN, 0:1])
                dve.drain()
                for s in range(SEQS):
                    last = nc.vector.tensor_copy(wcol[REL:DEN, s:s + 1], gate_col[REL:DEN, :])
                last.then_inc(s_cast, 1)
                dve.wait_ge(s_cast, 1)

        def group(i, n=GT):
            return bass.ds(i * n, n)

        class Tail:

            def __init__(self, part, last=False, route=None, on_act=False):
                self.last, self.route, self.on_act = last, route, on_act
                self.shift_ready = sem(f"{part}_shift_ready")
                self.y_ready = sem(f"{part}_y_ready")
                self.tok_ready = sem(f"{part}_tok_ready")
                self.stats_ready = sem(f"{part}_stats_ready")
                self.var_ready = sem(f"{part}_var_ready")
                self.rstd_ready = sem(f"{part}_rstd_ready")
                self.z_ready = sem(f"{part}_z_ready")
                self.feat_ready = sem(f"{part}_feat_ready")
                self.x_ready = sem(f"{part}_x_ready")
                self.stored = sem(f"{part}_stored")

            def pe_tokens(self, pe, i):
                pe.wait_ge(self.y_ready, i + 1)
                if counted(i):
                    pe.wait_ge(self.z_ready if self.last else self.x_ready, i)
                for t in range(TILES):
                    last = nc.tensor.transpose(bank[0][:, t * P:(t + 1) * P], y_sb[:, t * P:(t + 1) * P], ident[:])
                last.then_inc(self.tok_ready, 1)

            def pe_features(self, pe, i):
                if self.last:
                    return
                pe.wait_ge(self.z_ready, i + 1)
                for t in range(TILES):
                    last = nc.tensor.transpose(bank[0][:, t * P:(t + 1) * P], z_sb[:, t, :], ident[:])
                last.then_inc(self.feat_ready, 1)

            def dve_stats(self, dve, i):
                dve.wait_ge(s_cast, 1)
                if counted(i):
                    dve.wait_ge(self.rstd_ready, i)
                dve.wait_ge(self.tok_ready, i + 1)
                for t in range(TILES):
                    nc.vector.bn_stats(stats[:, t, :], bank[0][:, t * P:(t + 1) * P])
                dve.drain()
                for t in range(TILES):
                    last = nc.vector.bn_aggr(mv[:, t, 0:2], stats[:, t, :])
                if self.on_act:
                    dve.drain()
                    last = nc.vector.tensor_scalar(mv[:, :, 2], mv[:, :, 0], -1.0, None, ALU.mult)
                last.then_inc(self.stats_ready, 1)

            def pool_rstd(self, pool, i):
                normalised, ready = snapped(pool, i), snapped(pool, i + 1)
                pool.wait_ge(s_cast, 1)
                if counted(normalised):
                    pool.wait_ge(self.z_ready, normalised)
                pool.wait_ge(self.stats_ready, ready)
                nc.gpsimd.tensor_scalar(var_eps[:], mv[:, :, 1], EPS_LN, None, ALU.add).then_inc(self.var_ready, 1)
                pool.wait_ge(self.var_ready, i + 1)
                nc.gpsimd.tensor_tensor(rstd[:], var_eps[:], half[:], ALU.pow).then_inc(self.rstd_ready, 1)
                if self.on_act:
                    pool.wait_ge(self.rstd_ready, i + 1)
                    nc.gpsimd.tensor_tensor(shift[:], mv[:, :, 2], rstd[:], ALU.mult).then_inc(self.shift_ready, 1)

            def dve_normalise(self, dve, i, tiles=range(TILES)):
                if tiles[0] == 0 and counted(i):
                    if self.last:
                        dve.wait_ge(self.stored, 16 * i)
                    else:
                        dve.wait_ge(self.feat_ready, i)
                dve.wait_ge(self.rstd_ready, i + 1)
                for t in tiles:
                    last = nc.vector.tensor_scalar(z_sb[:, t, :], bank[0][:, t * P:(t + 1) * P], mv[:, t, 0:1],
                                                   rstd[:, t:t + 1], ALU.subtract, ALU.mult)
                if tiles[-1] == TILES - 1:
                    last.then_inc(self.z_ready, 1)

            def act_normalise(self, act, i):
                if counted(i):
                    act.wait_ge(self.feat_ready, i)
                act.wait_ge(self.shift_ready, i + 1)
                for t in range(TILES):
                    last = nc.scalar.activation(z_sb[:, t, :], bank[0][:, t * P:(t + 1) * P], ACT.Identity,
                                                scale=rstd[:, t:t + 1], bias=shift[:, t:t + 1])
                last.then_inc(self.z_ready, 1)

            def act_resid(self, act, i):
                if self.route:
                    if counted(i):
                        act.wait_ge(self.route.logits_ready, i)
                act.wait_ge(self.feat_ready, i + 1)
                if self.route:
                    nc.scalar.activation(xf[:], bank[0][:], ACT.Copy)
                act.wait_ge(s_cast, 1)
                nc.scalar.activation(resid[:, group(i)], bank[0][:], ACT.Copy).then_inc(self.x_ready, 1)

            def sp_store(self, sp, i):
                sp.wait_ge(self.z_ready, i + 1)
                sp.dma_start(out[group(i), :].rearrange("(t p) f -> p t f", p=P), z_sb[:]).then_inc(self.stored, 16)

        class Split:

            def __init__(self, part):
                self.hi_ready, self.lo_ready = sem(f"{part}_x_hi_ready"), sem(f"{part}_x_lo_ready")

            def act_hi(self, act, i):
                nc.scalar.activation(x_hi[:], resid[:, group(i)], ACT.Copy).then_inc(self.hi_ready, 1)

            def pool_lo(self, pool, i):
                pool.wait_ge(self.hi_ready, i + 1)
                pool.wait_ge(s_cast, 1)
                nc.gpsimd.tensor_tensor(x_lo[:], resid[:, group(i)], x_hi[:].bitcast(F32), ALU.subtract)\
                    .then_inc(self.lo_ready, 1)

        class Stream:

            def __init__(self, part, src, chunk):
                self.src, self.chunk = src, chunk
                self.loaded, self.hi_done, self.split = (sem(f"{part}_chunk_{n}") for n in ("loaded", "hi", "split"))

            def sp_load(self, sp, i):
                if counted(i):
                    sp.wait_ge(self.split, i)
                sp.dma_start(stage[:, 0:self.chunk], self.src[:, group(i, self.chunk)]).then_inc(self.loaded, 16)

            def pool_split(self, pool, i):
                c = self.chunk
                pool.wait_ge(s_cast, 1)
                pool.wait_ge(self.loaded, 16 * i + 16)
                nc.gpsimd.tensor_copy(ffn_hi[:, group(i, c)], stage[:, 0:c]).then_inc(self.hi_done, 1)
                pool.wait_ge(self.hi_done, i + 1)
                pool.wait_ge(s_cast, 1)
                nc.gpsimd.tensor_tensor(ffn_lo[:, group(i, c)], stage[:, 0:c], ffn_hi[:, group(i, c)].bitcast(F32),
                                        ALU.subtract).then_inc(self.split, 1)

        def three_pass(out_, w_hi, w_lo, m_hi, m_lo, start=True, stop=True):
            nc.tensor.matmul(out_, w_hi, m_hi, start=start, stop=False)
            nc.tensor.matmul(out_, w_hi, m_lo, start=False, stop=False)
            return nc.tensor.matmul(out_, w_lo, m_hi, start=False, stop=stop)

        def run(engine, first, rest):
            first(0)
            with engine.Fori(1, GROUPS) as i:
                rest(i)

        class Route:
            def __init__(self, part, e, router):
                self.e, self.router = e, router
                self.logits_ready = sem(f"{part}_logits_ready")
                self.logits_read = sem(f"{part}_logits_read")
                self.pre_exp, self.exp_done = sem(f"{part}_route_pre_exp"), sem(f"{part}_route_exp")
                self.cw_ready = sem(f"{part}_cw_ready")
                self.part_done = sem(f"{part}_cw_part")
                self.cwT_psum = sem(f"{part}_cwT_psum")
                self.cwT_ready = sem(f"{part}_cwT_ready")
                self.use(bank[1])

            def use(self, psum):
                self.logits = psum[:, 0:TILES * self.e].rearrange("p (t e) -> p t e", e=self.e)
                self.cwT_p = psum[:, GT // 2:GT].bitcast(BF16)

            def pe_logits(self, pe, i, tail, lag=0):
                if counted(i - lag):
                    pe.wait_ge(self.cwT_ready, i - lag)
                pe.wait_ge(tail.x_ready, i + 1)
                pe.wait_ge(s_cast, 1)
                for t in range(TILES):
                    last = nc.tensor.matmul(self.logits[:, t, :], xf[:, t * P:(t + 1) * P], self.router[:],
                                            start=True, stop=True)
                last.then_inc(self.logits_ready, 1)

            def pool_parts(self, pool, i):
                e = self.e
                transposed, ready = snapped(pool, i), snapped(pool, i + 1)
                pool.wait_ge(s_cast, 1)
                if counted(transposed):
                    pool.wait_ge(self.cwT_psum, transposed)
                pool.wait_ge(self.cw_ready, ready)
                src = cw[:, :, 0:e]
                for k in range(3):
                    part = cw3[:, :, k * e:(k + 1) * e]
                    nc.gpsimd.tensor_copy(part, src).then_inc(self.part_done, 1)
                    pool.wait_ge(self.part_done, 5 * i + 2 * k + 1)
                    if k < 2:
                        nc.gpsimd.tensor_tensor(rest_w[:, :, 0:e], src, part, ALU.subtract).then_inc(self.part_done, 1)
                        done = snapped(pool, 5 * i + 2 * k + 2)
                        pool.wait_ge(s_cast, 1)
                        pool.wait_ge(self.part_done, done)
                        src = rest_w[:, :, 0:e]

            def pe_transpose(self, pe, i):
                e3 = 3 * self.e
                pe.wait_ge(self.part_done, 5 * i + 5)
                for t in range(TILES):
                    last = nc.tensor.transpose(self.cwT_p[0:e3, t * P:(t + 1) * P], cw3[:, t, 0:e3], ident_bf[:])
                last.then_inc(self.cwT_psum, 1)

            def act_cwT(self, act, i):
                e3 = 3 * self.e
                act.wait_ge(self.cwT_psum, i + 1)
                act.wait_ge(s_cast, 1)
                nc.scalar.activation(cwT[0:e3, group(i)], self.cwT_p[0:e3, :], ACT.Copy).then_inc(self.cwT_ready, 1)

        class RouteTop2(Route):
            exp_step = 13

            def dve_1(self, dve, i):
                dve.wait_ge(self.logits_ready, i + 1)
                nc.vector.tensor_tensor(lg[:, :, 0:8], self.logits, bias0_sb[:].unsqueeze(1).broadcast_to([P, TILES, 8]),
                                        ALU.add).then_inc(self.logits_read, 1)
                dve.drain()
                for t in range(TILES):
                    nc.vector.max(top[:, t, :], lg[:, t, 0:8])
                dve.drain()
                for t in range(TILES):
                    nc.vector.max_index(idx[:, t, :], top[:, t, :], lg[:, t, 0:8])
                nc.vector.tensor_tensor(pair[:, 0, :], top[:, :, 1], top[:, :, 0], ALU.subtract).then_inc(self.pre_exp, 1)

            def act_exp(self, act, i):
                act.wait_ge(self.pre_exp, i + 1)
                nc.scalar.activation(pair[:, 1, :], pair[:, 0, :], ACT.Exp).then_inc(self.exp_done, 1)

            def dve_2(self, dve, i):
                dve.drain()
                if counted(5 * i):
                    dve.wait_ge(self.part_done, 5 * i)
                nc.vector.tensor_copy(idxf[:], idx[:])
                dve.drain()
                dve.wait_ge(self.exp_done, i + 1)
                nc.vector.tensor_scalar(pair[:, 2, :], pair[:, 1, :], 1.0, None, ALU.add)
                dve.drain()
                nc.vector.reciprocal(pair[:, 2, :], pair[:, 2, :])
                dve.drain()
                nc.vector.tensor_tensor(pair[:, 3, :], pair[:, 1, :], pair[:, 2, :], ALU.mult)
                io = iota8[:].unsqueeze(1).broadcast_to([P, TILES, 8])
                for k, m in ((0, gmask), (1, gsum)):
                    nc.vector.tensor_tensor(m[:], io, idxf[:, :, k:k + 1].broadcast_to([P, TILES, 8]), ALU.is_equal)
                dve.drain()
                for k, m in ((2, gmask), (3, gsum)):
                    nc.vector.tensor_tensor(m[:], m[:], pair[:, k, :].unsqueeze(2).broadcast_to([P, TILES, 8]), ALU.mult)
                dve.drain()
                nc.vector.tensor_tensor(cw[:, :, 0:8], gmask[:], gsum[:], ALU.add).then_inc(self.cw_ready, 1)

        class RouteGrouped(Route):
            exp_step = 11

            def act_exp(self, act, i):
                act.wait_ge(self.logits_ready, i + 1)
                nc.scalar.activation(lg[:], self.logits, ACT.Exp, scale=-1.0).then_inc(self.exp_done, 1)

            def dve_1(self, dve, i):
                dve.wait_ge(self.exp_done, i + 1)
                nc.vector.tensor_scalar(lg[:], lg[:], 1.0, None, ALU.add)
                dve.drain()
                nc.vector.reciprocal(sg[:], lg[:]).then_inc(self.pre_exp, 1)
                dve.drain()
                nc.vector.tensor_reduce(gsum[:], sg[:].rearrange("p t (g k) -> p t g k", k=L1_PER), AX, ALU.add)
                dve.drain()
                for t in range(TILES):
                    nc.vector.max(top[:, t, :], gsum[:, t, :])
                dve.drain()
                for t in range(TILES):
                    nc.vector.max_index(idx[:, t, :], top[:, t, :], gsum[:, t, :])
                dve.drain()
                nc.vector.tensor_copy(idxf[:], idx[:])
                dve.drain()

            def dve_2(self, dve, i):
                for t in range(TILES):
                    nc.vector.tensor_tensor(eq4[:, t, :, :], iota8[:].unsqueeze(2).broadcast_to([P, 8, 4]),
                                            idxf[:, t, 0:4].unsqueeze(1).broadcast_to([P, 8, 4]), ALU.is_equal)
                dve.drain()
                nc.vector.tensor_reduce(gmask[:], eq4[:], AX, ALU.add)
                dve.drain()
                nc.vector.tensor_tensor(sg[:].rearrange("p t (g k) -> p (t g) k", k=L1_PER),
                                        sg[:].rearrange("p t (g k) -> p (t g) k", k=L1_PER),
                                        gmask[:].rearrange("p t g -> p (t g)").unsqueeze(2)
                                        .broadcast_to([P, TILES * 8, L1_PER]), ALU.mult)
                dve.drain()
                for t in range(TILES):
                    nc.vector.max(top[:, t, :], sg[:, t, :])
                dve.drain()
                for t in range(TILES):
                    nc.vector.match_replace(lg[:, t, :], top[:, t, :], sg[:, t, :], 0.0)
                nc.vector.tensor_reduce(pair[:, 0, :], top[:], AX, ALU.add)
                dve.drain()
                nc.vector.tensor_scalar(pair[:, 0, :], pair[:, 0, :], EPS_TOPK, None, ALU.max)
                nc.vector.tensor_tensor(sg[:], sg[:], lg[:], ALU.subtract)
                dve.drain()
                nc.vector.reciprocal(pair[:, 1, :], pair[:, 0, :])
                dve.drain()
                if counted(5 * i):
                    dve.wait_ge(self.part_done, 5 * i)
                nc.vector.tensor_tensor(cw[:], sg[:], pair[:, 1, :].unsqueeze(2).broadcast_to([P, TILES, L1_E]),
                                        ALU.mult).then_inc(self.cw_ready, 1)

        def attention0():
            s = lambda n: sem(f"a0_{n}")
            route = RouteTop2("a0", L0_E, router0_sb)
            tail, split, stream = Tail("a0", route=route, on_act=True), Split("a0"), Stream("a0", w_ffn0, CH0)
            k_ready, q_ready, v_ready = s("k_ready"), s("q_ready"), s("v_ready")
            ek_ready, eq_ready = s("exp_k_ready"), s("exp_q_ready")
            sk_ready, sq_ready = s("sk_ready"), s("sq_ready")
            kv_ready, cum_ready = s("kv_ready"), s("cum_ready")
            qk_ready, qkv_ready = s("qk_ready"), s("qkv_ready")
            den_ready, neg_ready = s("den_ready"), s("neg_ready")
            rsT_ready, dlt_ready, ew_ready = s("relsum_T"), s("softmax_in"), s("softmax_exp")
            w_ready, wT_ready, wcol_ready = s("w_ready"), s("w_T"), s("wcol_ready")
            rec_ready, r_ready = s("reciprocals"), s("factors")
            bc_ready, qm_ready = s("spread_ready"), s("qm_ready")
            acc_ready, o_ready, wo_ready = s("acc_ready"), s("o_ready"), s("wo_ready")
            ORDER = [MEMS, 0, 1, 2, 3]

            def staged(engine, period):
                period(0, True, False, False, False)
                period(1, True, True, False, False)
                period(2, True, True, True, False)
                period(3, True, True, True, True)
                with engine.Fori(4, GROUPS - 1) as i:
                    period(i, True, True, True, True)
                period(GROUPS - 1, True, True, True, True)
                period(GROUPS, False, True, True, True)
                period(GROUPS + 1, False, False, True, True)

            def routed(i):
                return not isinstance(i, int) or i != GROUPS + 1


            with ExitStack() as own:
                def tb(name, shape, dt=F32):
                    return own.enter_context(nc.sbuf_tensor(f"a0_{name}", shape, dt))

                ek, eq, sq, sq4 = tb("ek", [P, GT]), tb("eq", [P, GT]), tb("sq", [P, GT]), tb("sq4", [P, GT])
                kv = tb("kv", [P, 3, GT])
                cum = tb("cum", [P, L0_D + 1, GT])
                qkv = tb("qkv", [P, 3, GT])
                qsum, rowT = tb("qsum", [P, SEQS]), tb("rowT", [SEQS, REL])
                erow, mx, wrow = tb("erow", [SEQS, REL]), tb("mx", [SEQS, L0_HEADS]), tb("wrow", [SEQS, REL])
                clip, rec, fac = tb("clip", [DEN, GT]), tb("rec", [DEN, GT]), tb("fac", [DEN, GT])
                qm = tb("qm", [P, 2, GT])
                o_sb = tb("o_sb", [P, GT])
                ring, spreadP, denP, acc = bank[2:4], bank[5:7], bank[4], bank[7]
                rsT, wT = bank[1][0:SEQS, 128:128 + REL], bank[1][0:REL, 192:192 + SEQS]
                block = own.enter_context(nc.Block())

                @block.sync
                def _(sp):
                    with sp.Fori(0, GROUPS - 1) as i:
                        sp.wait_ge(x_loaded, 16 * i + 16)
                        sp.dma_start(resid[:, bass.ds(i * GT + GT, GT)], xT[:, bass.ds(i * GT + GT, GT)])\
                            .then_inc(x_loaded, 16)
                    stream.sp_load(sp, 0)
                    with sp.Fori(1, GROUPS) as i:
                        stream.sp_load(sp, i)

                @block.tensor
                def _(pe):
                    def values(i, e):
                        if e == 0:
                            pe.wait_ge(sk_ready, i + 1)
                        elif e == 1:
                            pe.wait_ge(sq_ready, i + 1)
                        else:
                            pe.wait_ge(kv_ready, 8 * i + e - 1)
                        three_pass(ring[e % 2][:], wl0_hi[:, 2 + e, :], wl0_lo[:, 2 + e, :], x_hi[:], x_lo[:])\
                            .then_inc(v_ready, 1)

                    def spread_factor(g, o):
                        if o == 0:
                            pe.wait_ge(r_ready, g + 1)
                            if counted(5 * g):
                                pe.wait_ge(qm_ready, 5 * g)
                        elif o == 1:
                            if counted(g):
                                pe.wait_ge(tail.y_ready, g)
                        else:
                            pe.wait_ge(qm_ready, 5 * g + o - 1)
                        nc.tensor.matmul(spreadP[o % 2][:], spread[:, ORDER[o], :], fac[:], start=True, stop=True)\
                            .then_inc(bc_ready, 1)

                    def memory(g, m):
                        if m == 0:
                            if counted(g):
                                pe.wait_ge(o_ready, g)
                        pe.wait_ge(qm_ready, 5 * g + m + 2)
                        nc.tensor.matmul(acc[:], mem_sb[:, m, :], qm[:, m % 2, :], start=(m == 0), stop=False)\
                            .then_inc(acc_ready, 1)

                    def local(g, e):
                        pe.wait_ge(qkv_ready, 8 * g + e + 1)
                        nc.tensor.matmul(acc[:], blocksum[:, e, :], qkv[:, e % 2, :], start=False, stop=(e == L0_D - 1))\
                            .then_inc(acc_ready, 1)

                    def keys_and_queries(i):
                        pe.wait_ge(split.hi_ready, i + 1)
                        if counted(8 * i - 1):
                            pe.wait_ge(kv_ready, 8 * i - 1)
                        nc.tensor.matmul(ring[0][:], wl0_hi[:, 1, :], x_hi[:], start=True, stop=False)
                        nc.tensor.matmul(ring[0][:], wl0_lo[:, 1, :], x_hi[:], start=False, stop=False)
                        pe.wait_ge(split.lo_ready, i + 1)
                        nc.tensor.matmul(ring[0][:], wl0_hi[:, 1, :], x_lo[:], start=False, stop=True).then_inc(k_ready, 1)
                        if counted(8 * i):
                            pe.wait_ge(kv_ready, 8 * i)
                        three_pass(ring[1][:], wl0_hi[:, 0, :], wl0_lo[:, 0, :], x_hi[:], x_lo[:]).then_inc(q_ready, 1)

                    def period(i, A, B, C, D):
                        g, c, d = i - 1, i - 2, i - 3
                        if B:
                            spread_factor(g, 0)
                        if C and routed(i):
                            tail.pe_tokens(pe, c)
                        if B:
                            spread_factor(g, 1)
                        if A:
                            values(i, 0)
                        if B:
                            spread_factor(g, 2)
                            memory(g, 0)
                            spread_factor(g, 3)
                            memory(g, 1)
                            spread_factor(g, 4)
                            memory(g, 2)
                            memory(g, 3)
                        if A:
                            values(i, 1)
                        for e in range(L0_D):
                            if A and 1 <= e < L0_D - 1:
                                values(i, e + 1)
                            if C and e == 2 and routed(i):
                                tail.pe_features(pe, c)
                            if A and e == 1:
                                if counted(i):
                                    pe.wait_ge(rec_ready, 4 * i)
                                nc.tensor.matmul(denP[0:REL, :], norms_sb[:], sq[:], start=True, stop=True)
                                if counted(i - 3):
                                    pe.wait_ge(route.cwT_ready, i - 3)
                                nc.tensor.matmul(rsT, qsum[:], norms_sb[:], start=True, stop=True).then_inc(rsT_ready, 1)
                            if B:
                                local(g, e)
                            if A and e == 3:
                                pe.wait_ge(qk_ready, i + 1)
                                nc.tensor.matmul(denP[REL:DEN, :], headsum[:], qkv[:, 2, :], start=True, stop=True)\
                                    .then_inc(den_ready, 1)
                            if A and e == 4:
                                pe.wait_ge(s_cast, 1)
                                pe.wait_ge(w_ready, i + 1)
                                nc.tensor.transpose(wT, wrow[:], ident[0:SEQS, 0:SEQS]).then_inc(wT_ready, 1)
                            if C and e == 6 and routed(i):
                                if A:
                                    pe.wait_ge(wcol_ready, i + 1)
                                route.pe_logits(pe, c, tail, lag=1)
                        if A and not (isinstance(i, int) and i == GROUPS - 1):
                            keys_and_queries(i + 1)
                        if B:
                            pe.wait_ge(o_ready, g + 1)
                            nc.tensor.matmul(spreadP[1][:], wo0[:], o_sb[:], start=True, stop=True).then_inc(wo_ready, 1)
                        if D:
                            if routed(i):
                                pe.wait_ge(route.logits_read, c + 1)
                            else:
                                pe.wait_ge(route.cwT_ready, d)
                            route.pe_transpose(pe, d)

                    keys_and_queries(0)
                    staged(pe, period)

                @block.scalar
                def _(act):
                    def prepare(i):
                        act.wait_ge(x_loaded, 16 * i + 16)
                        if counted(8 * i):
                            act.wait_ge(v_ready, 8 * i)
                        act.wait_ge(s_cast, 1)
                        split.act_hi(act, i)

                    def exp_k(i):
                        act.wait_ge(k_ready, i + 1)
                        nc.scalar.activation(ek[:], ring[0][:], ACT.Relu, scale=-1.0).then_inc(neg_ready, 1)
                        act.wait_ge(neg_ready, 2 * i + 1)
                        nc.scalar.activation(ek[:], ek[:], ACT.Exp, scale=-1.0).then_inc(ek_ready, 1)

                    def period(i, A, B, C, D):
                        g, c, d = i - 1, i - 2, i - 3
                        if A:
                            act.wait_ge(q_ready, i + 1)
                            nc.scalar.activation(eq[:], ring[1][:], ACT.Relu, scale=-1.0).then_inc(neg_ready, 1)
                            act.wait_ge(neg_ready, 2 * i + 2)
                            nc.scalar.activation(eq[:], eq[:], ACT.Exp, scale=-1.0).then_inc(eq_ready, 1)
                        if C and routed(i):
                            tail.act_normalise(act, c)
                            tail.act_resid(act, c)
                        if A:
                            act.wait_ge(dlt_ready, i + 1)
                            nc.scalar.activation(erow[:], rowT[:], ACT.Exp, scale=1.0 / SEQ).then_inc(ew_ready, 1)
                        if A and not (isinstance(i, int) and i == GROUPS - 1):
                            prepare(i + 1)
                        if B:
                            if counted(g):
                                act.wait_ge(wo_ready, g)
                            act.wait_ge(acc_ready, 12 * g + 12)
                            nc.scalar.activation(o_sb[:], acc[:], ACT.Copy).then_inc(o_ready, 1)
                        if A:
                            if counted(5 * i):
                                act.wait_ge(bc_ready, 5 * i)
                            act.wait_ge(wcol_ready, i + 1)
                            act.wait_ge(rec_ready, 4 * i + 4)
                            for q in range(SEQS):
                                cols = slice(q * SEQ, (q + 1) * SEQ)
                                last = nc.scalar.activation(fac[:, cols], rec[:, cols], ACT.Copy, scale=wcol[:, q:q + 1])
                            last.then_inc(r_ready, 1)
                        if A and not (isinstance(i, int) and i == GROUPS - 1):
                            exp_k(i + 1)
                        if C and routed(i):
                            route.act_exp(act, c)
                        if D:
                            route.act_cwT(act, d)

                    prepare(0)
                    exp_k(0)
                    staged(act, period)

                @block.vector
                def _(dve):
                    def elu(i, e_ready, e_sb, src, dst, done):
                        dve.wait_ge(e_ready, i + 1)
                        if done is sk_ready:
                            if counted(9 * i):
                                dve.wait_ge(cum_ready, 9 * i)
                        else:
                            if counted(i):
                                dve.wait_ge(qk_ready, i)
                        if done is sk_ready:
                            nc.vector.scalar_tensor_tensor(out=dst, in0=src[:], scalar=0.0, in1=e_sb[:], op0=ALU.max,
                                                           op1=ALU.add).then_inc(done, 1)
                        else:
                            for n in range(SEQS):
                                cols = slice(n * SEQ, (n + 1) * SEQ)
                                last = nc.vector.scalar_tensor_tensor(
                                    out=sq[:, cols], in0=src[:, cols], scalar=0.0, in1=e_sb[:, cols], op0=ALU.max,
                                    op1=ALU.add, accum_out=qsum[:, n:n + 1])
                            last.then_inc(done, 1)

                    def product(i, e):
                        if counted(v := 9 * i + e if e >= 2 else 9 * (i - 1) + 8 + e):
                            dve.wait_ge(cum_ready, v)
                        dve.wait_ge(v_ready, 8 * i + e + 1)
                        nc.vector.tensor_tensor(kv[:, e % 2, :], ring[e % 2][:], kv[:, 2, :], ALU.mult).then_inc(kv_ready, 1)

                    def running(i, e):
                        if counted(8 * (i - 1) + e + 1):
                            dve.wait_ge(qkv_ready, 8 * (i - 1) + e + 1)
                        dve.wait_ge(kv_ready, 8 * i + e + 1)
                        nc.vector.tensor_tensor_scan(cum[:, e, :], reset[:], kv[:, e % 2, :], 0.0, ALU.mult, ALU.add)\
                            .then_inc(cum_ready, 1)

                    def scaled_q(g, o):
                        if o == 0:
                            if counted(8 * g):
                                dve.wait_ge(qkv_ready, 8 * g)
                        else:
                            if counted(v := 12 * g + o - 2 if o >= 3 else 12 * (g - 1) + 2 + o):
                                dve.wait_ge(acc_ready, v)
                        dve.wait_ge(bc_ready, 5 * g + o + 1)
                        nc.vector.tensor_tensor(sq4[:] if o == 0 else qm[:, (o - 1) % 2, :], spreadP[o % 2][:], sq[:],
                                                ALU.mult).then_inc(qm_ready, 1)

                    def softmax_in(i):
                        dve.wait_ge(rsT_ready, i + 1)
                        nc.vector.tensor_reduce(mx[:], rsT.rearrange("p (m h) -> p h m", m=MEMS), AX, ALU.max)
                        dve.drain()
                        nc.vector.tensor_tensor(rowT[:].rearrange("p (m h) -> p m h", m=MEMS),
                                                rsT.rearrange("p (m h) -> p m h", m=MEMS),
                                                mx[:].unsqueeze(1).broadcast_to([SEQS, MEMS, L0_HEADS]),
                                                ALU.subtract).then_inc(dlt_ready, 1)

                    def softmax_out(i):
                        dve.wait_ge(ew_ready, i + 1)
                        nc.vector.tensor_reduce(mx[:], erow[:].rearrange("p (m h) -> p h m", m=MEMS), AX, ALU.add)
                        dve.drain()
                        nc.vector.reciprocal(mx[:], mx[:])
                        dve.drain()
                        nc.vector.tensor_tensor(mx[:], mx[:], gate_row[:], ALU.mult)
                        dve.drain()
                        nc.vector.tensor_tensor(wrow[:].rearrange("p (m h) -> p m h", m=MEMS),
                                                erow[:].rearrange("p (m h) -> p m h", m=MEMS),
                                                mx[:].unsqueeze(1).broadcast_to([SEQS, MEMS, L0_HEADS]),
                                                ALU.mult).then_inc(w_ready, 1)

                    def period(i, A, B, C, D):
                        g, c, d = i - 1, i - 2, i - 3
                        if C:
                            if counted(c):
                                dve.wait_ge(tail.tok_ready, c)
                            dve.wait_ge(wo_ready, c + 1)
                            nc.vector.tensor_tensor(y_sb[:], spreadP[1][:], resid[:, group(c)], ALU.add)\
                                .then_inc(tail.y_ready, 1)
                        if A:
                            elu(i, ek_ready, ek, ring[0], kv[:, 2, :], sk_ready)
                        if B:
                            scaled_q(g, 0)
                        if D:
                            route.dve_2(dve, d)
                        if B:
                            scaled_q(g, 1)
                        if A:
                            if counted(i):
                                dve.wait_ge(qk_ready, i)
                            dve.wait_ge(sk_ready, i + 1)
                            nc.vector.tensor_tensor_scan(cum[:, L0_D, :], reset[:], kv[:, 2, :], 0.0, ALU.mult, ALU.add)\
                                .then_inc(cum_ready, 1)
                        if B:
                            scaled_q(g, 2)
                        if C and routed(i):
                            tail.dve_stats(dve, c)
                        if B:
                            scaled_q(g, 3)
                        if A:
                            product(i, 0)
                        if B:
                            scaled_q(g, 4)
                        if A:
                            if counted(5 * i):
                                dve.wait_ge(qm_ready, 5 * i)
                            elu(i, eq_ready, eq, ring[1], sq[:], sq_ready)
                        for e in range(1, L0_D):
                            if A:
                                product(i, e)
                            if A and e == 5:
                                dve.wait_ge(wT_ready, i + 1)
                                nc.vector.tensor_copy(wcol[0:REL, :], wT).then_inc(wcol_ready, 1)
                            if A:
                                running(i, e - 1)
                            if A and e == 2:
                                softmax_in(i)
                            if A and e == 3:
                                softmax_out(i)
                            if A and e == 4:
                                if counted(i):
                                    dve.wait_ge(rec_ready, 4 * i)
                                dve.wait_ge(den_ready, i + 1)
                                nc.vector.tensor_scalar(clip[:], denP[0:DEN, :], EPS_DEN, None, ALU.max)
                                dve.drain()
                                if counted(i):
                                    dve.wait_ge(r_ready, i)
                            if A and e >= 4:
                                cols = slice((e - 4) * P, (e - 3) * P)
                                nc.vector.reciprocal(rec[:, cols], clip[:, cols]).then_inc(rec_ready, 1)
                        if A:
                            running(i, L0_D - 1)
                        if C and routed(i):
                            route.dve_1(dve, c)

                    staged(dve, period)

                @block.gpsimd
                def _(pool):
                    def period(i, A, B, C, D):
                        g, c, d = i - 1, i - 2, i - 3
                        if B:
                            pool.wait_ge(qm_ready, 5 * g + 1)
                        for e in range(L0_D):
                            if B:
                                if counted(v := 12 * g + 4 + e - 1 if e >= 2 else 12 * (g - 1) + 11 + e):
                                    pool.wait_ge(acc_ready, v)
                                pool.wait_ge(cum_ready, 9 * g + e + 2)
                                nc.gpsimd.tensor_tensor(qkv[:, e % 2, :], cum[:, e, :], sq4[:], ALU.mult)\
                                    .then_inc(qkv_ready, 1)
                            if C and e == 1 and routed(i):
                                tail.pool_rstd(pool, c)
                            if D and e == 2:
                                route.pool_parts(pool, d)
                            if A and e == 1:
                                if counted(i):
                                    pool.wait_ge(den_ready, i)
                                pool.wait_ge(sq_ready, i + 1)
                                pool.wait_ge(cum_ready, 9 * i + 1)
                                nc.gpsimd.tensor_tensor(qkv[:, 2, :], cum[:, L0_D, :], sq[:], ALU.mult).then_inc(qk_ready, 1)
                        if A:
                            if not (isinstance(i, int) and i == GROUPS - 1):
                                split.pool_lo(pool, i + 1)
                            stream.pool_split(pool, i)

                    split.pool_lo(pool, 0)
                    staged(pool, period)
            return route, tail

        def attention1(before):
            s = lambda n: sem(f"a1_{n}")
            route = RouteGrouped("a1", L1_E, router1_sb)
            tail, split, stream = Tail("a1", route=route), Split("a1"), Stream("a1", w_ffn1, CH1)
            H, U = L1_HEADS, L1_HEADS * SEQS
            kp_ready, vp_ready, qp_ready = s("k_psum"), s("v_psum"), s("q_psum")
            k_ready, v_ready, q_ready = s("k_ready"), s("v_ready"), s("q_ready")
            sc_ready, nm_ready = s("scores_ready"), s("masked_ready")
            e_ready, r_ready, p_ready = s("exp_ready"), s("recip_ready"), s("probs_ready")
            tr_ready, pt_ready = s("probsT_psum"), s("probsT_ready")
            pv_ready, at_ready, acc_ready = s("pv_ready"), s("attn_ready"), s("acc_ready")

            with ExitStack() as own:
                def tb(name, shape, dt=F32):
                    return own.enter_context(nc.sbuf_tensor(f"a1_{name}", shape, dt))

                kT, vt, qT = tb("kT", [P, GT]), tb("vt", [P, TILES, P]), tb("qT", [P, 2, GT])
                SC = 3 * P
                ms, ex, pn = tb("ms", [P, 4, SC]), tb("ex", [P, 4, SC]), tb("pn", [P, 4, SC])
                mx, nm, rs, rr = (tb(n, [P, 4, 2]) for n in ("mx", "nm", "rs", "rr"))
                pT = tb("pT", [P, 2, SEQS, SC])
                at = tb("at", [P, H, GT])
                ring, scP, trP, pvP = bank[2:4], bank[4:6], bank[6], bank[7]
                block = own.enter_context(nc.Block())

                @block.sync
                def _(sp):
                    stream.sp_load(sp, 0)
                    with sp.Fori(1, GROUPS) as i:
                        stream.sp_load(sp, i)

                def after(i, groups):
                    return not isinstance(i, int) or i >= groups

                def works(i, live, m):
                    return live if m >= 0 else after(i, 1)

                def has_next(i):
                    return not isinstance(i, int) or i < GROUPS - 1

                def stream_groups(engine, body):
                    for i in range(3):
                        body(i, True)
                    with engine.Fori(3, GROUPS - 1) as i:
                        body(i, True)
                    body(GROUPS - 1, True)
                    body(GROUPS, False)

                def q_bank(h):
                    return ring[(1 + h) % 2 if h < 4 else h % 2]

                @block.tensor
                def _(pe):
                    def project_k(i):
                        pe.wait_ge(split.lo_ready, i + 1)
                        if counted(H * i - 1):
                            pe.wait_ge(q_ready, H * i - 1)
                        three_pass(ring[0][:], wl1_hi[:, H, :], wl1_lo[:, H, :], x_hi[:], x_lo[:]).then_inc(kp_ready, 1)

                    def project_v(i):
                        pe.wait_ge(q_ready, H * i + 3)
                        for t in range(TILES):
                            c = slice(t * P, (t + 1) * P)
                            last = three_pass(ring[1][:, c], x_hi[:, c], x_lo[:, c], wl1_hi[:, H + 1, :],
                                              wl1_lo[:, H + 1, :])
                        last.then_inc(vp_ready, 1)

                    def project_q(i, h):
                        if h == 1:
                            pe.wait_ge(k_ready, i + 1)
                        elif h == 5:
                            pe.wait_ge(v_ready, i + 1)
                        else:
                            before = {0: -1, 2: 0, 3: 1, 4: 3, 6: 4, 7: 5}[h]
                            if counted(H * i + before + 1):
                                pe.wait_ge(q_ready, H * i + before + 1)
                        three_pass(q_bank(h)[:], wl1_hi[:, h, :], wl1_lo[:, h, :], x_hi[:], x_lo[:])\
                            .then_inc(qp_ready, 1)

                    def scores(i, h, q):
                        u = SEQS * h + q
                        if q == 0:
                            pe.wait_ge(q_ready, H * i + h + 1)
                        if counted(U * i + u - 1):
                            pe.wait_ge(nm_ready, U * i + u - 1)
                        o = q * SEQ
                        nc.tensor.matmul(scP[u % 2][:, 0:P], qT[:, h % 2, o:o + P], kT[:, o:o + P],
                                         start=True, stop=True)
                        nc.tensor.matmul(scP[u % 2][:, P:SC], qT[:, h % 2, o + P:o + SEQ], kT[:, o:o + SEQ],
                                         start=True, stop=True).then_inc(sc_ready, 1)

                    def transpose_probs(i, h, q):
                        u = SEQS * h + q
                        if counted(U * i + u):
                            pe.wait_ge(pt_ready, U * i + u)
                        pe.wait_ge(p_ready, U * i + u + 1)
                        for b in range(3):
                            cols = slice(b * P, (b + 1) * P)
                            last = nc.tensor.transpose(trP[:, cols], pn[:, u % 4, cols], ident[:])
                        last.then_inc(tr_ready, 1)

                    def values(i, h, q):
                        if h == 0 and q == 0:
                            pe.wait_ge(v_ready, i + 1)
                        if q == 0:
                            if counted(H * i + h):
                                pe.wait_ge(at_ready, H * i + h)
                            pe.wait_ge(pt_ready, U * i + SEQS * h + SEQS)
                        nc.tensor.matmul(pvP[:, q * SEQ:(q + 1) * SEQ], vt[:, 2 * q, :],
                                         pT[:, h % 2, q, 0:SEQ], start=True, stop=False)
                        last = nc.tensor.matmul(pvP[:, q * SEQ + P:(q + 1) * SEQ], vt[:, 2 * q + 1, :],
                                                pT[:, h % 2, q, SEQ:SC], start=False, stop=True)
                        if q == SEQS - 1:
                            last.then_inc(pv_ready, 1)

                    def output(i, heads):
                        for h in heads:
                            if h == 0 and counted(i):
                                pe.wait_ge(tail.x_ready, i)
                            pe.wait_ge(at_ready, H * i + h + 1)
                            last = nc.tensor.matmul(bank[0][:], wo1[:, h, :], at[:, h, :], start=(h == 0),
                                                    stop=(h == H - 1))
                        return last

                    def body(i, live):
                        for h in range(H):
                            if live and h + 1 < H:
                                project_q(i, h + 1)
                            if h == 1 and not after(i, 1):
                                before.pe_tokens(pe, GROUPS - 1)
                            if h == 4 and not after(i, 1):
                                before.pe_features(pe, GROUPS - 1)
                            if h == 4 and after(i, 1) and live:
                                tail.pe_tokens(pe, i - 1)
                            if live:
                                scores(i, h, 0)
                            if works(i, live, h - 2):
                                transpose_probs(i, h - 2, 0)
                            if h == 3 and after(i, 1):
                                output(i - 1, (7,)).then_inc(acc_ready, 1)
                            if live:
                                scores(i, h, 1)
                            if h == 6 and after(i, 1) and live:
                                tail.pe_features(pe, i - 1)
                            if works(i, live, h - 3):
                                values(i, h - 3, 0)
                            if h < 3 and after(i, 1):
                                output(i - 1, ((0, 1, 2, 3), (4, 5), (6,))[h])
                            if works(i, live, h - 2):
                                transpose_probs(i, h - 2, 1)
                            if works(i, live, h - 3):
                                values(i, h - 3, 1)
                            if live and h == 2:
                                project_v(i)
                            if h == 5 and after(i, 2):
                                route.pe_transpose(pe, i - 2)
                            if h == 7 and after(i, 1) and live:
                                route.pe_logits(pe, i - 1, tail)
                        if live and has_next(i):
                            project_k(i + 1)
                            project_q(i + 1, 0)

                    project_k(0)
                    project_q(0, 0)
                    stream_groups(pe, body)

                @block.scalar
                def _(act):
                    def exponent(i, h, q):
                        u = SEQS * h + q
                        if counted(U * i + u - 3):
                            act.wait_ge(p_ready, U * i + u - 3)
                        act.wait_ge(nm_ready, U * i + u + 1)
                        for b, c in enumerate((slice(0, P), slice(P, SC))):
                            last = nc.scalar.activation(ex[:, u % 4, c], ms[:, u % 4, c], ACT.Exp, scale=SCALE,
                                                        bias=nm[:, u % 4, b:b + 1], accum_out=rs[:, u % 4, b:b + 1])
                        last.then_inc(e_ready, 1)

                    def store_transposed(i, h, q):
                        u = SEQS * h + q
                        if counted(H * i + h - 1):
                            act.wait_ge(pv_ready, H * i + h - 1)
                        act.wait_ge(tr_ready, U * i + u + 1)
                        nc.scalar.activation(pT[:, h % 2, q, :], trP[:, 0:SC], ACT.Copy).then_inc(pt_ready, 1)

                    def store_values(i, h):
                        if h == 0 and counted(i):
                            act.wait_ge(acc_ready, i)
                        act.wait_ge(pv_ready, H * i + h + 1)
                        nc.scalar.activation(at[:, h % H, :], pvP[:], ACT.Copy).then_inc(at_ready, 1)

                    def body(i, live):
                        for h in range(H):
                            if works(i, live, h - 2):
                                store_transposed(i, h - 2, 0)
                            if live:
                                exponent(i, h, 0)
                            if h == 0 and after(i, 2):
                                route.act_exp(act, i - 2)
                            if h == 6 and after(i, 2):
                                route.act_cwT(act, i - 2)
                            if h == 5 and not after(i, 1):
                                before.act_resid(act, GROUPS - 1)
                            if h == 7 and after(i, 1) and live:
                                tail.act_resid(act, i - 1)
                            if live:
                                exponent(i, h, 1)
                            if works(i, live, h - 2):
                                store_transposed(i, h - 2, 1)
                            if works(i, live, h - 3):
                                store_values(i, h - 3)
                            if h == 6 and live and has_next(i):
                                act.wait_ge(qp_ready, H * i + H)
                                act.wait_ge(s_cast, 1)
                                split.act_hi(act, i + 1)

                    split.act_hi(act, 0)
                    stream_groups(act, body)

                @block.vector
                def _(dve):
                    def evacuate_k(i):
                        if counted(U * i):
                            dve.wait_ge(sc_ready, U * i)
                        dve.wait_ge(kp_ready, i + 1)
                        nc.vector.scalar_tensor_tensor(out=kT[:], in0=ring[0][:], scalar=b_sb[:, H:H + 1], in1=pe_sb[:],
                                                       op0=ALU.add, op1=ALU.add).then_inc(k_ready, 1)

                    def evacuate_v(i):
                        if counted(H * i):
                            dve.wait_ge(pv_ready, H * i)
                        dve.wait_ge(vp_ready, i + 1)
                        nc.vector.tensor_tensor(vt[:], ring[1][:].rearrange("p (t n) -> p t n", t=TILES),
                                                bv_sb[:].unsqueeze(1).broadcast_to([P, TILES, P]), ALU.add)\
                            .then_inc(v_ready, 1)

                    def evacuate_q(i, h):
                        if counted(U * i + SEQS * (h - 1)):
                            dve.wait_ge(sc_ready, U * i + SEQS * (h - 1))
                        dve.wait_ge(qp_ready, H * i + h + 1)
                        nc.vector.scalar_tensor_tensor(out=qT[:, h % 2, :], in0=q_bank(h)[:], scalar=b_sb[:, h:h + 1],
                                                       in1=pe_sb[:], op0=ALU.add, op1=ALU.add).then_inc(q_ready, 1)

                    def mask_and_max(i, h, q):
                        u = SEQS * h + q
                        read, scored = snapped(dve, U * i + u - 3), snapped(dve, U * i + u + 1)
                        dve.wait_ge(s_cast, 1)
                        if counted(read):
                            dve.wait_ge(e_ready, read)
                        dve.wait_ge(sc_ready, scored)
                        nc.vector.tensor_tensor_reduce(out=ms[:, u % 4, 0:P], in0=scP[u % 2][:, 0:P], in1=tri[:, 1, :],
                                                       scale=1.0, scalar=MASKED, op0=ALU.add, op1=ALU.max,
                                                       accum_out=mx[:, u % 4, 0:1])
                        nc.vector.tensor_tensor_reduce(out=ms[:, u % 4, P:SC], in0=scP[u % 2][:, P:SC],
                                                       in1=tri[:].rearrange("p a b -> p (a b)"),
                                                       scale=1.0, scalar=MASKED, op0=ALU.add, op1=ALU.max,
                                                       accum_out=mx[:, u % 4, 1:2])
                        dve.drain()
                        nc.vector.tensor_scalar(nm[:, u % 4, :], mx[:, u % 4, :], -SCALE, None, ALU.mult)\
                            .then_inc(nm_ready, 1)

                    def reciprocals(i, h):
                        for u in range(SEQS * h, SEQS * h + SEQS):
                            dve.wait_ge(e_ready, U * i + u + 1)
                            nc.vector.reciprocal(rr[:, u % 4, :], rs[:, u % 4, :]).then_inc(r_ready, 1)

                    def residual(i):
                        if counted(i):
                            dve.wait_ge(tail.tok_ready, i)
                        dve.wait_ge(acc_ready, i + 1)
                        nc.vector.tensor_tensor(y_sb[:], bank[0][:], resid[:, group(i)], ALU.add).then_inc(tail.y_ready, 1)

                    def body(i, live):
                        for h in range(H):
                            if live and h == 3:
                                evacuate_v(i)
                            if live and h + 1 < H:
                                evacuate_q(i, h + 1)
                            if works(i, live, h - 1):
                                reciprocals(i, h - 1)
                            if live:
                                mask_and_max(i, h, 0)
                            if h == 1 and not after(i, 1):
                                before.dve_stats(dve, GROUPS - 1)
                            if h == 3 and not after(i, 1):
                                before.dve_normalise(dve, GROUPS - 1)
                            if h == 4 and after(i, 1) and live:
                                tail.dve_stats(dve, i - 1)
                            if h == 5 and after(i, 1) and live:
                                tail.dve_normalise(dve, i - 1, range(0, 2))
                            if live:
                                mask_and_max(i, h, 1)
                            if h == 0 and after(i, 2):
                                route.dve_1(dve, i - 2)
                            if h == 1 and after(i, 2):
                                route.dve_2(dve, i - 2)
                            if h == 3 and after(i, 1):
                                residual(i - 1)
                            if h == 5 and after(i, 1) and live:
                                tail.dve_normalise(dve, i - 1, range(2, 4))
                        if live and has_next(i):
                            evacuate_k(i + 1)
                            evacuate_q(i + 1, 0)

                    evacuate_k(0)
                    evacuate_q(0, 0)
                    stream_groups(dve, body)

                @block.gpsimd
                def _(pool):
                    def normalise_probs(i, h):
                        for u in range(SEQS * h, SEQS * h + SEQS):
                            if counted(U * i + u - 3):
                                pool.wait_ge(tr_ready, U * i + u - 3)
                            pool.wait_ge(r_ready, U * i + u + 1)
                            nc.gpsimd.tensor_tensor(pn[:, u % 4, 0:P], ex[:, u % 4, 0:P],
                                                    rr[:, u % 4, 0:1].broadcast_to([P, P]), ALU.mult)
                            nc.gpsimd.tensor_tensor(pn[:, u % 4, P:SC], ex[:, u % 4, P:SC],
                                                    rr[:, u % 4, 1:2].broadcast_to([P, SC - P]), ALU.mult)\
                                .then_inc(p_ready, 1)

                    def body(i, live):
                        for h in range(H):
                            if works(i, live, h - 1):
                                normalise_probs(i, h - 1)
                            if h == 2 and not after(i, 1):
                                before.pool_rstd(pool, GROUPS - 1)
                            if h == 4 and after(i, 1) and live:
                                tail.pool_rstd(pool, i - 1)
                            if h == 7 and live and has_next(i):
                                split.pool_lo(pool, i + 1)
                            if h == 3 and after(i, 2):
                                route.pool_parts(pool, i - 2)
                            if h == 1 and live:
                                stream.pool_split(pool, i)

                    split.pool_lo(pool, 0)
                    stream_groups(pool, body)
            return route, tail

        class LaterWeights:

            def __init__(self, raw):
                self.raw = raw
                self.loaded, self.hi = sem("l1_loaded"), sem("l1_hi")
                self.chunk = 10 * P // L0_TILES + 1

            def columns(self, t):
                return slice(t * self.chunk, min((t + 1) * self.chunk, 10 * P))

            def sp_load(self, sp):
                sp.dma_start(self.raw[:, 0:10 * P].rearrange("p (a b) -> p a b", a=10), w_l1).then_inc(self.loaded, 16)
                sp.dma_start(wo1[:], wo_l1).then_inc(self.loaded, 16)
                sp.dma_start(b_sb[:], b_l1).then_inc(self.loaded, 16)
                sp.dma_start(bv_sb[:], bv_l1.partition_broadcast(P)).then_inc(self.loaded, 16)
                sp.dma_start(pe_sb[:], peT).then_inc(self.loaded, 16)
                sp.dma_start(tri[:], c_tri).then_inc(self.loaded, 16)

            def act_hi(self, act, t):
                act.wait_ge(self.loaded, 96)
                c = self.columns(t)
                nc.scalar.activation(w1_hi[:, c], self.raw[:, c], ACT.Copy).then_inc(self.hi, 1)

            def dve_lo(self, dve, t):
                c = self.columns(t)
                dve.wait_ge(self.hi, t + 1)
                nc.vector.tensor_tensor(w1_lo[:, c], self.raw[:, c], w1_hi[:, c].bitcast(F32), ALU.subtract)

        def experts(part, NT, routed, per_weight, sel, e3, last, pending, later=None):
            s = lambda n: sem(f"{part}_{n}")
            tail, split = Tail(part, last=last), Split(part)
            route, before = pending
            route.use(bank[0])
            NB = routed // per_weight
            gu_ready, bc_ready = s("gate_up_ready"), s("weight_psum")
            s_ready, bw_ready = s("silu_ready"), s("weight_ready")
            w_ready = s("weighted_ready")
            h_ready, hhi_ready, hlo_ready = s("h_ready"), s("h_hi_ready"), s("h_lo_ready")
            down_ready = s("down_done")
            LAG, RING = 3, 4
            GATE, UP, DOWN = 0, NT * P, 2 * NT * P

            def w(which, base, t):
                return which[:, base + t * P:base + (t + 1) * P]

            def number(slot, t):
                return slot * NT + t

            def pairs(engine, body, peel_last=False):
                body(0, 0)
                body(0, 1)
                end = GROUPS // 2 - 1 if peel_last else GROUPS // 2
                with engine.Fori(1, end) as j:
                    body(j, 0)
                    body(j, 1)
                if peel_last:
                    body(end, 0)
                    body(end, 1)

            with ExitStack() as own:
                def tb(name, shape, dt=F32):
                    return own.enter_context(nc.sbuf_tensor(f"{part}_{name}", shape, dt))

                xh, xl = tb("xh", [P, 2, GT], F32R), tb("xl", [P, 2, GT], F32R)
                sl, sw, bw = tb("sl", [P, 2, GT]), tb("sw", [P, 2, GT]), tb("bw", [P, 2, GT])
                hh, h_hi, h_lo = tb("hh", [P, 2, GT]), tb("h_hi", [P, RING, GT], F32R), tb("h_lo", [P, RING, GT], F32R)
                bcP, gP, uP, acc = bank[1], bank[2:4], bank[4:6], bank[6]
                block = own.enter_context(nc.Block())

                if later:
                    @block.sync
                    def _(sp):
                        later.sp_load(sp)

                if last:
                    @block.sync
                    def _(sp):
                        def body(i):
                            tail.sp_store(sp, i)
                        run(sp, body, body)
                        sp.wait_ge(tail.stored, 16 * GROUPS)

                @block.tensor
                def _(pe):
                    def down(j, slot, t):
                        i, r = 2 * j + slot, number(slot, t) % RING
                        if t == 0 and counted(i):
                            pe.wait_ge(tail.y_ready, i)
                        pe.wait_ge(hlo_ready, NT * i + t + 1)
                        three_pass(acc[:], w(ffn_hi, DOWN, t), w(ffn_lo, DOWN, t), h_hi[:, r, :], h_lo[:, r, :],
                                   start=(t == 0), stop=(t == NT - 1)).then_inc(down_ready, 1)

                    def body(j, slot):
                        i = 2 * j + slot
                        first, second = (isinstance(i, int) and i == n for n in (0, 1))
                        pe.wait_ge(split.lo_ready, i + 1)
                        for t in range(NT):
                            r = number(slot, t) % 2
                            if t < routed and t % per_weight == 0:
                                b = t // per_weight
                                read = snapped(pe, NB * i + b)
                                pe.wait_ge(s_cast, 1)
                                if counted(read):
                                    pe.wait_ge(bw_ready, read)
                                nc.tensor.matmul(bcP[:], sel[:, b, :], cwT[0:e3, group(i)], start=True, stop=True)\
                                    .then_inc(bc_ready, 1)
                            if counted(NT * i + t - 1):
                                pe.wait_ge(s_ready, NT * i + t - 1)
                            three_pass(gP[r][:], w(ffn_hi, GATE, t), w(ffn_lo, GATE, t), xh[:, slot, :], xl[:, slot, :])
                            if counted(NT * i + t - 1):
                                pe.wait_ge(h_ready, NT * i + t - 1)
                            three_pass(uP[r][:], w(ffn_hi, UP, t), w(ffn_lo, UP, t), xh[:, slot, :], xl[:, slot, :])\
                                .then_inc(gu_ready, 1)
                            if t >= LAG:
                                down(j, slot, t - LAG)
                            elif not first:
                                down(j if slot else j - 1, 1 - slot, NT + t - LAG)
                            if first and t == 1:
                                before.pe_tokens(pe, GROUPS - 1)
                            if first and t == 7:
                                before.pe_features(pe, GROUPS - 1)
                            if first and t == 10:
                                route.pe_logits(pe, GROUPS - 1, before)
                            if second and t == 1:
                                route.pe_transpose(pe, GROUPS - 1)
                            if second and t == 4:
                                pe.wait_ge(route.cwT_ready, GROUPS)
                            if not first and t == 4:
                                tail.pe_tokens(pe, i - 1)
                            if not first and t == 10:
                                tail.pe_features(pe, i - 1)

                    pairs(pe, body)
                    for t in range(NT - LAG, NT):
                        down(GROUPS // 2 - 1, 1, t)
                    if last:
                        tail.pe_tokens(pe, GROUPS - 1)

                @block.scalar
                def _(act):
                    def prepare(i, slot):
                        if counted(NT * (i - 1)):
                            act.wait_ge(gu_ready, NT * (i - 1))
                        act.wait_ge(s_cast, 1)
                        nc.scalar.activation(xh[:, slot, :], resid[:, group(i)], ACT.Copy).then_inc(split.hi_ready, 1)

                    def high(j, slot, t):
                        n = number(slot, t)
                        if counted(v := last_use(j, n, 2 * NT, RING)):
                            act.wait_ge(down_ready, v)
                        act.wait_ge(h_ready, NT * (2 * j + slot) + t + 1)
                        nc.scalar.activation(h_hi[:, n % RING, :], hh[:, n % 2, :], ACT.Copy).then_inc(hhi_ready, 1)

                    def body(j, slot):
                        i = 2 * j + slot
                        first, second = (isinstance(i, int) and i == n for n in (0, 1))
                        for t in range(NT):
                            r = number(slot, t) % 2
                            if t < routed and t % per_weight == 0:
                                b = t // per_weight
                                if counted(v := NT * i + t - per_weight if b >= 2
                                           else NT * (i - 1) + routed - per_weight * (1 - b)):
                                    act.wait_ge(h_ready, v)
                                act.wait_ge(bc_ready, NB * i + b + 1)
                                nc.scalar.activation(bw[:, b % 2, :], bcP[:], ACT.Copy).then_inc(bw_ready, 1)
                            if counted(NT * i + t - 1):
                                act.wait_ge(h_ready, NT * i + t - 1)
                            act.wait_ge(gu_ready, NT * i + t + 1)
                            nc.scalar.activation(sl[:, r, :], gP[r][:], ACT.Silu).then_inc(s_ready, 1)
                            if t >= 1:
                                high(j, slot, t - 1)
                            elif not first:
                                high(j if slot else j - 1, 1 - slot, NT - 1)
                            if first and t == 5 and before.on_act:
                                before.act_normalise(act, GROUPS - 1)
                            if first and t == 8:
                                before.act_resid(act, GROUPS - 1)
                            if first and t == route.exp_step:
                                route.act_exp(act, GROUPS - 1)
                            if second and t == 2:
                                route.act_cwT(act, GROUPS - 1)
                            if first and later:
                                later.act_hi(act, t)
                            if not first and not last and t == 12:
                                tail.act_resid(act, i - 1)
                            if t == 13 and not (isinstance(i, int) and i == GROUPS - 1):
                                prepare(i + 1, 1 - slot)

                    prepare(0, 0)
                    pairs(act, body, peel_last=True)
                    high(GROUPS // 2 - 1, 1, NT - 1)

                @block.vector
                def _(dve):
                    def low(j, slot, t):
                        n = number(slot, t)
                        if counted(v := last_use(j, n, 2 * NT, RING)):
                            dve.wait_ge(down_ready, v)
                        dve.wait_ge(hhi_ready, NT * (2 * j + slot) + t + 1)
                        nc.vector.tensor_tensor(h_lo[:, n % RING, :], hh[:, n % 2, :], h_hi[:, n % RING, :].bitcast(F32),
                                                ALU.subtract).then_inc(hlo_ready, 1)

                    def residual(i):
                        if counted(i):
                            dve.wait_ge(tail.tok_ready, i)
                        dve.wait_ge(down_ready, NT * i + NT)
                        nc.vector.tensor_tensor(y_sb[:], acc[:], resid[:, group(i)], ALU.add).then_inc(tail.y_ready, 1)

                    def body(j, slot):
                        i = 2 * j + slot
                        first, second = (isinstance(i, int) and i == n for n in (0, 1))
                        for t in range(NT):
                            r = number(slot, t) % 2
                            if not first and t == LAG - 1:
                                residual(i - 1)
                            if counted(NT * i + t - 1):
                                dve.wait_ge(hlo_ready, NT * i + t - 1)
                            dve.wait_ge(gu_ready, NT * i + t + 1)
                            if t < routed:
                                dve.wait_ge(w_ready, routed * i + t + 1)
                            else:
                                dve.wait_ge(s_ready, NT * i + t + 1)
                            nc.vector.tensor_tensor(hh[:, r, :], uP[r][:], (sw if t < routed else sl)[:, r, :],
                                                    ALU.mult).then_inc(h_ready, 1)
                            if t >= 1:
                                low(j, slot, t - 1)
                            elif not first:
                                low(j if slot else j - 1, 1 - slot, NT - 1)
                            if first and t == 2:
                                before.dve_stats(dve, GROUPS - 1)
                            if first and t == 5 and not before.on_act:
                                before.dve_normalise(dve, GROUPS - 1)
                            if first and t == 12:
                                route.dve_1(dve, GROUPS - 1)
                            if first and t == 14:
                                route.dve_2(dve, GROUPS - 1)
                            if first and later:
                                later.dve_lo(dve, t)
                            if not first and t == 5:
                                tail.dve_stats(dve, i - 1)
                            if not first and t == 7:
                                tail.dve_normalise(dve, i - 1)

                    pairs(dve, body)
                    low(GROUPS // 2 - 1, 1, NT - 1)
                    residual(GROUPS - 1)
                    if last:
                        tail.dve_stats(dve, GROUPS - 1)
                        tail.dve_normalise(dve, GROUPS - 1)

                @block.gpsimd
                def _(pool):
                    def prepare(i, slot):
                        pool.wait_ge(split.hi_ready, i + 1)
                        nc.gpsimd.tensor_tensor(xl[:, slot, :], resid[:, group(i)], xh[:, slot, :].bitcast(F32),
                                                ALU.subtract).then_inc(split.lo_ready, 1)

                    def body(j, slot):
                        i = 2 * j + slot
                        first, second = (isinstance(i, int) and i == n for n in (0, 1))
                        for t in range(routed):
                            b, r = t // per_weight, number(slot, t) % 2
                            if counted(NT * i + t - 1):
                                pool.wait_ge(h_ready, NT * i + t - 1)
                            pool.wait_ge(bw_ready, NB * i + b + 1)
                            pool.wait_ge(s_ready, NT * i + t + 1)
                            nc.gpsimd.tensor_tensor(sw[:, r, :], sl[:, r, :], bw[:, b % 2, :], ALU.mult).then_inc(w_ready, 1)
                            if first and t == 3:
                                before.pool_rstd(pool, GROUPS - 1)
                            if first and t == 15:
                                route.pool_parts(pool, GROUPS - 1)
                            if not first and t == 6:
                                tail.pool_rstd(pool, i - 1)
                            if t == 14 and not (isinstance(i, int) and i == GROUPS - 1):
                                prepare(i + 1, 1 - slot)

                    prepare(0, 0)
                    pairs(pool, body, peel_last=True)
                    if last:
                        tail.pool_rstd(pool, GROUPS - 1)
            return tail

        routing0 = attention0()
        only_l0.close()
        w1_hi, w1_lo = sb("w1_hi", [P, 10 * P], F32R), sb("w1_lo", [P, 10 * P], F32R)
        wl1_hi, wl1_lo = (w[:, 0:10 * P].rearrange("p (a b) -> p a b", a=10) for w in (w1_hi, w1_lo))
        wo1 = sb("wo1", [P, L1_HEADS, P])
        b_sb, bv_sb, pe_sb = sb("b_sb", [P, 9]), sb("bv_sb", [P, P]), sb("pe_sb", [P, GT])
        tri = sb("tri", [P, 2, P])
        with nc.sbuf_tensor("w1_raw", [P, 10 * P], F32) as w1_raw:
            norm0 = experts("f0", L0_TILES, L0_E * L0_HID // P, L0_HID // P, sel0, 3 * L0_E, False, routing0,
                            LaterWeights(w1_raw))
        routing1 = attention1(norm0)
        experts("f1", L1_TILES, L1_TILES - 1, 1, sel1, 3 * L1_E, True, routing1)


def constants():
    p = np.arange(P)
    head = p // L0_D
    f = [np.eye(P), head[:, None] == np.arange(L0_HEADS)[None, :]]
    e, c = np.arange(L0_D)[None, :, None], p[None, None, :]
    f.append(((head[:, None, None] == c // L0_D) & (c % L0_D == e)).reshape(P, -1))
    f.append(np.broadcast_to(np.arange(GT)[None, :] % SEQ != 0, (P, GT)))
    f.append(np.broadcast_to(np.arange(8), (P, 8)))
    row = p[:, None, None]
    f.append((row == np.arange(MEMS + 1)[None, :, None] * L0_HEADS + head[None, None, :]).reshape(P, -1))
    c_f32 = np.concatenate([np.asarray(a, np.float32) for a in f], axis=1)
    tri = np.stack([np.zeros((P, P)), np.where(p[None, :] <= p[:, None], 0.0, MASKED)], axis=1).astype(np.float32)
    r0 = np.arange(3 * L0_E) % L0_E
    sel0 = np.broadcast_to(r0[:, None, None] == np.arange(L0_E)[None, :, None], (3 * L0_E, L0_E, P))
    r1 = np.arange(3 * L1_E) % L1_E
    per = P // L1_HID
    sel1 = r1[:, None, None] == np.arange(L1_TILES - 1)[None, :, None] * per + p[None, None, :] // L1_HID
    pos = np.arange(SEQ, dtype=np.float32)[:, None]
    inv = np.exp(np.float32(-math.log(10000.0)) * np.arange(0, P, 2, dtype=np.float32) / np.float32(P))
    ang = (pos * inv[None, :]).astype(np.float32)
    pe = np.zeros((SEQ, P), np.float32)
    pe[:, 0::2], pe[:, 1::2] = np.sin(ang), np.cos(ang)
    peT = np.concatenate([pe.T] * SEQS, axis=1)
    return (np.ascontiguousarray(c_f32), tri, np.ascontiguousarray(sel0.astype(np.float32)),
            np.ascontiguousarray(sel1.astype(np.float32)), np.ascontiguousarray(peT))


def kernel(**inputs):
    import concourse.bacc as bacc
    from concourse.bass_utils import run_bass_kernel_spmd

    g = {k: np.asarray(v) for k, v in inputs.items()}
    c_f32, c_tri, c_sel0, c_sel1, peT = constants()
    a = {}
    a["xT"] = g["L0_attn_hidden_states"].reshape(TOKENS, DM).T
    wl0 = np.zeros((P, 11, P), np.float32)
    wl0[:, 0], wl0[:, 1], wl0[:, 10] = g["L0_attn_w_q"].T, g["L0_attn_w_k"].T, g["L0_attn_w_o"].T
    wv = g["L0_attn_w_v"].T.reshape(P, L0_HEADS, L0_D)
    for e in range(L0_D):
        wl0[:, 2 + e] = np.repeat(wv[:, :, e], L0_D, axis=1)
    a["w_l0"] = wl0
    mem = np.zeros((P, MEMS, P), np.float32)
    norms = np.zeros((P, REL), np.float32)
    for h in range(L0_HEADS):
        r = slice(h * L0_D, (h + 1) * L0_D)
        for m in range(MEMS):
            mem[r, m, r] = g["L0_attn_memories"][m, h]
            norms[r, m * L0_HEADS + h] = g["L0_attn_memory_norms"][m, h]
    a["mem_bd"], a["norms_bd"], a["gate"] = mem, norms, g["L0_attn_gate"]

    def up(*ws):
        return np.concatenate([w.reshape(-1, DM).T for w in ws], axis=1)

    def down(*ws):
        rows = np.concatenate([w.swapaxes(1, 2).reshape(-1, DM) for w in ws], axis=0)
        return rows.reshape(-1, P, DM).swapaxes(0, 1).reshape(P, -1)

    def padded(w, axis):
        return np.concatenate([w, np.zeros_like(w)], axis=axis)

    a["w_ffn0"] = np.concatenate([up(g["L0_ffn_w1"], g["L0_ffn_sw1"]), up(g["L0_ffn_w3"], g["L0_ffn_sw3"]),
                                  down(g["L0_ffn_w2"], g["L0_ffn_sw2"])], axis=1)
    a["w_ffn1"] = np.concatenate([
        up(g["L1_ffn_expert_gate"], padded(g["L1_ffn_shared_gate_w"], 0)),
        up(g["L1_ffn_expert_up"], padded(g["L1_ffn_shared_up_w"], 0)),
        down(g["L1_ffn_expert_down"], padded(g["L1_ffn_shared_down_w"], 1)[None])], axis=1)
    a["router0"], a["bias0"], a["router1"] = g["L0_ffn_router_w"].T, g["L0_ffn_expert_bias"], g["L1_ffn_gate_w"].T
    wl1 = np.concatenate([g["L1_attn_Wq"], g["L1_attn_Wkv"]], axis=1)
    a["w_l1"] = wl1.reshape(P, 10, P)
    a["wo_l1"] = g["L1_attn_Wo"].reshape(L1_HEADS, P, P).swapaxes(0, 1)
    a["b_l1"] = np.concatenate([g["L1_attn_bq"].reshape(L1_HEADS, P).T, g["L1_attn_bkv"][:P, None]], axis=1)
    a["bv_l1"] = g["L1_attn_bkv"][P:]
    a["peT"], a["c_f32"], a["c_tri"], a["c_sel0"], a["c_sel1"] = peT, c_f32, c_tri, c_sel0, c_sel1

    nc = bacc.Bacc("TRN2", target_bir_lowering=False, num_devices=1)
    arrays, args = {}, []
    for name, x in a.items():
        x = np.ascontiguousarray(x)
        arrays[f"in_{name}"] = x
        args.append(nc.dram_tensor(f"in_{name}", x.shape, mybir.dt.from_np(x.dtype), kind="ExternalInput").ap())
    args.append(nc.dram_tensor("out_x", (TOKENS, DM), F32, kind="ExternalOutput").ap())
    build(nc, *args)
    r = run_bass_kernel_spmd(nc, [arrays], core_ids=[0])
    return r.results[0]["out_x"].reshape(BATCH, SEQ, DM)
```
